# Optimizing a Trainium2 kernel written in Bass

```python
import numpy as np
import jax
import jax.numpy as jnp

def _softmax(x, axis=-1):
    return jax.nn.softmax(x, axis=axis)

def _gelu(x):
    return jax.nn.gelu(x, approximate=True)

def _silu(x):
    return jax.nn.silu(x)

def _sigmoid(x):
    return jax.nn.sigmoid(x)

def _layernorm(x, axis=-1, eps=1e-05):
    m = jnp.mean(x, axis=axis, keepdims=True)
    v = jnp.var(x, axis=axis, keepdims=True)
    return (x - m) / jnp.sqrt(v + eps)

def _scatter_add(tgt, idx, src, axis=0):
    return tgt.at[idx].add(src)

def _segment_sum(src, seg, n):
    return jax.ops.segment_sum(src, seg, n)
kernel_name = 'mk_adaln_d2_jaxref_r4_32729c'

def setup_inputs(seed: int=0):
    np.random.seed(seed)
    _w = jnp.asarray

    def _L0_attn_setup():
        import jax, jax.numpy as jnp
        import numpy as np
        NUM_HEADS = 16
        LN_EPS = 1e-05

        def _gelu(x):
            return jax.nn.gelu(x, approximate=False)
        key = jax.random.key(seed)
        ks = jax.random.split(key, 12)
        B, S, E = (2, 512, 256)
        H = E // 2
        s = lambda fan_in: 1.0 / np.sqrt(fan_in)
        inp = {'x': jax.random.normal(ks[0], (B, S, E), jnp.float32), 'Wq': jax.random.normal(ks[1], (E, E), jnp.float32) * s(E), 'bq': jnp.zeros((E,), jnp.float32), 'Wk': jax.random.normal(ks[2], (E, E), jnp.float32) * s(E), 'bk': jnp.zeros((E,), jnp.float32), 'Wv': jax.random.normal(ks[3], (E, E), jnp.float32) * s(E), 'bv': jnp.zeros((E,), jnp.float32), 'Wo': jax.random.normal(ks[4], (E, E), jnp.float32) * s(E), 'bo': jnp.zeros((E,), jnp.float32), 'dp_w1': jax.random.normal(ks[5], (E, H), jnp.float32) * s(E), 'dp_b1': jnp.zeros((H,), jnp.float32), 'ln_g': jnp.ones((H,), jnp.float32), 'ln_b': jnp.zeros((H,), jnp.float32), 'dp_w2': jax.random.normal(ks[6], (H, 1), jnp.float32) * s(H), 'dp_b2': jnp.zeros((1,), jnp.float32), 'g_w1': jax.random.normal(ks[7], (1, 16), jnp.float32), 'g_b1': jnp.zeros((16,), jnp.float32), 'g_w2': jax.random.normal(ks[8], (16, 1), jnp.float32) * s(16), 'g_b2': jnp.zeros((1,), jnp.float32)}
        return inp
    _L0_attn_in = _L0_attn_setup()

    def _L0_ffn_setup():
        import jax, jax.numpy as jnp
        import numpy as np
        B, T, C, H, E, K = (4, 256, 256, 256, 8, 2)

        def _swiglu(x):
            a, b = jnp.split(x, 2, axis=-1)
            return jax.nn.silu(a) * b
        key = jax.random.key(seed)
        ks = jax.random.split(key, 6)
        s = 0.02
        x = jax.random.normal(ks[0], (B, T, C), jnp.float32)
        w_shared_in = jax.random.normal(ks[1], (C, 2 * H), jnp.float32) * s
        w_shared_out = jax.random.normal(ks[2], (H, C), jnp.float32) * s
        w1_shared = jax.random.normal(ks[3], (C, 2 * H), jnp.float32) * s
        w2 = jax.random.normal(ks[4], (E, H, C), jnp.float32) * s
        w_gate = jax.random.normal(ks[5], (C, E), jnp.float32) * s
        gate_bias = jnp.zeros((E,), jnp.float32)
        return {'x': x, 'w_shared_in': w_shared_in, 'w_shared_out': w_shared_out, 'w1_shared': w1_shared, 'w2': w2, 'w_gate': w_gate, 'gate_bias': gate_bias}
    _L0_ffn_in = _L0_ffn_setup()
    _L0_c = _w((lambda *s: np.random.randn(*s).astype(np.float32) * 0.05)(1, 256))
    _L0_wmod = _w((lambda *s: np.random.randn(*s).astype(np.float32) * 0.05)(256, 6 * 256) * 256 ** (-0.5))

    def _L1_attn_setup():
        import jax, jax.numpy as jnp
        import numpy as np
        CHUNK = 32

        def l2norm(x, eps=1e-06):
            return x * jax.lax.rsqrt(jnp.sum(x * x, axis=-1, keepdims=True) + eps)

        def rmsnorm(x, w, eps=1e-05):
            return x * jax.lax.rsqrt(jnp.mean(x * x, axis=-1, keepdims=True) + eps) * w

        def short_conv(x, w):
            K = w.shape[1]
            l = x.shape[1]
            xp = jnp.pad(x, ((0, 0), (K - 1, 0), (0, 0)))
            y = sum((xp[:, t:t + l, :] * w[:, t] for t in range(K)))
            return y * jax.nn.sigmoid(y)

        def build_sin_cos(l, d):
            inv_freq = 1.0 / 10000.0 ** (jnp.arange(0, d, 2, dtype=jnp.float32) / d)
            ang = jnp.arange(l, dtype=jnp.float32)[:, None] * inv_freq[None, :]
            return (jnp.sin(ang), jnp.cos(ang))

        def apply_rotary(x, sin, cos):
            s = sin[None, :, None, :]
            c = cos[None, :, None, :]
            x1, x2 = (x[..., ::2], x[..., 1::2])
            return jnp.concatenate([x1 * c - x2 * s, x1 * s + x2 * c], axis=-1)

        def delta_rule_chunkwise(q, k, v, beta, gamma, chunk=CHUNK):
            b, h, l, dk = q.shape
            dv = v.shape[-1]
            n = l // chunk
            q = l2norm(q)
            k = l2norm(k)
            v = v * beta[..., None]
            kb = k * beta[..., None]
            rs = lambda x: x.reshape(b, h, n, chunk, -1)
            q, k, v, kb = (rs(q), rs(k), rs(v), rs(kb))
            gm = gamma.reshape(b, h, n, chunk).mean(-1)
            idx = jnp.arange(chunk)
            strict_lower = (idx[:, None] > idx[None, :]).astype(q.dtype)
            A = -(kb @ jnp.swapaxes(k, -1, -2)) * strict_lower
            for i in range(1, chunk):
                A = A.at[..., i, :i].add(jnp.einsum('...j,...jc->...c', A[..., i, :i], A[..., :i, :i]))
            T = A + jnp.eye(chunk, dtype=A.dtype)
            u = T @ v
            w = T @ kb
            tril_inc = (idx[:, None] >= idx[None, :]).astype(q.dtype)

            def step(S, xs):
                qi, ki, ui, wi, g = xs
                attn = qi @ jnp.swapaxes(ki, -1, -2) * tril_inc
                u_t = ui - wi @ S
                o_i = qi @ S + attn @ u_t
                S_new = g[..., None, None] * S + jnp.einsum('bhck,bhcv->bhkv', ki, u_t)
                return (S_new, o_i)
            mv = lambda x: jnp.moveaxis(x, 2, 0)
            S0 = jnp.zeros((b, h, dk, dv), dtype=q.dtype)
            S, o = jax.lax.scan(step, S0, (mv(q), mv(k), mv(u), mv(w), mv(gm)))
            o = jnp.moveaxis(o, 0, 2).reshape(b, h, l, dv)
            return (o, S)

        def fractal_mixer(x, conv_w):
            out = 2.0 * x
            l = x.shape[1]
            for i in range(conv_w.shape[0]):
                dil = 2 ** i
                x_shift = jnp.pad(x, ((0, 0), (dil, 0), (0, 0)))[:, :l, :]
                out = out + x_shift * conv_w[i, :, 0] + x * conv_w[i, :, 1]
            return out
        key = jax.random.key(seed)
        ks = jax.random.split(key, 16)
        B, L, D, H = (2, 1024, 256, 4)
        hd = D // H
        s = 0.02
        return {'hidden_states': jax.random.normal(ks[0], (B, L, D), jnp.float32), 'Wq': jax.random.normal(ks[1], (D, D), jnp.float32) * s, 'Wk': jax.random.normal(ks[2], (D, D), jnp.float32) * s, 'Wv': jax.random.normal(ks[3], (D, D), jnp.float32) * s, 'Wb': jax.random.normal(ks[4], (D, H), jnp.float32) * s, 'Wgamma': jax.random.normal(ks[5], (D, H), jnp.float32) * s, 'rot_logit': jnp.zeros((H,), jnp.float32), 'conv_q': jax.random.normal(ks[6], (D, 4), jnp.float32) * 0.1, 'conv_k': jax.random.normal(ks[7], (D, 4), jnp.float32) * 0.1, 'conv_v': jax.random.normal(ks[8], (D, 4), jnp.float32) * 0.1, 'o_norm_w': jnp.ones((hd,), jnp.float32), 'Wo': jax.random.normal(ks[9], (D, D), jnp.float32) * s, 'frac_conv_w': jax.random.normal(ks[10], (4, D, 2), jnp.float32) * 0.02, 'frac_gate_w': jax.random.normal(ks[11], (D, 1), jnp.float32) * s, 'frac_gate_b': jnp.full((1,), -1.0, jnp.float32), 'mixer_norm_w': jnp.ones((D,), jnp.float32)}
    _L1_attn_in = _L1_attn_setup()

    def _L1_ffn_setup():
        import jax, jax.numpy as jnp
        import numpy as np
        B, S, IN, OUT = (4, 2048, 256, 256)
        EPS = 1e-06

        def _xla_quantized_matmul(x2d, weight_q, weight_scale):
            amax = jnp.max(jnp.abs(x2d), axis=-1, keepdims=True)
            x_scale = jnp.maximum(amax, EPS) / 127.0
            x_q = jnp.clip(jnp.round(x2d / x_scale), -128, 127).astype(jnp.int8)
            acc = jax.lax.dot_general(x_q, weight_q, (((1,), (1,)), ((), ())), preferred_element_type=jnp.int32)
            return acc.astype(jnp.float32) * x_scale * weight_scale[None, :]
        key = jax.random.key(seed)
        k1, k2, k3, k4 = jax.random.split(key, 4)
        x = jax.random.normal(k1, (B, S, IN), dtype=jnp.float32)
        weight_q = jax.random.randint(k2, (OUT, IN), -128, 128, dtype=jnp.int32).astype(jnp.int8)
        weight_scale = jax.random.uniform(k3, (OUT,), dtype=jnp.float32, minval=0.001, maxval=0.01)
        bias = jax.random.normal(k4, (OUT,), dtype=jnp.float32) * 0.01
        return {'x': x, 'weight_q': weight_q, 'weight_scale': weight_scale, 'bias': bias}
    _L1_ffn_in = _L1_ffn_setup()
    _L1_c = _w((lambda *s: np.random.randn(*s).astype(np.float32) * 0.05)(1, 256))
    _L1_wmod = _w((lambda *s: np.random.randn(*s).astype(np.float32) * 0.05)(256, 6 * 256) * 256 ** (-0.5))
    _d = {'L0_attn_x': _L0_attn_in['x'], 'L0_attn_Wq': _L0_attn_in['Wq'], 'L0_attn_bq': _L0_attn_in['bq'], 'L0_attn_Wk': _L0_attn_in['Wk'], 'L0_attn_bk': _L0_attn_in['bk'], 'L0_attn_Wv': _L0_attn_in['Wv'], 'L0_attn_bv': _L0_attn_in['bv'], 'L0_attn_Wo': _L0_attn_in['Wo'], 'L0_attn_bo': _L0_attn_in['bo'], 'L0_attn_dp_w1': _L0_attn_in['dp_w1'], 'L0_attn_dp_b1': _L0_attn_in['dp_b1'], 'L0_attn_ln_g': _L0_attn_in['ln_g'], 'L0_attn_ln_b': _L0_attn_in['ln_b'], 'L0_attn_dp_w2': _L0_attn_in['dp_w2'], 'L0_attn_dp_b2': _L0_attn_in['dp_b2'], 'L0_attn_g_w1': _L0_attn_in['g_w1'], 'L0_attn_g_b1': _L0_attn_in['g_b1'], 'L0_attn_g_w2': _L0_attn_in['g_w2'], 'L0_attn_g_b2': _L0_attn_in['g_b2'], 'L0_ffn_w_shared_in': _L0_ffn_in['w_shared_in'], 'L0_ffn_w_shared_out': _L0_ffn_in['w_shared_out'], 'L0_ffn_w1_shared': _L0_ffn_in['w1_shared'], 'L0_ffn_w2': _L0_ffn_in['w2'], 'L0_ffn_w_gate': _L0_ffn_in['w_gate'], 'L0_ffn_gate_bias': _L0_ffn_in['gate_bias'], 'L0_c': _L0_c, 'L0_wmod': _L0_wmod, 'L1_attn_Wq': _L1_attn_in['Wq'], 'L1_attn_Wk': _L1_attn_in['Wk'], 'L1_attn_Wv': _L1_attn_in['Wv'], 'L1_attn_Wb': _L1_attn_in['Wb'], 'L1_attn_Wgamma': _L1_attn_in['Wgamma'], 'L1_attn_rot_logit': _L1_attn_in['rot_logit'], 'L1_attn_conv_q': _L1_attn_in['conv_q'], 'L1_attn_conv_k': _L1_attn_in['conv_k'], 'L1_attn_conv_v': _L1_attn_in['conv_v'], 'L1_attn_o_norm_w': _L1_attn_in['o_norm_w'], 'L1_attn_Wo': _L1_attn_in['Wo'], 'L1_attn_frac_conv_w': _L1_attn_in['frac_conv_w'], 'L1_attn_frac_gate_w': _L1_attn_in['frac_gate_w'], 'L1_attn_frac_gate_b': _L1_attn_in['frac_gate_b'], 'L1_attn_mixer_norm_w': _L1_attn_in['mixer_norm_w'], 'L1_ffn_weight_q': _L1_ffn_in['weight_q'], 'L1_ffn_weight_scale': _L1_ffn_in['weight_scale'], 'L1_ffn_bias': _L1_ffn_in['bias'], 'L1_c': _L1_c, 'L1_wmod': _L1_wmod}
    _x0 = _d['L0_attn_x']
    _d['L0_attn_x'] = jax.random.normal(jax.random.fold_in(jax.random.key(seed), 1), (1, 4096, 256), dtype=_x0.dtype)
    del _x0
    return _d

def reference(L0_attn_x, L0_attn_Wq, L0_attn_bq, L0_attn_Wk, L0_attn_bk, L0_attn_Wv, L0_attn_bv, L0_attn_Wo, L0_attn_bo, L0_attn_dp_w1, L0_attn_dp_b1, L0_attn_ln_g, L0_attn_ln_b, L0_attn_dp_w2, L0_attn_dp_b2, L0_attn_g_w1, L0_attn_g_b1, L0_attn_g_w2, L0_attn_g_b2, L0_ffn_w_shared_in, L0_ffn_w_shared_out, L0_ffn_w1_shared, L0_ffn_w2, L0_ffn_w_gate, L0_ffn_gate_bias, L0_c, L0_wmod, L1_attn_Wq, L1_attn_Wk, L1_attn_Wv, L1_attn_Wb, L1_attn_Wgamma, L1_attn_rot_logit, L1_attn_conv_q, L1_attn_conv_k, L1_attn_conv_v, L1_attn_o_norm_w, L1_attn_Wo, L1_attn_frac_conv_w, L1_attn_frac_gate_w, L1_attn_frac_gate_b, L1_attn_mixer_norm_w, L1_ffn_weight_q, L1_ffn_weight_scale, L1_ffn_bias, L1_c, L1_wmod):

    def _L0_attn_ref(x, Wq, bq, Wk, bk, Wv, bv, Wo, bo, dp_w1, dp_b1, ln_g, ln_b, dp_w2, dp_b2, g_w1, g_b1, g_w2, g_b2):
        import jax, jax.numpy as jnp
        import numpy as np
        NUM_HEADS = 16
        LN_EPS = 1e-05

        def _gelu(x):
            return jax.nn.gelu(x, approximate=False)
        B, S, E = x.shape
        Hn = NUM_HEADS
        Dh = E // Hn
        scale = Dh ** (-0.5)
        Q = (x @ Wq + bq).reshape(B, S, Hn, Dh)
        K = (x @ Wk + bk).reshape(B, S, Hn, Dh)
        V = (x @ Wv + bv).reshape(B, S, Hn, Dh)
        logits = jnp.einsum('bqhd,bkhd->bhqk', Q, K) * scale
        causal = jnp.tril(jnp.ones((S, S), bool))
        logits = jnp.where(causal, logits, -jnp.inf)
        attn = jax.nn.softmax(logits, axis=-1)
        h = x @ dp_w1 + dp_b1
        mu = h.mean(-1, keepdims=True)
        var = ((h - mu) ** 2).mean(-1, keepdims=True)
        h = (h - mu) / jnp.sqrt(var + LN_EPS) * ln_g + ln_b
        drift = (_gelu(h) @ dp_w2 + dp_b2)[..., 0]
        g = _gelu(drift[..., None] * g_w1[0] + g_b1)
        gate = jnp.tanh(g @ g_w2 + g_b2)[..., 0]
        gated = attn * gate[:, None, None, :]
        out = jnp.einsum('bhqk,bkhd->bqhd', gated, V).reshape(B, S, E)
        return out @ Wo + bo

    def _L0_ffn_ref(x, w_shared_in, w_shared_out, w1_shared, w2, w_gate, gate_bias):
        import jax, jax.numpy as jnp
        import numpy as np
        B, T, C, H, E, K = (4, 256, 256, 256, 8, 2)

        def _swiglu(x):
            a, b = jnp.split(x, 2, axis=-1)
            return jax.nn.silu(a) * b
        Bx, Tx, Cx = x.shape
        S = Bx * Tx
        fx = x.reshape(S, Cx)
        shared_out = _swiglu(fx @ w_shared_in) @ w_shared_out
        logits = fx @ w_gate + gate_bias
        probs = jax.nn.softmax(logits, axis=-1)
        top_val, top_idx = jax.lax.top_k(probs, K)
        wdense = jnp.zeros((S, E), probs.dtype).at[jnp.arange(S)[:, None], top_idx].add(top_val)
        hid = _swiglu(fx @ w1_shared)
        routed_out = jnp.zeros_like(shared_out)
        for e in range(E):
            routed_out = routed_out + wdense[:, e:e + 1] * (hid @ w2[e])
        return (shared_out + routed_out).reshape(Bx, Tx, Cx)

    def _L1_attn_ref(hidden_states, Wq, Wk, Wv, Wb, Wgamma, rot_logit, conv_q, conv_k, conv_v, o_norm_w, Wo, frac_conv_w, frac_gate_w, frac_gate_b, mixer_norm_w):
        import jax, jax.numpy as jnp
        import numpy as np
        CHUNK = 32

        def l2norm(x, eps=1e-06):
            return x * jax.lax.rsqrt(jnp.sum(x * x, axis=-1, keepdims=True) + eps)

        def rmsnorm(x, w, eps=1e-05):
            return x * jax.lax.rsqrt(jnp.mean(x * x, axis=-1, keepdims=True) + eps) * w

        def short_conv(x, w):
            K = w.shape[1]
            l = x.shape[1]
            xp = jnp.pad(x, ((0, 0), (K - 1, 0), (0, 0)))
            y = sum((xp[:, t:t + l, :] * w[:, t] for t in range(K)))
            return y * jax.nn.sigmoid(y)

        def build_sin_cos(l, d):
            inv_freq = 1.0 / 10000.0 ** (jnp.arange(0, d, 2, dtype=jnp.float32) / d)
            ang = jnp.arange(l, dtype=jnp.float32)[:, None] * inv_freq[None, :]
            return (jnp.sin(ang), jnp.cos(ang))

        def apply_rotary(x, sin, cos):
            s = sin[None, :, None, :]
            c = cos[None, :, None, :]
            x1, x2 = (x[..., ::2], x[..., 1::2])
            return jnp.concatenate([x1 * c - x2 * s, x1 * s + x2 * c], axis=-1)

        def delta_rule_chunkwise(q, k, v, beta, gamma, chunk=CHUNK):
            b, h, l, dk = q.shape
            dv = v.shape[-1]
            n = l // chunk
            q = l2norm(q)
            k = l2norm(k)
            v = v * beta[..., None]
            kb = k * beta[..., None]
            rs = lambda x: x.reshape(b, h, n, chunk, -1)
            q, k, v, kb = (rs(q), rs(k), rs(v), rs(kb))
            gm = gamma.reshape(b, h, n, chunk).mean(-1)
            idx = jnp.arange(chunk)
            strict_lower = (idx[:, None] > idx[None, :]).astype(q.dtype)
            A = -(kb @ jnp.swapaxes(k, -1, -2)) * strict_lower
            for i in range(1, chunk):
                A = A.at[..., i, :i].add(jnp.einsum('...j,...jc->...c', A[..., i, :i], A[..., :i, :i]))
            T = A + jnp.eye(chunk, dtype=A.dtype)
            u = T @ v
            w = T @ kb
            tril_inc = (idx[:, None] >= idx[None, :]).astype(q.dtype)

            def step(S, xs):
                qi, ki, ui, wi, g = xs
                attn = qi @ jnp.swapaxes(ki, -1, -2) * tril_inc
                u_t = ui - wi @ S
                o_i = qi @ S + attn @ u_t
                S_new = g[..., None, None] * S + jnp.einsum('bhck,bhcv->bhkv', ki, u_t)
                return (S_new, o_i)
            mv = lambda x: jnp.moveaxis(x, 2, 0)
            S0 = jnp.zeros((b, h, dk, dv), dtype=q.dtype)
            S, o = jax.lax.scan(step, S0, (mv(q), mv(k), mv(u), mv(w), mv(gm)))
            o = jnp.moveaxis(o, 0, 2).reshape(b, h, l, dv)
            return (o, S)

        def fractal_mixer(x, conv_w):
            out = 2.0 * x
            l = x.shape[1]
            for i in range(conv_w.shape[0]):
                dil = 2 ** i
                x_shift = jnp.pad(x, ((0, 0), (dil, 0), (0, 0)))[:, :l, :]
                out = out + x_shift * conv_w[i, :, 0] + x * conv_w[i, :, 1]
            return out
        x = hidden_states
        b, l, d = x.shape
        H = rot_logit.shape[0]
        q = short_conv(x @ Wq, conv_q)
        k = short_conv(x @ Wk, conv_k)
        v = short_conv(x @ Wv, conv_v)
        dk = q.shape[-1] // H
        dv = v.shape[-1] // H
        q = q.reshape(b, l, H, dk)
        k = k.reshape(b, l, H, dk)
        v = v.reshape(b, l, H, dv)
        sin, cos = build_sin_cos(l, dk)
        mix = jax.nn.sigmoid(rot_logit)[None, None, :, None]
        q = mix * apply_rotary(q, sin, cos) + (1.0 - mix) * q
        k = mix * apply_rotary(k, sin, cos) + (1.0 - mix) * k
        beta = jax.nn.sigmoid(x @ Wb)
        gamma = jax.nn.sigmoid(x @ Wgamma)
        bh = lambda t: jnp.transpose(t, (0, 2, 1, 3))
        o, _ = delta_rule_chunkwise(bh(q), bh(k), bh(v), jnp.transpose(beta, (0, 2, 1)), jnp.transpose(gamma, (0, 2, 1)))
        o = jnp.transpose(o, (0, 2, 1, 3))
        o = rmsnorm(o, o_norm_w)
        core = o.reshape(b, l, H * dv) @ Wo
        frac = rmsnorm(fractal_mixer(x, frac_conv_w), mixer_norm_w)
        gate = jax.nn.sigmoid(x @ frac_gate_w + frac_gate_b)
        return core + gate * frac

    def _L1_ffn_ref(x, weight_q, weight_scale, bias):
        import jax, jax.numpy as jnp
        import numpy as np
        B, S, IN, OUT = (4, 2048, 256, 256)
        EPS = 1e-06

        def _xla_quantized_matmul(x2d, weight_q, weight_scale):
            amax = jnp.max(jnp.abs(x2d), axis=-1, keepdims=True)
            x_scale = jnp.maximum(amax, EPS) / 127.0
            x_q = jnp.clip(jnp.round(x2d / x_scale), -128, 127).astype(jnp.int8)
            acc = jax.lax.dot_general(x_q, weight_q, (((1,), (1,)), ((), ())), preferred_element_type=jnp.int32)
            return acc.astype(jnp.float32) * x_scale * weight_scale[None, :]
        orig_shape = x.shape
        x2d = x.reshape(-1, orig_shape[-1])
        out = _xla_quantized_matmul(x2d, weight_q, weight_scale)
        out = out.reshape(*orig_shape[:-1], out.shape[-1])
        out = out + bias
        return out
    x = L0_attn_x
    mod = (_silu(L0_c) @ L0_wmod).reshape(L0_c.shape[0], 6, 1, -1)
    sa, ca, ga, sb, cb, gb = (mod[:, 0], mod[:, 1], mod[:, 2], mod[:, 3], mod[:, 4], mod[:, 5])
    ga = (2 * (ga >= 0) - 1) * jnp.maximum(jnp.abs(ga), 0.25)
    gb = (2 * (gb >= 0) - 1) * jnp.maximum(jnp.abs(gb), 0.25)
    h = _layernorm(x, axis=-1) * (1 + ca) + sa
    x = x + ga * _L0_attn_ref(h, L0_attn_Wq, L0_attn_bq, L0_attn_Wk, L0_attn_bk, L0_attn_Wv, L0_attn_bv, L0_attn_Wo, L0_attn_bo, L0_attn_dp_w1, L0_attn_dp_b1, L0_attn_ln_g, L0_attn_ln_b, L0_attn_dp_w2, L0_attn_dp_b2, L0_attn_g_w1, L0_attn_g_b1, L0_attn_g_w2, L0_attn_g_b2)
    h = _layernorm(x, axis=-1) * (1 + cb) + sb
    x = x + gb * _L0_ffn_ref(h, L0_ffn_w_shared_in, L0_ffn_w_shared_out, L0_ffn_w1_shared, L0_ffn_w2, L0_ffn_w_gate, L0_ffn_gate_bias)
    mod = (_silu(L1_c) @ L1_wmod).reshape(L1_c.shape[0], 6, 1, -1)
    sa, ca, ga, sb, cb, gb = (mod[:, 0], mod[:, 1], mod[:, 2], mod[:, 3], mod[:, 4], mod[:, 5])
    ga = (2 * (ga >= 0) - 1) * jnp.maximum(jnp.abs(ga), 0.25)
    gb = (2 * (gb >= 0) - 1) * jnp.maximum(jnp.abs(gb), 0.25)
    h = _layernorm(x, axis=-1) * (1 + ca) + sa
    x = x + ga * _L1_attn_ref(h, L1_attn_Wq, L1_attn_Wk, L1_attn_Wv, L1_attn_Wb, L1_attn_Wgamma, L1_attn_rot_logit, L1_attn_conv_q, L1_attn_conv_k, L1_attn_conv_v, L1_attn_o_norm_w, L1_attn_Wo, L1_attn_frac_conv_w, L1_attn_frac_gate_w, L1_attn_frac_gate_b, L1_attn_mixer_norm_w)
    h = _layernorm(x, axis=-1) * (1 + cb) + sb
    x = x + gb * _L1_ffn_ref(h, L1_ffn_weight_q, L1_ffn_weight_scale, L1_ffn_bias)
    return x

_drawn_inputs = setup_inputs


def setup_inputs(seed=0):
    import zlib

    import numpy as np

    out = dict(_drawn_inputs(seed))
    spreads = {'L0_attn_bq': (0.0, 0.8),
     'L0_attn_bk': (0.0, 2.0),
     'L0_attn_bv': (0.0, 0.8),
     'L0_attn_bo': (0.0, 2.0),
     'L0_attn_dp_b1': (0.0, 0.8),
     'L0_attn_ln_g': (1.0, 0.6),
     'L0_attn_ln_b': (0.0, 0.8),
     'L0_attn_g_b1': (0.0, 0.8),
     'L0_ffn_gate_bias': (0.0, 0.8),
     'L1_attn_rot_logit': (0.0, 2.0),
     'L1_attn_o_norm_w': (1.0, 0.6),
     'L1_attn_mixer_norm_w': (1.0, 0.6)}
    factors = {'L0_attn_Wq': 8.0,
     'L0_attn_Wk': 8.0,
     'L0_attn_Wv': 8.0,
     'L0_attn_Wo': 7.155,
     'L0_attn_dp_w1': 8.0,
     'L0_attn_dp_w2': 8.0,
     'L0_attn_g_w1': 8.0,
     'L0_attn_g_w2': 7.506,
     'L0_ffn_w_shared_in': 8.0,
     'L0_ffn_w_shared_out': 8.0,
     'L0_ffn_w1_shared': 8.0,
     'L0_ffn_w2': 8.0,
     'L0_ffn_w_gate': 8.0,
     'L1_attn_Wb': 31.648,
     'L1_attn_Wgamma': 200.0,
     'L1_attn_frac_conv_w': 200.0,
     'L1_attn_frac_gate_w': 124.177,
     'L1_ffn_bias': 200.0,
     'L1_attn_Wq': 6.764,
     'L1_attn_Wk': 6.693,
     'L1_attn_Wv': 6.602,
     'L1_attn_conv_q': 6.589,
     'L1_attn_conv_k': 6.723,
     'L1_attn_conv_v': 6.556,
     'L1_attn_Wo': 6.72}
    for name, (base, spread) in spreads.items():
        noise = np.random.default_rng([zlib.crc32(name.encode()), seed]).standard_normal(out[name].shape)
        drawn = base * np.exp(spread * noise) if base else spread * noise
        out[name] = jnp.asarray(drawn.astype(out[name].dtype))
    for name, factor in factors.items():
        out[name] = (out[name] * factor).astype(out[name].dtype)
    return out
```

```python
import concourse.bass as bass
from concourse import mybir
from contextlib import ExitStack


F32 = mybir.dt.float32
BF16 = mybir.dt.bfloat16
ACT = mybir.ActivationFunctionType
ALU = mybir.AluOpType
AX = mybir.AxisListType

P = 128
S, E = 4096, 256
T = S // P
G = S // 512
J = 4
EH = E // P
H, DH = 16, 16
HID = 128
GW = 16
LN_EPS = 1e-5
NEG = -1e30


class Steps:

    def __init__(self, *names, back=1):
        self.primed = back * len(names)
        self.at = {n: i + 1 for i, n in enumerate(names)}
        self.n = len(names)

    def __call__(self, turn, name):
        return turn * self.n + self.primed + self.at[name]


def bcast(ap, n):
    return ap.rearrange("(o c) -> o c", o=1).broadcast_to([n, ap.shape[0]])


def setup(nc, k, d, sb, sem):
    ld = sem("loaded_weights")
    n_ld = [0]

    def load(q, dst, src):
        q.dma_start(dst, src, allow_slow_non_contiguous=True).then_inc(ld, 16)
        n_ld[0] += 16

    for l in (0, 1):
        k[f"silu{l}"] = sb(f"silu{l}", [P, EH], F32)
        k[f"silubc{l}"] = sb(f"silubc{l}", [P, EH, P], F32)
        k[f"mod{l}"] = sb(f"mod{l}", [P, 12], F32)
        k[f"ga{l}"] = sb(f"ga{l}", [P, E], F32)
        k[f"gb{l}"] = sb(f"gb{l}", [P, E], F32)
    k["cb1"] = sb("cb1", [P, E], F32)
    k["sb1"] = sb("sb1", [P, E], F32)
    k["ident"] = sb("ident", [P, P], F32)
    k["identb"] = sb("identb", [P, P], BF16)
    k["ones"] = sb("ones", [P, P], F32)

    with ExitStack() as st:
        c = [st.enter_context(nc.sbuf_tensor(f"c{l}", [P, EH], F32)) for l in (0, 1)]
        wm = [st.enter_context(nc.sbuf_tensor(f"wm{l}", [P, EH, 6 * E], F32)) for l in (0, 1)]
        tmp = st.enter_context(nc.sbuf_tensor("sgn", [P, 4, E], F32))
        raw = st.enter_context(nc.sbuf_tensor("rawrow", [P, 4, E], F32))
        colp = st.enter_context(nc.psum_tensor("colp", [P, 2, 512], F32))
        rowp = st.enter_context(nc.psum_tensor("rowp", [P, 6, 512], F32))
        silu_done, mm_done, v_done, id_done = sem("silu_done"), sem("modmm_done"), sem("mod_done"), sem("id_done")
        block = st.enter_context(nc.Block())
        rows = [(0, 2), (0, 5), (1, 2), (1, 5), (1, 4), (1, 3)]

        @block.sync
        def _(sp):
            for l in (0, 1):
                load(sp, c[l][:], d[f"L{l}_c"].rearrange("o (h p) -> p (o h)", p=P))
                load(sp, wm[l][:], d[f"L{l}_wmod"].rearrange("(h p) n -> p h n", p=P))
            load(sp, k["ident"][:], d["c_ident"])

        @block.gpsimd
        def _(pool):
            nc.gpsimd.memset(k["ones"][:], 1.0).then_inc(id_done, 1)

        @block.scalar
        def _(act):
            act.wait_ge(ld, 16 * 5)
            for l in (0, 1):
                last = nc.scalar.activation(k[f"silu{l}"][:], c[l][:], ACT.Silu)
            last.then_inc(silu_done, 1)

        @block.vector
        def _(dve):
            dve.wait_ge(ld, 16 * 5)
            nc.vector.tensor_copy(k["identb"][:], k["ident"][:]).then_inc(id_done, 1)
            dve.wait_ge(silu_done, 1)
            dve.wait_ge(id_done, 2)
            for l in (0, 1):
                for h in range(EH):
                    last = nc.vector.tensor_scalar(k[f"silubc{l}"][:, h, :], k["ones"][:],
                                                   k[f"silu{l}"][:, h:h + 1], None, ALU.mult)
            last.then_inc(v_done, 1)
            dve.wait_ge(mm_done, 1)
            for l in (0, 1):
                nc.vector.tensor_copy(k[f"mod{l}"][:], colp[:, l, 0:12])
            for i in range(4):
                nc.vector.tensor_copy(raw[:, i, :], rowp[:, i, 0:E])
            nc.vector.tensor_scalar(k["cb1"][:], rowp[:, 4, 0:E], 1.0, None, ALU.add)
            nc.vector.tensor_copy(k["sb1"][:], rowp[:, 5, 0:E]).then_inc(v_done, 1)
            dve.wait_ge(v_done, 2)
            for l in (0, 1):
                for w in (1, 4):
                    nc.vector.tensor_scalar(k[f"mod{l}"][:, 2 * w:2 * w + 2], k[f"mod{l}"][:, 2 * w:2 * w + 2],
                                            1.0, None, ALU.add)
            nc.vector.tensor_scalar(tmp[:], raw[:], 0.0, 2.0, ALU.is_ge, ALU.mult).then_inc(v_done, 1)
            dve.wait_ge(v_done, 3)
            nc.vector.scalar_tensor_tensor(raw[:], raw[:], -1.0, raw[:], ALU.mult, ALU.max)
            nc.vector.tensor_scalar(tmp[:], tmp[:], -1.0, None, ALU.add).then_inc(v_done, 1)
            dve.wait_ge(v_done, 4)
            for i, name in enumerate(("ga0", "gb0", "ga1", "gb1")):
                last = nc.vector.scalar_tensor_tensor(k[name][:], raw[:, i, :], 0.25, tmp[:, i, :], ALU.max, ALU.mult)
            last.then_inc(v_done, 1)

        @block.tensor
        def _(pe):
            pe.wait_ge(v_done, 1)
            for l in (0, 1):
                for m in range(12):
                    for h in range(EH):
                        nc.tensor.matmul(colp[:, l, m:m + 1], wm[l][:, h, m * P:(m + 1) * P],
                                         k[f"silu{l}"][:, h:h + 1], start=(h == 0), stop=(h == 1))
            for i, (l, w) in enumerate(rows):
                for h in range(EH):
                    last = nc.tensor.matmul(rowp[:, i, 0:E], k[f"silubc{l}"][:, h, :],
                                            wm[l][:, h, w * E:(w + 1) * E], start=(h == 0), stop=(h == 1))
            last.then_inc(mm_done, 1)


def project(nc, k, d, sem, x_res, v17, qk_dram):
    V = Steps("stats", "aggr", "rstd", "xn", "r1_0", "r1_1", "r1_2", "r1_3", "v", "haggr", "hrstd", "hn")
    A = Steps("std", "hT", "hi_0", "mid_0", "hi_1", "mid_1", "hi_2", "mid_2", "hi_3", "mid_3", "hstd")
    M = Steps("tp", "qk_0", "qk_1", "qk_2", "qk_3", "vh_01", "vh_23")
    with ExitStack() as st:
        def sb(n, s, t=F32):
            return st.enter_context(nc.sbuf_tensor(f"project_{n}", s, t))
        def ps(n, s, t=F32):
            return st.enter_context(nc.psum_tensor(f"project_{n}", s, t))
        wqk = sb("wqk", [P, EH, 2, E])
        wvh = sb("wvh", [P, EH, E + HID])
        bqk = sb("bqk", [P, 4])
        bvh = sb("bvh", [1, E + HID])
        rows = sb("rows", [P, 3, HID])
        grow = sb("grow", [P, 3, GW])
        g2 = sb("g2", [P, 2])
        st6 = sb("st6", [P, J, 6]); mv = sb("mv", [P, J, 2]); sd = sb("sd", [P, J]); rs = sb("rs", [P, J])
        hs6 = sb("hs6", [P, J, 6]); hmv = sb("hmv", [P, J, 2]); hsd = sb("hsd", [P, J]); hrs = sb("hrs", [P, J])
        xn = sb("xn", [P, J, E])
        hT = sb("hT", [P, EH, 512])
        hi = sb("hi", [P, 4, 512], BF16); mid = sb("mid", [P, 4, 512], BF16); lo = sb("lo", [P, 4, 512], BF16)
        r1 = sb("r1", [P, 4, 512])
        HD = sb("HD", [P, T, HID])
        G1 = sb("G1", [P, T, GW])
        drift = sb("drift", [P, T]); gate = sb("gate", [P, T])
        eps = sb("eps", [P, 1])
        tp = ps("tp", [P, EH, 512]); qkp = ps("qkp", [P, 4, 512]); vhp = ps("vhp", [P, 2, 512])
        xl, wl = sem("x_loaded"), sem("w1_loaded")
        vd, ad, md, pd = sem("p1_dve"), sem("p1_act"), sem("p1_pe"), sem("p1_pool")
        hi_out, mid_out, lo_out = sem("hi_out"), sem("mid_out"), sem("lo_out")
        vd2, ad2, held = sem("p1b_dve"), sem("p1b_act"), sem("aggr_held")
        sheld = sem("project_sp_held")
        block = st.enter_context(nc.Block())
        qk_out = [part.rearrange("(m p) n -> p m n", p=P) for part in qk_dram]

        @block.sync
        def _(sp):
            for h in range(1):
                sp.dma_start(wqk[:, :, 0, :], d["L0_attn_Wq"].rearrange("(h p) n -> p h n", p=P)).then_inc(wl, 16)
                sp.dma_start(wqk[:, :, 1, :], d["L0_attn_Wk"].rearrange("(h p) n -> p h n", p=P)).then_inc(wl, 16)
                sp.dma_start(wvh[:, :, 0:E], d["L0_attn_Wv"].rearrange("(h p) n -> p h n", p=P)).then_inc(wl, 16)
                sp.dma_start(wvh[:, :, E:], d["L0_attn_dp_w1"].rearrange("(h p) n -> p h n", p=P)).then_inc(wl, 16)
            sp.dma_start(bqk[:, 0:2], d["L0_attn_bq"].rearrange("(h p) -> p h", p=P), allow_slow_non_contiguous=True).then_inc(wl, 16)
            sp.dma_start(bqk[:, 2:4], d["L0_attn_bk"].rearrange("(h p) -> p h", p=P), allow_slow_non_contiguous=True).then_inc(wl, 16)
            sp.dma_start(bvh[:, 0:E], d["L0_attn_bv"].rearrange("(o n) -> o n", o=1)).then_inc(wl, 16)
            sp.dma_start(bvh[:, E:], d["L0_attn_dp_b1"].rearrange("(o n) -> o n", o=1)).then_inc(wl, 16)
            for i, n in enumerate(("ln_g", "ln_b")):
                sp.dma_start(rows[:, i, :], bcast(d[f"L0_attn_{n}"], P)).then_inc(wl, 16)
            sp.dma_start(rows[:, 2, :], bcast(d["L0_attn_dp_w2"].rearrange("a o -> (a o)"), P)).then_inc(wl, 16)
            sp.dma_start(grow[:, 0, :], bcast(d["L0_attn_g_w1"].rearrange("o a -> (o a)"), P)).then_inc(wl, 16)
            sp.dma_start(grow[:, 1, :], bcast(d["L0_attn_g_b1"], P)).then_inc(wl, 16)
            sp.dma_start(grow[:, 2, :], bcast(d["L0_attn_g_w2"].rearrange("a o -> (a o)"), P)).then_inc(wl, 16)
            sp.dma_start(g2[:, 0:1], bcast(d["L0_attn_dp_b2"], P)).then_inc(wl, 16)
            sp.dma_start(g2[:, 1:2], bcast(d["L0_attn_g_b2"], P)).then_inc(wl, 16)
            for out in (hi_out, mid_out, lo_out):
                sp.sem_inc(out, 16)
            with sp.Fori(0, G) as g:
                cols = bass.ds(g * 512, 512)
                sp.wait_ge(ad, A(g, "hi_3"))
                sp.sem_inc(sheld, 1)
                sp.dma_start(qk_out[0][:, :, cols], hi[:]).then_inc(hi_out, 16)
                sp.wait_ge(ad, A(g, "mid_3"))
                sp.dma_start(qk_out[1][:, :, cols], mid[:]).then_inc(mid_out, 16)
                sp.wait_ge(pd, 4 * g + 8)
                sp.dma_start(qk_out[2][:, :, cols], lo[:]).then_inc(lo_out, 16)
            sp.wait_ge(hi_out, 16 * G + 16)
            sp.wait_ge(mid_out, 16 * G + 16)
            sp.wait_ge(lo_out, 16 * G + 16)

        @block.scalar
        def _(act):
            xv = d["L0_attn_x"].rearrange("o (t p) c -> p (o t) c", p=P)
            for g in range(G):
                act.dma_start(x_res[:, J * g:J * g + J, :], xv[:, J * g:J * g + J, :]).then_inc(xl, 16)
            act.wait_ge(wl, 16 * 16)
            act.wait_ge(pd, 4)
            act.sem_inc(ad, A.primed)
            with act.Fori(0, G) as g:
                act.wait_ge(vd, V(g, "aggr"))
                nc.scalar.activation(sd[:], mv[:, :, 1], ACT.Sqrt, bias=eps[:]).then_inc(ad, 1)
                act.wait_ge(md, M(g, "tp"))
                for h in range(EH):
                    last = nc.scalar.activation(hT[:, h, :], tp[:, h, :], ACT.Identity,
                                                bias=k["mod0"][:, h:h + 1], scale=k["mod0"][:, 2 + h:3 + h])
                last.then_inc(ad, 1)
                for m in range(4):
                    act.wait_ge(md, M(g, f"qk_{m}"))
                    act.wait_ge(hi_out, 16 * g + 16)
                    nc.scalar.activation(hi[:, m, :], qkp[:, m, :], ACT.Identity, bias=bqk[:, m:m + 1]).then_inc(ad, 1)
                    act.wait_ge(vd, V(g, f"r1_{m}"))
                    act.wait_ge(mid_out, 16 * g + 16)
                    nc.scalar.activation(mid[:, m, :], r1[:, m, :], ACT.Copy).then_inc(ad, 1)
                act.wait_ge(vd, V(g, "haggr"))
                nc.scalar.activation(hsd[:], hmv[:, :, 1], ACT.Sqrt, bias=eps[:]).then_inc(ad, 1)
            act.wait_ge(vd2, 2)
            nc.scalar.activation(HD[:], HD[:], ACT.Gelu).then_inc(ad2, 1)
            act.wait_ge(vd2, 6)
            nc.scalar.activation(G1[:], G1[:], ACT.Gelu).then_inc(ad2, 1)
            act.wait_ge(vd2, 8)
            nc.scalar.activation(gate[:], gate[:], ACT.Tanh, bias=g2[:, 1:2]).then_inc(ad2, 1)

        @block.gpsimd
        def _(pool):
            nc.gpsimd.memset(eps[:], LN_EPS)
            nc.gpsimd.memset(v17[:, :, :, DH:DH + 1], 1.0).then_inc(pd, 4)
            with pool.Fori(0, G) as g:
                for m in range(4):
                    pool.wait_ge(ad, A(g, f"mid_{m}"))
                    pool.wait_ge(lo_out, 16 * g + 16)
                    nc.gpsimd.tensor_tensor(lo[:, m, :], r1[:, m, :], mid[:, m, :], ALU.subtract).then_inc(pd, 1)

        @block.vector
        def _(dve):
            dve.sem_inc(vd, V.primed)
            with dve.Fori(0, G) as g:
                xt = x_res[:, bass.ds(g * J, J), :]
                dve.wait_ge(xl, 16 * G)
                for j in range(J):
                    last = nc.vector.bn_stats(st6[:, j, :], xt[:, j, :])
                last.then_inc(vd, 1)
                dve.wait_ge(vd, V(g, "stats"))
                dve.wait_ge(ad, A(g - 1, "std"))
                dve.sem_inc(held, 1)
                for j in range(J):
                    last = nc.vector.bn_aggr(mv[:, j, :], st6[:, j, :])
                last.then_inc(vd, 1)
                dve.wait_ge(ad, A(g, "std"))
                nc.vector.reciprocal(rs[:], sd[:]).then_inc(vd, 1)
                dve.wait_ge(vd, V(g, "rstd"))
                dve.wait_ge(md, M(g - 1, "tp"))
                for j in range(J):
                    last = nc.vector.tensor_scalar(xn[:, j, :], xt[:, j, :], mv[:, j, 0:1], rs[:, j:j + 1],
                                                   ALU.subtract, ALU.mult)
                last.then_inc(vd, 1)
                for m in range(4):
                    dve.wait_ge(ad, A(g, f"hi_{m}"))
                    dve.wait_ge(pd, 4 * g + m + 1)
                    nc.vector.scalar_tensor_tensor(r1[:, m, :], qkp[:, m, :], bqk[:, m:m + 1], hi[:, m, :],
                                                   ALU.add, ALU.subtract).then_inc(vd, 1)
                for j in range(J):
                    if j % 2 == 0:
                        dve.wait_ge(md, M(g, "vh_01" if j == 0 else "vh_23"))
                    src = vhp[:, j % 2, :] if j < 2 else tp[:, j % 2, :]
                    nc.vector.tensor_copy(v17[:, bass.ds(g * J + j, 1), :, 0:DH],
                                          src[:, 0:E].rearrange("p (o h c) -> p o h c", o=1, c=DH))
                    last = nc.vector.bn_stats(hs6[:, j, :], src[:, E:E + HID])
                last.then_inc(vd, 1)
                dve.wait_ge(vd, V(g, "v"))
                dve.sem_inc(held, 1)
                for j in range(J):
                    last = nc.vector.bn_aggr(hmv[:, j, :], hs6[:, j, :])
                last.then_inc(vd, 1)
                dve.wait_ge(ad, A(g, "hstd"))
                nc.vector.reciprocal(hrs[:], hsd[:]).then_inc(vd, 1)
                dve.wait_ge(vd, V(g, "hrstd"))
                for j in range(J):
                    src = vhp[:, j % 2, :] if j < 2 else tp[:, j % 2, :]
                    last = nc.vector.tensor_scalar(HD[:, bass.ds(g * J + j, 1), :],
                                                   src[:, E:E + HID].rearrange("p (o c) -> p o c", o=1),
                                                   hmv[:, j, 0:1], hrs[:, j:j + 1], ALU.subtract, ALU.mult)
                last.then_inc(vd, 1)
            row = lambda i: rows[:, i:i + 1, :].broadcast_to([P, T, HID])
            wide = lambda i: grow[:, i:i + 1, :].broadcast_to([P, T, GW])
            dve.wait_ge(vd, V(G - 1, "hn"))
            nc.vector.tensor_tensor(HD[:], HD[:], row(0), ALU.mult).then_inc(vd2, 1)
            dve.wait_ge(vd2, 1)
            nc.vector.tensor_tensor(HD[:], HD[:], row(1), ALU.add).then_inc(vd2, 1)
            dve.wait_ge(ad2, 1)
            nc.vector.tensor_tensor(HD[:], HD[:], row(2), ALU.mult).then_inc(vd2, 1)
            dve.wait_ge(vd2, 3)
            nc.vector.tensor_reduce(drift[:], HD[:], AX.X, ALU.add).then_inc(vd2, 1)
            dve.wait_ge(vd2, 4)
            dr = drift[:].rearrange("p (t o) -> p t o", o=1).broadcast_to([P, T, GW])
            nc.vector.scalar_tensor_tensor(G1[:], dr, g2[:, 0:1], wide(0), ALU.add, ALU.mult).then_inc(vd2, 1)
            dve.wait_ge(vd2, 5)
            nc.vector.tensor_tensor(G1[:], G1[:], wide(1), ALU.add).then_inc(vd2, 1)
            dve.wait_ge(ad2, 2)
            nc.vector.tensor_tensor(G1[:], G1[:], wide(2), ALU.mult).then_inc(vd2, 1)
            dve.wait_ge(vd2, 7)
            nc.vector.tensor_reduce(gate[:], G1[:], AX.X, ALU.add).then_inc(vd2, 1)
            dve.wait_ge(ad2, 3)
            vv = v17[:, :, :, 0:DH]
            nc.vector.tensor_tensor(vv, vv, gate[:].rearrange("p (t o c) -> p t o c", o=1, c=1)
                                    .broadcast_to([P, T, H, DH]), ALU.mult).then_inc(vd2, 1)

        @block.tensor
        def _(pe):
            pe.wait_ge(wl, 16 * 16)
            pe.sem_inc(md, M.primed)
            with pe.Fori(0, G) as g:
                pe.wait_ge(vd, V(g, "xn"))
                pe.wait_ge(vd, V(g - 1, "hn"))
                for h in range(EH):
                    for j in range(J):
                        last = nc.tensor.transpose(tp[:, h, j * P:(j + 1) * P], xn[:, j, h * P:(h + 1) * P],
                                                   k["ident"][:])
                last.then_inc(md, 1)
                pe.wait_ge(ad, A(g, "hT"))
                for m in range(4):
                    pe.wait_ge(vd, V(g - 1, f"r1_{m}"))
                    for h in range(EH):
                        last = nc.tensor.matmul(qkp[:, m, :], wqk[:, h, m // 2, (m % 2) * P:(m % 2) * P + P],
                                                hT[:, h, :], start=(h == 0), stop=(h == 1))
                    last.then_inc(md, 1)
                for j in range(J):
                    dst = (vhp if j < 2 else tp)[:, j % 2, 0:E + HID]
                    nc.tensor.matmul(dst, k["ones"][0:1, :], bvh[:], start=True, stop=False)
                    for h in range(EH):
                        last = nc.tensor.matmul(dst, hT[:, h, j * P:(j + 1) * P], wvh[:, h, :],
                                                start=False, stop=(h == 1))
                    if j % 2:
                        last.then_inc(md, 1)


def attention(nc, k, d, sem, v17, qk_dram, ot_dram):
    ROWS = 6 * DH
    MAXR = ROWS + 3
    KPARTS = (0, 0, 0, 1, 1, 2)
    QPARTS = (0, 1, 2, 0, 1, 0)
    BLK = 1024
    NPT = 4
    units = []
    for s in range(2):
        for kt in range(16 * s + 16):
            for b in range(2):
                q0, q1 = 2048 * s + BLK * b, 2048 * s + BLK * b + BLK
                if kt * P < q1:
                    units.append((s, kt, max(q0, kt * P), q1))
    NE = len(units)
    last_of = [max(i for i, u in enumerate(units) if u[0] == s) for s in range(2)]
    pieces = [(i, c, min(512, P * (i + 1) - 512 * c)) for i in range(T) for c in range(i // 4 + 1)]
    NM = len(pieces) + 1
    PER = -(-len(pieces) // (NE - 9))
    LOADS = 12 * 16
    NB = 3
    TURNS = H // NB

    with ExitStack() as st:
        def sb(n, s, t=F32):
            return st.enter_context(nc.sbuf_tensor(f"attn_{n}", s, t))
        def ps(n, s, t=F32):
            return st.enter_context(nc.psum_tensor(f"attn_{n}", s, t))
        KX = [sb(f"KX{b}", [P, S], BF16) for b in range(NB)]
        QX = [sb(f"QX{b}", [P, S], BF16) for b in range(NB)]
        VH = [sb(f"VH{b}", [P, T, DH + 1]) for b in range(NB)]
        PT = [sb(f"PT{b}", [P, BLK]) for b in range(NPT)]
        OS = [sb(f"OS{b}", [P, 512]) for b in range(2)]
        maskf = sb("maskf", [P, 2, P]); maskb = sb("maskb", [P, 2, P], BF16)
        pm = sb("pm", [P, T, 8]); nm = sb("nm", [P, T])
        nmT = sb("nmT", [32, P]); rT = sb("rT", [32, P])
        parts = sb("parts", [32, 3, P], BF16)
        ES = [ps(f"ES{b}", [P, BLK]) for b in range(2)]
        MS = [ps(f"MS{b}", [P, 512]) for b in range(3)]
        OP = ps("OP", [P, 512])
        held = sem("pool_held")
        mask_in, ready = sem("mask_in"), sem("attn_ready")
        loaded = [sem(f"qk_loaded{b}") for b in range(NB)]
        max_scores, max_taken, negmax = sem("max_scores"), sem("max_taken"), sem("negmax")
        split, v_copied, max_rows = sem("max_split"), sem("v_copied"), sem("max_rows")
        exp_scores, exp_done, pv_done = sem("exp_scores"), sem("exp_done"), sem("pv_done")
        o_evac, o_out = sem("o_evac"), [sem(f"o_out{s}") for s in range(2)]
        sheld = sem("attn_sp_held")
        block = st.enter_context(nc.Block())

        @block.sync
        def _(sp):
            sp.dma_start(maskf[:], d["c_mask"].rearrange("a p n -> p a n")).then_inc(mask_in, 16)

            def load(h, b):
                for r in range(6):
                    sp.dma_start(KX[b][DH * r:DH * r + DH, :],
                                 qk_dram[KPARTS[r]][bass.ds(E + h * DH, DH), :]).then_inc(loaded[b], 16)
                    sp.dma_start(QX[b][DH * r:DH * r + DH, :],
                                 qk_dram[QPARTS[r]][bass.ds(h * DH, DH), :]).then_inc(loaded[b], 16)

            def store(h, s):
                sp.wait_ge(o_evac, 2 * h + s + 3)
                sp.sem_inc(sheld, 1)
                for j in range(4):
                    sp.dma_start(ot_dram[bass.ds(h * (DH + 1), DH + 1), 2048 * s + 512 * j:2048 * s + 512 * j + 512],
                                 OS[s][32 * j:32 * j + DH + 1, :]).then_inc(o_out[s], 16)

            def turn(h, b, more):
                store(h, 0)
                if more:
                    sp.wait_ge(exp_scores, NE * h + NE)
                    sp.sem_inc(sheld, 1)
                    load(h + NB, b)
                store(h, 1)

            for s in range(2):
                sp.sem_inc(o_out[s], 64)
            for b in range(NB):
                load(b, b)
            with sp.Fori(0, TURNS - 1) as i:
                for b in range(NB):
                    turn(NB * i + b, b, True)
            for h in range(H - 1 - NB, H):
                turn(h, h % NB, h + NB < H)
            for s in range(2):
                sp.wait_ge(o_out[s], 64 * H + 64)

        @block.gpsimd
        def _(pool):
            for b in range(NB):
                nc.gpsimd.memset(KX[b][ROWS:MAXR, :], 1.0).then_inc(ready, 1)

            def split_max(h, b):
                pool.wait_ge(pv_done, NE * h + NE)
                nc.gpsimd.tensor_copy(VH[b][:].rearrange("p t (o c) -> p t o c", o=1),
                                      v17[:, :, bass.ds(h, 1), :]).then_inc(v_copied, 1)
                pool.wait_ge(max_taken, NM * h + NM)
                pool.sem_inc(held, 1)
                nc.gpsimd.tensor_scalar(parts[:, 0, :], nmT[:], 1.0, None, ALU.mult).then_inc(split, 1)
                pool.wait_ge(split, 4 * h + 5)
                nc.gpsimd.tensor_tensor(rT[:], nmT[:], parts[:, 0, :], ALU.subtract).then_inc(split, 1)
                pool.wait_ge(split, 4 * h + 6)
                pool.sem_inc(held, 1)
                nc.gpsimd.tensor_scalar(parts[:, 1, :], rT[:], 1.0, None, ALU.mult).then_inc(split, 1)
                pool.wait_ge(split, 4 * h + 7)
                nc.gpsimd.tensor_tensor(parts[:, 2, :], rT[:], parts[:, 1, :], ALU.subtract).then_inc(split, 1)
                pool.wait_ge(split, 4 * h + 8)
                pool.sem_inc(held, 1)
                for r in range(3):
                    pool.dma_start(QX[b][ROWS + r:ROWS + r + 1, :].rearrange("o (t c) -> o t c", c=P),
                                   parts[:, r, :]).then_inc(max_rows, 16)
            pool.sem_inc(split, 4)
            with pool.Fori(0, TURNS) as i:
                for b in range(NB):
                    split_max(NB * i + b, b)
            split_max(H - 1, (H - 1) % NB)

        @block.scalar
        def _(act):
            act.sem_inc(o_evac, 2)
            with act.Fori(0, H) as h:
                for u, (s, kt, q0, q1) in enumerate(units):
                    w = q1 - q0
                    act.wait_ge(exp_scores, NE * h + u + 1)
                    act.wait_ge(pv_done, NE * h + u - NPT + 1 + 3 * NE)
                    nc.scalar.activation(PT[u % NPT][:, BLK - w:], ES[u % 2][:, BLK - w:], ACT.Exp,
                                         scale=DH ** -0.5).then_inc(exp_done, 1)
                    if u == last_of[0] + 1 or u == last_of[1]:
                        e = 0 if u < last_of[1] else 1
                        act.wait_ge(pv_done, NE * h + last_of[e] + 1 + 3 * NE)
                        act.wait_ge(o_out[e], 64 * h + 64)
                        nc.scalar.activation(OS[e][:], OP[:], ACT.Copy).then_inc(o_evac, 1)

        @block.vector
        def _(dve):
            dve.wait_ge(mask_in, 16)
            nc.vector.tensor_copy(maskb[:], maskf[:])
            nc.vector.memset(OP[:], 0.0)
            nc.vector.memset(pm[:], NEG).then_inc(ready, 1)

            with dve.Fori(0, H) as h:
                for n, (i, c, w) in enumerate(pieces):
                    dve.wait_ge(max_scores, NM * h + n + 1)
                    nc.vector.tensor_reduce(pm[:, i, c:c + 1], MS[n % 3][:, 0:w], AX.X, ALU.max).then_inc(max_taken, 1)
                dve.wait_ge(max_taken, NM * h + NM - 1)
                nc.vector.tensor_reduce(nm[:], pm[:], AX.X, ALU.max, negate=True).then_inc(negmax, 1)
                dve.wait_ge(max_scores, NM * h + NM)
                dve.wait_ge(split, 4 * h + 4)
                nc.vector.tensor_copy(nmT[:], MS[(NM - 1) % 3][0:T, 0:P]).then_inc(max_taken, 1)

        @block.tensor
        def _(pe):
            def max_piece(h, b, n):
                if n < 3:
                    if not (isinstance(h, int) and h == 0):
                        pe.wait_ge(max_taken, NM * h)
                else:
                    pe.wait_ge(max_taken, NM * h + n - 2)
                if n == NM - 1:
                    pe.wait_ge(negmax, h + 1)
                    nc.tensor.transpose(MS[n % 3][0:T, 0:P], nm[:], k["ident"][:]).then_inc(max_scores, 1)
                    return
                i, c, w = pieces[n]
                diag = c == i // 4
                if diag:
                    nc.tensor.matmul(MS[n % 3][:, w - P:w], k["identb"][:], maskb[:, 0, :],
                                     start=True, stop=False, skip_group_check=True)
                last = nc.tensor.matmul(MS[n % 3][:, 0:w], QX[b][0:ROWS, i * P:(i + 1) * P],
                                        KX[b][0:ROWS, 512 * c:512 * c + w], start=not diag, stop=True,
                                        skip_group_check=True)
                last.then_inc(max_scores, 1)

            def scores(h, b, u):
                s, kt, q0, q1 = units[u]
                if u == 0:
                    pe.wait_ge(max_rows, 48 * h + 48)
                if u < 2:
                    if not (isinstance(h, int) and h == 0):
                        pe.wait_ge(exp_done, NE * h)
                else:
                    pe.wait_ge(exp_done, NE * h + u - 1)
                for c in (q1 - BLK, q1 - 512):
                    a = max(c, q0)
                    if a >= c + 512:
                        continue
                    o = a - (q1 - BLK)
                    diag = c <= kt * P
                    if diag:
                        nc.tensor.matmul(ES[u % 2][:, o:o + P], k["identb"][:], maskb[:, 1, :],
                                         start=True, stop=False, skip_group_check=True)
                    last = nc.tensor.matmul(ES[u % 2][:, o:o + c + 512 - a], KX[b][0:MAXR, kt * P:(kt + 1) * P],
                                            QX[b][0:MAXR, a:c + 512], start=not diag, stop=True,
                                            skip_group_check=True)
                last.then_inc(exp_scores, 1)

            def pv(h, b, u):
                s, kt, q0, q1 = units[u]
                if u == 0:
                    pe.wait_ge(v_copied, h + 1)
                    pe.wait_ge(o_evac, 2 * h + 2)
                if u == last_of[0] + 1:
                    pe.wait_ge(o_evac, 2 * h + 3)
                pe.wait_ge(exp_done, NE * h + u + 1)
                for c in (q1 - BLK, q1 - 512):
                    a = max(c, q0)
                    if a >= c + 512:
                        continue
                    j = c // 512 % 4
                    last = nc.tensor.matmul(OP[32 * j:32 * j + DH + 1, a - c:512], VH[b][:, kt, :],
                                            PT[u % NPT][:, a - (q1 - BLK):c + 512 - (q1 - BLK)],
                                            start=(kt == 0), stop=(kt >= c // P), skip_group_check=True)
                last.then_inc(pv_done, 1)

            pe.wait_ge(ready, NB + 1)
            pe.sem_inc(pv_done, 3 * NE)
            pe.wait_ge(loaded[0], LOADS)
            for n in range(NM):
                max_piece(0, 0, n)
            scores(0, 0, 0)
            scores(0, 0, 1)

            def turn(h, i, b):
                more = b is not None
                b = b or 0
                if more:
                    pe.wait_ge(loaded[(b + 1) % NB], LOADS * (i + 1 + (b + 1) // NB))
                for u in range(NE):
                    if more:
                        for n in range(PER * u, min(PER * u + PER, NM)):
                            max_piece(h + 1, (b + 1) % NB, n)
                    pv(h, b, u)
                    if u + 2 < NE:
                        scores(h, b, u + 2)
                    elif more:
                        scores(h + 1, (b + 1) % NB, u + 2 - NE)
            with pe.Fori(0, TURNS) as i:
                for b in range(NB):
                    turn(NB * i + b, i, b)
            turn(H - 1, TURNS, None)


NEXP = 8


def layer0_out(nc, k, d, sem, x_res, ot_dram):
    V = Steps("rl", "att", "x1", "stats", "aggr", "rstd", "xn", "s_0", "s_1", "s_2", "s_3", "lmax", "lsub", "esum",
              "erec", "p", "gt", "eq", "eqm", "cnt", "rank", "w",
              *[f"acc_{j}_{e}" for j in range(J) for e in range(NEXP + 1)])
    A = Steps("std", "hT", "sg_0", "sg_1", "sg_2", "sg_3", "exp")
    M = Steps("wo", "tp", "lg", "ab_0", "ab_1", "ab_2", "ab_3",
              *[n for j in range(J) for n in (f"sh_{j}", *[f"ex_{j}_{e}" for e in range(NEXP // 2)])])
    with ExitStack() as st:
        def sb(n, s, t=F32):
            return st.enter_context(nc.sbuf_tensor(f"l0out_{n}", s, t))
        def ps(n, s, t=F32):
            return st.enter_context(nc.psum_tensor(f"l0out_{n}", s, t))
        wo = sb("wo", [P, EH, E]); bo = sb("bo", [1, E])
        w_in = sb("w_in", [P, EH, 2, 2 * E]); w_so = sb("w_so", [P, EH, E]); w2 = sb("w2", [P, EH, NEXP, E])
        wg = sb("wg", [P, EH, NEXP]); bg = sb("bg", [1, NEXP])
        lower = sb("lower", [P, NEXP, NEXP])
        OTg = sb("OTg", [P, EH, 512]); LB = sb("LB", [P, EH, 512])
        st6 = sb("st6", [P, J, 6]); mv = sb("mv", [P, J, 2]); sd = sb("sd", [P, J]); rs = sb("rs", [P, J])
        eps = sb("eps", [P, 1])
        xn = sb("xn", [P, J, E]); hT = sb("hT", [P, EH, 512])
        sg = sb("sg", [P, 2, 512]); sT = sb("sT", [P, 4, 512])
        lm = sb("lm", [P, J, 1]); lx = sb("lx", [P, J, NEXP]); es = sb("es", [P, J, 1]); er = sb("er", [P, J, 1])
        p = sb("p", [P, J, NEXP]); gt = sb("gt", [P, J, NEXP, NEXP]); eq = sb("eq", [P, J, NEXP, NEXP])
        rank = sb("rank", [P, J, NEXP]); w = sb("w", [P, J, NEXP])
        tp = ps("tp", [P, EH, 512]); ring = ps("ring", [P, 4, 512]); shp = ps("shp", [P, 512]); lgp = ps("lgp", [P, 512])
        wl, scaled, eps_set = sem("w3_loaded"), sem("w3_scaled"), sem("eps_set")
        ol = sem("attn_loaded")
        vd, ad, md, held = sem("p3_dve"), sem("p3_act"), sem("p3_pe"), sem("p3_held")
        sheld = sem("l0out_sp_held")
        block = st.enter_context(nc.Block())
        NWL = 16 * 10
        ot3 = ot_dram.rearrange("(h r) q -> h r q", r=DH + 1)

        @block.sync
        def _(sp):
            def w(dst, src):
                sp.dma_start(dst, src).then_inc(wl, 16)
            w(wo[:], d["L0_attn_Wo"].rearrange("(h p) n -> p h n", p=P))
            w(bo[:], d["L0_attn_bo"].rearrange("(o n) -> o n", o=1))
            w(w_in[:, :, 0, :], d["L0_ffn_w_shared_in"].rearrange("(h p) n -> p h n", p=P))
            w(w_in[:, :, 1, :], d["L0_ffn_w1_shared"].rearrange("(h p) n -> p h n", p=P))
            w(w_so[:], d["L0_ffn_w_shared_out"].rearrange("(h p) n -> p h n", p=P))
            for h in range(EH):
                w(w2[:, h, :, :], d["L0_ffn_w2"][:, h * P:(h + 1) * P, :].rearrange("e p n -> p e n"))
            w(wg[:], d["L0_ffn_w_gate"].rearrange("(h p) n -> p h n", p=P))
            w(bg[:], d["L0_ffn_gate_bias"].rearrange("(o n) -> o n", o=1))
            w(lower[:], d["c_lower"].rearrange("(o a) b -> o a b", o=1).broadcast_to([P, NEXP, NEXP]))
            with sp.Fori(0, G) as g:
                cols = bass.ds(g * 512, 512)
                sp.wait_ge(md, M(g - 1, "wo"))
                sp.sem_inc(sheld, 1)
                for h in range(EH):
                    hs = slice(8 * h, 8 * h + 8)
                    sp.dma_start(OTg[:, h, :], ot3[hs, 0:DH, cols]).then_inc(ol, 16)
                    sp.dma_start(LB[:, h, :], ot3[hs, DH:DH + 1, cols].broadcast_to([8, DH, 512])).then_inc(ol, 16)

        @block.gpsimd
        def _(pool):
            nc.gpsimd.memset(eps[:], LN_EPS).then_inc(eps_set, 1)

        @block.scalar
        def _(act):
            act.wait_ge(eps_set, 1)
            act.sem_inc(ad, A.primed)
            with act.Fori(0, G) as g:
                act.wait_ge(vd, V(g, "aggr"))
                nc.scalar.activation(sd[:], mv[:, :, 1], ACT.Sqrt, bias=eps[:]).then_inc(ad, 1)
                act.wait_ge(md, M(g, "tp"))
                for h in range(EH):
                    last = nc.scalar.activation(hT[:, h, :], tp[:, h, :], ACT.Identity,
                                                bias=k["mod0"][:, 6 + h:7 + h], scale=k["mod0"][:, 8 + h:9 + h])
                last.then_inc(ad, 1)
                for i in range(4):
                    act.wait_ge(md, M(g, f"ab_{i}"))
                    if i < 2:
                        act.wait_ge(vd, V(g - 1, f"s_{i + 2}"))
                    else:
                        act.wait_ge(vd, V(g, f"s_{i - 2}"))
                    nc.scalar.activation(sg[:, i % 2, :], ring[:, 2 * (i % 2), :], ACT.Silu).then_inc(ad, 1)
                act.wait_ge(vd, V(g, "lsub"))
                nc.scalar.activation(lx[:], lx[:], ACT.Exp).then_inc(ad, 1)

        @block.vector
        def _(dve):
            dve.wait_ge(wl, NWL)
            nc.vector.tensor_tensor(wo[:], wo[:], k["ga0"][:].rearrange("p (o c) -> p o c", o=1)
                                    .broadcast_to([P, EH, E]), ALU.mult)
            nc.vector.tensor_tensor(bo[:], bo[:], k["ga0"][0:1, :], ALU.mult)
            nc.vector.tensor_tensor(w_so[:], w_so[:], k["gb0"][:].rearrange("p (o c) -> p o c", o=1)
                                    .broadcast_to([P, EH, E]), ALU.mult)
            for h in range(EH):
                last = nc.vector.tensor_tensor(w2[:, h, :, :], w2[:, h, :, :],
                                               k["gb0"][:].rearrange("p (o c) -> p o c", o=1)
                                               .broadcast_to([P, NEXP, E]), ALU.mult)
            last.then_inc(scaled, 1)
            dve.sem_inc(vd, V.primed)
            with dve.Fori(0, G) as g:
                xt = x_res[:, bass.ds(g * J, J), :]
                dve.wait_ge(ol, 64 * g + 64)
                nc.vector.reciprocal(LB[:], LB[:]).then_inc(vd, 1)
                dve.wait_ge(vd, V(g, "rl"))
                nc.vector.tensor_tensor(OTg[:], OTg[:], LB[:], ALU.mult).then_inc(vd, 1)
                dve.wait_ge(md, M(g, "wo"))
                for a in range(2):
                    last = nc.vector.tensor_tensor(xt[:, 2 * a:2 * a + 2, :], xt[:, 2 * a:2 * a + 2, :],
                                                   tp[:, a, :].rearrange("p (j c) -> p j c", j=2), ALU.add)
                last.then_inc(vd, 1)
                dve.wait_ge(vd, V(g, "x1"))
                dve.sem_inc(held, 1)
                for j in range(J):
                    last = nc.vector.bn_stats(st6[:, j, :], xt[:, j, :])
                last.then_inc(vd, 1)
                dve.wait_ge(vd, V(g, "stats"))
                dve.sem_inc(held, 1)
                for j in range(J):
                    last = nc.vector.bn_aggr(mv[:, j, :], st6[:, j, :])
                last.then_inc(vd, 1)
                dve.wait_ge(ad, A(g, "std"))
                nc.vector.reciprocal(rs[:], sd[:]).then_inc(vd, 1)
                dve.wait_ge(vd, V(g, "rstd"))
                for j in range(J):
                    last = nc.vector.tensor_scalar(xn[:, j, :], xt[:, j, :], mv[:, j, 0:1], rs[:, j:j + 1],
                                                   ALU.subtract, ALU.mult)
                last.then_inc(vd, 1)
                for i in range(4):
                    dve.wait_ge(ad, A(g, f"sg_{i}"))
                    nc.vector.tensor_tensor(sT[:, i, :], ring[:, 2 * (i % 2) + 1, :], sg[:, i % 2, :],
                                            ALU.mult).then_inc(vd, 1)
                lg = lgp[:, 0:J * NEXP].rearrange("p (j e) -> p j e", e=NEXP)
                nc.vector.tensor_reduce(lm[:, :, 0], lg, AX.X, ALU.max).then_inc(vd, 1)
                dve.wait_ge(vd, V(g, "lmax"))
                nc.vector.tensor_tensor(lx[:], lg, lm[:].broadcast_to([P, J, NEXP]), ALU.subtract).then_inc(vd, 1)
                dve.wait_ge(ad, A(g, "exp"))
                nc.vector.tensor_reduce(es[:, :, 0], lx[:], AX.X, ALU.add).then_inc(vd, 1)
                dve.wait_ge(vd, V(g, "esum"))
                nc.vector.reciprocal(er[:], es[:]).then_inc(vd, 1)
                dve.wait_ge(vd, V(g, "erec"))
                nc.vector.tensor_tensor(p[:], lx[:], er[:].broadcast_to([P, J, NEXP]), ALU.mult).then_inc(vd, 1)
                dve.wait_ge(vd, V(g, "p"))
                pj = p[:].rearrange("p j (o e) -> p j o e", o=1).broadcast_to([P, J, NEXP, NEXP])
                pe_ = p[:].rearrange("p j (e o) -> p j e o", o=1).broadcast_to([P, J, NEXP, NEXP])
                nc.vector.tensor_tensor(gt[:], pj, pe_, ALU.is_gt).then_inc(vd, 1)
                nc.vector.tensor_tensor(eq[:], pj, pe_, ALU.is_equal).then_inc(vd, 1)
                dve.wait_ge(vd, V(g, "eq"))
                nc.vector.tensor_tensor(eq[:], eq[:], lower[:].rearrange("p (o a) b -> p o a b", o=1)
                                        .broadcast_to([P, J, NEXP, NEXP]), ALU.mult).then_inc(vd, 1)
                dve.wait_ge(vd, V(g, "eqm"))
                nc.vector.tensor_tensor(gt[:], gt[:], eq[:], ALU.add).then_inc(vd, 1)
                dve.wait_ge(vd, V(g, "cnt"))
                nc.vector.tensor_reduce(rank[:], gt[:], AX.X, ALU.add).then_inc(vd, 1)
                dve.wait_ge(vd, V(g, "rank"))
                nc.vector.scalar_tensor_tensor(w[:], rank[:], 1.5, p[:], ALU.is_lt, ALU.mult).then_inc(vd, 1)
                for j in range(J):
                    dve.wait_ge(md, M(g, f"sh_{j}"))
                    nc.vector.tensor_tensor(xt[:, j, :], xt[:, j, :], (shp, lgp)[j % 2][:, 0:E],
                                            ALU.add).then_inc(vd, 1)
                    for e in range(NEXP):
                        if e % 2 == 0:
                            dve.wait_ge(md, M(g, f"ex_{j}_{e // 2}"))
                        dve.wait_ge(vd, V(g, f"acc_{j}_{e}"))
                        nc.vector.scalar_tensor_tensor(xt[:, j, :], ring[:, e // 2, (e % 2) * E:(e % 2) * E + E],
                                                       w[:, j, e:e + 1], xt[:, j, :], ALU.mult, ALU.add).then_inc(vd, 1)

        @block.tensor
        def _(pe):
            pe.wait_ge(scaled, 1)
            pe.sem_inc(md, M.primed)
            with pe.Fori(0, G) as g:
                pe.wait_ge(vd, V(g, "att"))
                for j in range(J):
                    dst = tp[:, j // 2, (j % 2) * E:(j % 2) * E + E]
                    nc.tensor.matmul(dst, k["ones"][0:1, :], bo[:], start=True, stop=False)
                    for h in range(EH):
                        last = nc.tensor.matmul(dst, OTg[:, h, j * P:(j + 1) * P], wo[:, h, :],
                                                start=False, stop=(h == 1))
                last.then_inc(md, 1)
                pe.wait_ge(vd, V(g, "xn"))
                for h in range(EH):
                    for j in range(J):
                        last = nc.tensor.transpose(tp[:, h, j * P:(j + 1) * P], xn[:, j, h * P:(h + 1) * P],
                                                   k["ident"][:])
                last.then_inc(md, 1)
                pe.wait_ge(ad, A(g, "hT"))
                for j in range(J):
                    dst = lgp[:, j * NEXP:(j + 1) * NEXP]
                    nc.tensor.matmul(dst, k["ones"][0:1, :], bg[:], start=True, stop=False)
                    for h in range(EH):
                        last = nc.tensor.matmul(dst, hT[:, h, j * P:(j + 1) * P], wg[:, h, :],
                                                start=False, stop=(h == 1))
                last.then_inc(md, 1)
                for i in range(4):
                    if i < 2:
                        pe.wait_ge(vd, V(g - 1, f"acc_{J - 1}_{NEXP}"))
                    else:
                        pe.wait_ge(vd, V(g, f"s_{i - 2}"))
                    for ab in range(2):
                        for h in range(EH):
                            o = ab * E + (i % 2) * P
                            last = nc.tensor.matmul(ring[:, 2 * (i % 2) + ab, :], w_in[:, h, i // 2, o:o + P],
                                                    hT[:, h, :], start=(h == 0), stop=(h == 1))
                    last.then_inc(md, 1)
                for j in range(J):
                    if j == 0:
                        pe.wait_ge(vd, V(g, "s_3"))
                    if j == 1:
                        pe.wait_ge(vd, V(g, "lsub"))
                    if j >= 2:
                        pe.wait_ge(vd, V(g, f"acc_{j - 2}_0"))
                    for h in range(EH):
                        last = nc.tensor.matmul((shp, lgp)[j % 2][:, 0:E], sT[:, h, j * P:(j + 1) * P],
                                                w_so[:, h, :], start=(h == 0), stop=(h == 1))
                    last.then_inc(md, 1)
                    for e in range(NEXP // 2):
                        if j:
                            pe.wait_ge(vd, V(g, f"acc_{j - 1}_{2 * e + 2}"))
                        for h in range(EH):
                            last = nc.tensor.matmul(ring[:, e, :], sT[:, 2 + h, j * P:(j + 1) * P],
                                                    w2[:, h, 2 * e:2 * e + 2, :].rearrange("p a b -> p (a b)"),
                                                    start=(h == 0), stop=(h == 1))
                        last.then_inc(md, 1)


HB, DK = 4, 64
C = 32
CT = P // C
TAPS = 4


def layer1_front(nc, k, d, sem, x_res, gam, kn_dram, vk_dram, a_dram, qk_dram):
    V = Steps("stats", "aggr", "rstd", "xn",
              *[f"fr_{h}_{t}" for t in range(5) for h in range(2)],
              *[f"cv_{m}_{t}" for a in (0, 2, 4) for t in range(TAPS) for m in (a, a + 1)],
              *[f"vb_{j}" for j in range(J)],
              "t1", "t2", "t3", "t4", "ra", "rb", "sc", "ro", "ss", "rr", "nrm",
              *[f"A_{j}" for j in range(J)], "frr", "frg", "frx")
    A = Steps("std", "halo", "hT", "pre_0", "pre_1", "pre_2", "pre_3", "pre_4", "pre_5",
              "silu_0", "silu_1", "silu_2", "silu_3", "silu_4", "silu_5", "sig",
              "X_0", "X_1", "X_2", "X_3", "sq", "fstd", "sstd", "qkT_0", "qkT_1", "qkT_2", "qkT_3")
    M = Steps("tp", "pr_0", "pr_1", "pr_2", "pr_3", "pr_4", "pr_5", "lg", "ftp",
              "nat_0", "nat_1", "nat_2", "nat_3", "qkT_0", "G_0", "qkT_1", "G_1", "qkT_2", "G_2", "qkT_3", "G_3")
    O = Steps("cm", "sm", "t1", "t2", "t3", "t4", "ra", "rb", "sc", "ro", "m2", "kb", "fx")
    with ExitStack() as st:
        def sb(n, s, t=F32):
            return st.enter_context(nc.sbuf_tensor(f"front_{n}", s, t))
        def ps(n, s, t=F32):
            return st.enter_context(nc.psum_tensor(f"front_{n}", s, t))
        wq = sb("wqkv", [P, EH, 3, E]); wl9 = sb("wl9", [P, EH, 9]); b9 = sb("b9", [1, 9])
        cw = sb("cw", [P, 6, TAPS]); fw = sb("fw", [P, EH, 4, 2]); f1 = sb("f1", [P, EH]); mw = sb("mw", [P, E])
        mix = sb("mix", [P, HB]); omx = sb("omx", [P, HB]); trim = sb("trim", [P, C])
        st6 = sb("st6", [P, J, 6]); mv = sb("mv", [P, J, 2]); sd = sb("sd", [P, J]); rs = sb("rs", [P, J])
        eps = sb("eps", [P, 2])
        xn = sb("xn", [P, J, E]); hT = sb("hT", [P, EH, 8 + 512])
        fr = sb("fr", [P, 2, EH, 512])
        pre = sb("pre", [P, 6, 3 + 512]); acc = sb("acc", [P, 2, 6, 512])
        lg = sb("lg", [P, J, 9])
        X = sb("X", [P, J, 2, HB, DK]); XR = sb("XR", [P, J, 2, HB, DK]); SQ = sb("SQ", [P, J, 2, HB, DK])
        cs = sb("cs", [P, 2, J, 32]); csm = sb("csm", [P, 2, J, HB, 32])
        tq = [sb(f"tq{i}", [P, J, HB, 32]) for i in range(4)]
        tk = [sb(f"tk{i}", [P, J, HB, 32]) for i in range(4)]
        ss = sb("ss", [P, J, 2, HB]); ssd = sb("ssd", [P, J, 2, HB]); rr = sb("rr", [P, J, 2, HB, 1])
        vk = sb("vk", [P, J, HB, 2 * DK]); m2 = sb("m2", [P, J, HB, C]); AB = sb("AB", [P, J, HB, C])
        fss = sb("fss", [P, J]); fsd = sb("fsd", [P, J]); frr = sb("frr", [P, J]); frg = sb("frg", [P, J])
        qkG = sb("qkG", [P, J, 4 * P])
        fx = sb("fx", [P, J, E]); junk = sb("junk", [P, E])
        tp = ps("tp", [P, EH, 512]); pr = ps("pr", [P, 2, 512]); nat = ps("nat", [P, 2, 512]); gp = ps("gp", [P, 2, 512])
        wl, csl, xout = sem("w4_loaded"), sem("cs_loaded"), [sem("kn_out"), sem("vk_out"), sem("a_out"), sem("qkT_out")]
        vd, ad, md, od = sem("p4_dve"), sem("p4_act"), sem("p4_pe"), sem("p4_pool")
        held, sheld, pheld, sw = sem("p4_held"), sem("p4_sp_held"), sem("p4_pool_held"), sem("trim_loaded")
        sw2, fsq, cleared, mixed, coef = sem("w4_sum"), sem("frac_squares"), sem("cleared"), sem("mixed"), sem("coefs")
        block = st.enter_context(nc.Block())
        NWL = 16 * 20
        cos_v = d["c_cos"].rearrange("(t p) f -> p t f", p=P)
        sin_v = d["c_sin"].rearrange("(t p) f -> p t f", p=P)

        @block.sync
        def _(sp):
            def w(dst, src):
                sp.dma_start(dst, src, allow_slow_non_contiguous=True).then_inc(wl, 16)
            for i, n in enumerate(("Wq", "Wk", "Wv")):
                w(wq[:, :, i, :], d[f"L1_attn_{n}"].rearrange("(h p) n -> p h n", p=P))
            w(wl9[:, :, 0:4], d["L1_attn_Wb"].rearrange("(h p) n -> p h n", p=P))
            w(wl9[:, :, 4:8], d["L1_attn_Wgamma"].rearrange("(h p) n -> p h n", p=P))
            w(wl9[:, :, 8:9], d["L1_attn_frac_gate_w"].rearrange("(h p) n -> p h n", p=P))
            w(b9[:, 8:9], d["L1_attn_frac_gate_b"].rearrange("(o n) -> o n", o=1))
            for i, n in enumerate(("conv_q", "conv_k", "conv_v")):
                w(cw[:, 2 * i:2 * i + 2, :], d[f"L1_attn_{n}"].rearrange("(h p) n -> p h n", p=P))
            for i in range(4):
                for h in range(EH):
                    w(fw[:, h, i, :], d["L1_attn_frac_conv_w"][i, h * P:(h + 1) * P, :])
            w(mw[:], bcast(d["L1_attn_mixer_norm_w"], P))
            w(mix[:], bcast(d["L1_attn_rot_logit"], P))
            for s in xout:
                sp.sem_inc(s, 16)
            with sp.Fori(0, G) as g:
                tiles = bass.ds(g * J, J)
                sp.wait_ge(od, O(g - 1, "sm"))
                sp.sem_inc(sheld, 1)
                sp.dma_start(cs[:, 0, :, :], cos_v[:, tiles, :]).then_inc(csl, 16)
                sp.dma_start(cs[:, 1, :, :], sin_v[:, tiles, :]).then_inc(csl, 16)
                sp.wait_ge(vd, V(g, "nrm"))
                sp.dma_start(kn_dram[:, tiles, :], XR[:, :, 1, :, :].rearrange("p j h c -> p j (h c)"))\
                    .then_inc(xout[0], 16)
                sp.wait_ge(od, O(g, "kb"))
                sp.sem_inc(sheld, 1)
                sp.wait_ge(vd, V(g, f"vb_{J - 1}"))
                sp.dma_start(vk_dram[:, tiles, :], vk[:].rearrange("p j h c -> p j (h c)")).then_inc(xout[1], 16)
                sp.wait_ge(vd, V(g, f"A_{J - 1}"))
                sp.dma_start(a_dram[:, tiles, :], AB[:].rearrange("p j h c -> p j (h c)")).then_inc(xout[2], 16)
                sp.wait_ge(ad, A(g, f"qkT_{J - 1}"))
                sp.dma_start(qk_dram[:, tiles, :], qkG[:]).then_inc(xout[3], 16)
            for s in xout:
                sp.wait_ge(s, 16 * G + 16)

        @block.gpsimd
        def _(pool):
            nc.gpsimd.memset(eps[:, 0:1], LN_EPS)
            nc.gpsimd.memset(eps[:, 1:2], 1e-6)
            nc.gpsimd.memset(hT[:], 0.0)
            nc.gpsimd.memset(b9[:, 0:8], 0.0)
            nc.gpsimd.memset(pre[:], 0.0).then_inc(cleared, 1)
            pool.dma_start(trim[:], d["c_trim"]).then_inc(sw, 16)
            pool.wait_ge(sw, 16)
            pool.wait_ge(coef, 1)
            pool.sem_inc(od, O.primed)
            with pool.Fori(0, G) as g:
                mb = mix[:].rearrange("p (o h c) -> p o h c", o=1, c=1).broadcast_to([P, J, HB, 32])
                ob = omx[:].rearrange("p (o h c) -> p o h c", o=1, c=1).broadcast_to([P, J, HB, DK])
                pool.wait_ge(csl, 32 * g + 32)
                pool.wait_ge(vd, V(g - 1, "t4"))
                pool.wait_ge(od, O(g - 1, "t4"))
                for i in range(2):
                    nc.gpsimd.tensor_tensor(csm[:, i, :, :, :], cs[:, i, :, :].rearrange("p j (o c) -> p j o c", o=1)
                                            .broadcast_to([P, J, HB, 32]), mb, ALU.mult).then_inc(od, 1)
                pool.wait_ge(ad, A(g, "X_3"))
                pool.wait_ge(od, O(g, "sm"))
                c_, s_ = csm[:, 0, :, :, :], csm[:, 1, :, :, :]
                x1, x2 = X[:, :, 1, :, 0:DK:2], X[:, :, 1, :, 1:DK:2]
                for o_, a_, b_ in ((0, x1, c_), (1, x2, s_), (2, x1, s_), (3, x2, c_)):
                    nc.gpsimd.tensor_tensor(tk[o_][:], a_, b_, ALU.mult).then_inc(od, 1)
                pool.wait_ge(od, O(g, "t4"))
                nc.gpsimd.tensor_tensor(tk[0][:], tk[0][:], tk[1][:], ALU.subtract).then_inc(od, 1)
                nc.gpsimd.tensor_tensor(tk[2][:], tk[2][:], tk[3][:], ALU.add).then_inc(od, 1)
                nc.gpsimd.tensor_tensor(X[:, :, 1, :, :], X[:, :, 1, :, :], ob, ALU.mult).then_inc(od, 1)
                pool.wait_ge(od, O(g, "sc"))
                pool.wait_ge(md, M(g - 1, "qkT_3"))
                pool.wait_ge(xout[0], 16 * g + 16)
                nc.gpsimd.tensor_tensor(XR[:, :, 1, :, 0:32], X[:, :, 1, :, 0:32], tk[0][:], ALU.add)
                nc.gpsimd.tensor_tensor(XR[:, :, 1, :, 32:64], X[:, :, 1, :, 32:64], tk[2][:], ALU.add).then_inc(od, 1)
                bt = lg[:, :, 0:4].rearrange("p j (h o) -> p j h o", o=1)
                nc.gpsimd.tensor_tensor(m2[:], trim[:].rearrange("p (a b c) -> p a b c", a=1, b=1)
                                        .broadcast_to([P, J, HB, C]), bt.broadcast_to([P, J, HB, C]),
                                        ALU.mult).then_inc(od, 1)
                pool.wait_ge(vd, V(g, "nrm"))
                nc.gpsimd.tensor_tensor(vk[:, :, :, DK:], XR[:, :, 1, :, :], bt.broadcast_to([P, J, HB, DK]),
                                        ALU.mult).then_inc(od, 1)
                pool.wait_ge(vd, V(g, "frx"))
                pool.sem_inc(pheld, 1)
                xt = x_res[:, bass.ds(g * J, J), :]
                nc.gpsimd.tensor_tensor(xt, xt, fx[:], ALU.add).then_inc(od, 1)

        @block.scalar
        def _(act):
            act.wait_ge(wl, NWL)
            nc.scalar.activation(mix[:], mix[:], ACT.Sigmoid).then_inc(mixed, 1)
            act.wait_ge(coef, 1)
            act.wait_ge(cleared, 1)
            act.sem_inc(ad, A.primed)
            act.sem_inc(fsq, J)
            with act.Fori(0, G) as g:
                act.wait_ge(vd, V(g, "aggr"))
                nc.scalar.activation(sd[:], mv[:, :, 1], ACT.Sqrt, bias=eps[:, 0:1]).then_inc(ad, 1)
                act.wait_ge(vd, V(g - 1, "frx"))
                nc.scalar.activation(hT[:, :, 0:8], hT[:, :, 512:520], ACT.Copy)
                nc.scalar.activation(pre[:, :, 0:3], pre[:, :, 512:515], ACT.Copy).then_inc(ad, 1)
                act.wait_ge(ad, A(g, "halo"))
                act.wait_ge(md, M(g, "tp"))
                for h in range(EH):
                    last = nc.scalar.activation(hT[:, h, 8:], tp[:, h, :], ACT.Identity,
                                                bias=k["mod1"][:, h:h + 1], scale=k["mod1"][:, 2 + h:3 + h])
                last.then_inc(ad, 1)
                for m in range(6):
                    act.wait_ge(md, M(g, f"pr_{m}"))
                    nc.scalar.activation(pre[:, m, 3:], pr[:, m % 2, :], ACT.Copy).then_inc(ad, 1)
                for m in range(6):
                    act.wait_ge(vd, V(g, f"cv_{m}_3"))
                    nc.scalar.activation(acc[:, 0, m, :], acc[:, 1, m, :], ACT.Silu).then_inc(ad, 1)
                act.wait_ge(md, M(g, "lg"))
                act.wait_ge(od, O(g - 1, "kb"))
                nc.scalar.activation(lg[:], pr[:, 0, 0:J * 9].rearrange("p (j e) -> p j e", e=9), ACT.Sigmoid)
                nc.scalar.activation(gam[:, bass.ds(g * J, J), :],
                                     pr[:, 0, 0:J * 9].rearrange("p (j e) -> p j e", e=9)[:, :, 4:8],
                                     ACT.Sigmoid).then_inc(ad, 1)
                for j in range(J):
                    act.wait_ge(md, M(g, f"nat_{j}"))
                    nc.scalar.activation(X[:, j, :, :, :].rearrange("p a h c -> p (a h c)"), nat[:, 0, :],
                                         ACT.Copy).then_inc(ad, 1)
                act.wait_ge(md, M(g, "ftp"))
                for j in range(J):
                    if j:
                        act.wait_ge(fsq, J * g + j + J)
                    nc.scalar.activation(junk[:], tp[:, j // 2, (j % 2) * E:(j % 2) * E + E], ACT.Square,
                                         accum_out=fss[:, j:j + 1]).then_inc(fsq, 1)
                act.wait_ge(vd, V(g, "ro"))
                act.wait_ge(od, O(g, "ro"))
                nc.scalar.activation(SQ[:], XR[:], ACT.Square).then_inc(ad, 1)
                act.wait_ge(fsq, J * g + 2 * J)
                nc.scalar.activation(fsd[:], fss[:], ACT.Sqrt, bias=eps[:, 0:1], scale=1.0 / E).then_inc(ad, 1)
                act.wait_ge(vd, V(g, "ss"))
                nc.scalar.activation(ssd[:], ss[:], ACT.Sqrt, bias=eps[:, 1:2]).then_inc(ad, 1)
                for j in range(J):
                    act.wait_ge(md, M(g, f"qkT_{j}"))
                    act.wait_ge(xout[3], 16 * g + 16)
                    nc.scalar.activation(qkG[:, j, :], pr[:, 0, :], ACT.Copy).then_inc(ad, 1)

        @block.vector
        def _(dve):
            dve.wait_ge(mixed, 1)
            dve.wait_ge(wl, NWL)
            nc.vector.tensor_scalar(omx[:], mix[:], -1.0, 1.0, ALU.mult, ALU.add)
            nc.vector.tensor_tensor(mw[:], mw[:], k["ga1"][:], ALU.mult)
            nc.vector.tensor_reduce(f1[:], fw[:, :, :, 1], AX.X, ALU.add).then_inc(sw2, 1)
            dve.wait_ge(sw2, 1)
            nc.vector.tensor_scalar(f1[:], f1[:], 2.0, None, ALU.add).then_inc(coef, 1)
            dve.wait_ge(coef, 1)
            dve.sem_inc(vd, V.primed)
            with dve.Fori(0, G) as g:
                xt = x_res[:, bass.ds(g * J, J), :]
                for j in range(J):
                    last = nc.vector.bn_stats(st6[:, j, :], xt[:, j, :])
                last.then_inc(vd, 1)
                dve.wait_ge(vd, V(g, "stats"))
                dve.sem_inc(held, 1)
                for j in range(J):
                    last = nc.vector.bn_aggr(mv[:, j, :], st6[:, j, :])
                last.then_inc(vd, 1)
                dve.wait_ge(ad, A(g, "std"))
                nc.vector.reciprocal(rs[:], sd[:]).then_inc(vd, 1)
                dve.wait_ge(vd, V(g, "rstd"))
                for j in range(J):
                    last = nc.vector.tensor_scalar(xn[:, j, :], xt[:, j, :], mv[:, j, 0:1], rs[:, j:j + 1],
                                                   ALU.subtract, ALU.mult)
                last.then_inc(vd, 1)
                dve.wait_ge(ad, A(g, "hT"))
                for h in range(EH):
                    nc.vector.tensor_scalar(fr[:, 0, h, :], hT[:, h, 8:], f1[:, h:h + 1], None,
                                            ALU.mult).then_inc(vd, 1)
                for t in range(1, 5):
                    sh = 8 - 2 ** (t - 1)
                    for h in range(EH):
                        dve.wait_ge(vd, V(g, f"fr_{h}_{t - 1}"))
                        nc.vector.scalar_tensor_tensor(fr[:, t % 2, h, :], hT[:, h, sh:sh + 512], fw[:, h, t - 1, 0:1],
                                                       fr[:, (t - 1) % 2, h, :], ALU.mult, ALU.add).then_inc(vd, 1)
                for a in (0, 2, 4):
                    for t in range(TAPS):
                        for m in (a, a + 1):
                            if t == 0:
                                dve.wait_ge(ad, A(g, f"pre_{m}"))
                                dve.wait_ge(md, M(g - 1, "nat_3"))
                                nc.vector.tensor_scalar(acc[:, 0, m, :], pre[:, m, 0:512], cw[:, m, 0:1], None,
                                                        ALU.mult).then_inc(vd, 1)
                            else:
                                dve.wait_ge(vd, V(g, f"cv_{m}_{t - 1}"))
                                nc.vector.scalar_tensor_tensor(acc[:, t % 2, m, :], pre[:, m, t:t + 512],
                                                               cw[:, m, t:t + 1], acc[:, (t - 1) % 2, m, :],
                                                               ALU.mult, ALU.add).then_inc(vd, 1)
                dve.wait_ge(ad, A(g, "sig"))
                dve.wait_ge(xout[1], 16 * g + 16)
                for j in range(J):
                    dve.wait_ge(md, M(g, f"nat_{j}"))
                    nc.vector.tensor_tensor(vk[:, j, :, 0:DK], nat[:, 1, 0:E].rearrange("p (h c) -> p h c", h=HB),
                                            lg[:, j, 0:4].rearrange("p (h o) -> p h o", o=1)
                                            .broadcast_to([P, HB, DK]), ALU.mult).then_inc(vd, 1)
                ob = omx[:].rearrange("p (o h c) -> p o h c", o=1, c=1).broadcast_to([P, J, HB, DK])
                dve.wait_ge(ad, A(g, "X_3"))
                dve.wait_ge(od, O(g, "sm"))
                c_, s_ = csm[:, 0, :, :, :], csm[:, 1, :, :, :]
                x1, x2 = X[:, :, 0, :, 0:DK:2], X[:, :, 0, :, 1:DK:2]
                for o_, a_, b_ in ((0, x1, c_), (1, x2, s_), (2, x1, s_), (3, x2, c_)):
                    nc.vector.tensor_tensor(tq[o_][:], a_, b_, ALU.mult).then_inc(vd, 1)
                dve.wait_ge(vd, V(g, "t4"))
                nc.vector.tensor_tensor(tq[0][:], tq[0][:], tq[1][:], ALU.subtract).then_inc(vd, 1)
                nc.vector.tensor_tensor(tq[2][:], tq[2][:], tq[3][:], ALU.add).then_inc(vd, 1)
                nc.vector.tensor_tensor(X[:, :, 0, :, :], X[:, :, 0, :, :], ob, ALU.mult).then_inc(vd, 1)
                dve.wait_ge(vd, V(g, "sc"))
                dve.wait_ge(md, M(g - 1, "qkT_3"))
                nc.vector.tensor_tensor(XR[:, :, 0, :, 0:32], X[:, :, 0, :, 0:32], tq[0][:], ALU.add)
                nc.vector.tensor_tensor(XR[:, :, 0, :, 32:64], X[:, :, 0, :, 32:64], tq[2][:], ALU.add).then_inc(vd, 1)
                dve.wait_ge(ad, A(g, "sq"))
                nc.vector.tensor_reduce(ss[:], SQ[:], AX.X, ALU.add).then_inc(vd, 1)
                dve.wait_ge(ad, A(g, "sstd"))
                nc.vector.reciprocal(rr[:].rearrange("p j a h o -> p (j a h o)"),
                                     ssd[:].rearrange("p j a h -> p (j a h)")).then_inc(vd, 1)
                dve.wait_ge(vd, V(g, "rr"))
                xf = XR[:].rearrange("p j a h c -> p (j a h) c")
                nc.vector.tensor_tensor(xf, xf, rr[:].rearrange("p j a h o -> p (j a h) o")
                                        .broadcast_to([P, J * 2 * HB, DK]), ALU.mult).then_inc(vd, 1)
                dve.wait_ge(od, O(g, "m2"))
                dve.wait_ge(xout[2], 16 * g + 16)
                for j in range(J):
                    dve.wait_ge(md, M(g, f"G_{j}"))
                    for c in range(CT):
                        r = slice(C * c, C * c + C)
                        last = nc.vector.tensor_tensor(AB[r, j, :, :].rearrange("p (a b) c -> p b a c", b=2),
                                                       gp[r, :, 0:2 * P].rearrange("p b (a c) -> p b a c", a=2)[:, :, :, r],
                                                       m2[r, j, :, :].rearrange("p (a b) c -> p b a c", b=2), ALU.mult)
                    last.then_inc(vd, 1)
                dve.wait_ge(ad, A(g, "fstd"))
                nc.vector.reciprocal(frr[:], fsd[:]).then_inc(vd, 1)
                dve.wait_ge(vd, V(g, "frr"))
                nc.vector.tensor_tensor(frg[:], frr[:], lg[:, :, 8], ALU.mult).then_inc(vd, 1)
                dve.wait_ge(vd, V(g, "frg"))
                dve.wait_ge(od, O(g - 1, "fx"))
                for j in range(J):
                    last = nc.vector.scalar_tensor_tensor(fx[:, j, :], tp[:, j // 2, (j % 2) * E:(j % 2) * E + E],
                                                          frg[:, j:j + 1], mw[:], ALU.mult, ALU.mult)
                last.then_inc(vd, 1)

        @block.tensor
        def _(pe):
            pe.wait_ge(wl, NWL)
            pe.wait_ge(cleared, 1)
            pe.sem_inc(md, M.primed)
            with pe.Fori(0, G) as g:
                pe.wait_ge(vd, V(g, "xn"))
                for h in range(EH):
                    for j in range(J):
                        last = nc.tensor.transpose(tp[:, h, j * P:(j + 1) * P], xn[:, j, h * P:(h + 1) * P],
                                                   k["ident"][:])
                last.then_inc(md, 1)
                pe.wait_ge(ad, A(g, "hT"))
                for m in range(6):
                    pe.wait_ge(ad, A(g, f"pre_{m - 2}") if m >= 2 else A(g - 1, "qkT_3"))
                    for h in range(EH):
                        last = nc.tensor.matmul(pr[:, m % 2, :], wq[:, h, m // 2, (m % 2) * P:(m % 2) * P + P],
                                                hT[:, h, 8:], start=(h == 0), stop=(h == 1))
                    last.then_inc(md, 1)
                pe.wait_ge(ad, A(g, "pre_4"))
                for j in range(J):
                    dst = pr[:, 0, j * 9:j * 9 + 9]
                    nc.tensor.matmul(dst, k["ones"][0:1, :], b9[:], start=True, stop=False)
                    for h in range(EH):
                        last = nc.tensor.matmul(dst, hT[:, h, 8 + j * P:8 + (j + 1) * P], wl9[:, h, :],
                                                start=False, stop=(h == 1))
                last.then_inc(md, 1)
                pe.wait_ge(vd, V(g, "fr_1_4"))
                for j in range(J):
                    for h in range(EH):
                        o = (j % 2) * E + h * P
                        last = nc.tensor.transpose(tp[:, j // 2, o:o + P], fr[:, 0, h, j * P:(j + 1) * P],
                                                   k["ident"][:])
                last.then_inc(md, 1)
                pe.wait_ge(ad, A(g, "silu_5"))
                for j in range(J):
                    if j:
                        pe.wait_ge(ad, A(g, f"X_{j - 1}"))
                        pe.wait_ge(vd, V(g, f"vb_{j - 1}"))
                    for m in range(6):
                        last = nc.tensor.transpose(nat[:, m // 4, (m % 4) * P:(m % 4) * P + P],
                                                   acc[:, 0, m, j * P:(j + 1) * P], k["ident"][:])
                    last.then_inc(md, 1)
                pe.wait_ge(vd, V(g, "nrm"))
                for j in range(J):
                    pe.wait_ge(ad, A(g, f"qkT_{j - 1}") if j else A(g, "sig"))
                    for pair in range(2):
                        for i, a in ((0, 1), (1, 0)):
                            last = nc.tensor.transpose(pr[:, 0, (2 * pair + i) * P:(2 * pair + i + 1) * P],
                                                       XR[:, j, a, 2 * pair:2 * pair + 2, :]
                                                       .rearrange("p h c -> p (h c)"), k["ident"][:])
                    last.then_inc(md, 1)
                    pe.wait_ge(ad, A(g, f"qkT_{j}"))
                    pe.wait_ge(vd, V(g, f"A_{j - 1}") if j else V(g - 1, "A_3"))
                    for h in range(HB):
                        r = slice(DK * (h % 2), DK * (h % 2) + DK)
                        kT = qkG[r, j, (h // 2) * 2 * P:(h // 2) * 2 * P + P]
                        last = nc.tensor.matmul(gp[:, h % 2, (h // 2) * P:(h // 2) * P + P], kT, kT, start=True, stop=True)
                    last.then_inc(md, 1)


def solve_chunks(nc, k, d, sem, a_dram, tt_dram):
    with ExitStack() as st:
        AF = st.enter_context(nc.sbuf_tensor("AF", [P, J, C, C], F32))
        TT = st.enter_context(nc.sbuf_tensor("TT", [P, J, C, C], F32))
        tmp = [st.enter_context(nc.sbuf_tensor(f"tmp{i}", [P, J, C - 1, C - 1], F32)) for i in range(2)]
        al, unit, prod, row, out = sem("a_loaded"), sem("unit_set"), sem("products"), sem("rows_done"), sem("tt_out")
        block = st.enter_context(nc.Block())

        @block.sync
        def _(sp):
            for g in range(G):
                for c in range(CT):
                    r = 16 * g + 4 * c
                    for j in range(J):
                        sp.dma_start(AF[r:r + HB, j, :, :],
                                     a_dram[C * c:C * c + C, J * g + j, :].rearrange("i (h j) -> h i j", h=HB))\
                            .then_inc(al, 16)
            sp.wait_ge(row, C - 1)
            for g in range(G):
                sp.dma_start(tt_dram[J * g:J * g + J, :, :].rearrange("t q x -> q t x"),
                             TT[16 * g:16 * g + 16, :, :, :].rearrange("p t c i -> p t (c i)")).then_inc(out, 16)
            sp.wait_ge(out, 16 * G)

        @block.gpsimd
        def _(pool):
            nc.gpsimd.memset(TT[:], 0.0).then_inc(unit, 1)
            pool.wait_ge(unit, 1)
            nc.gpsimd.memset(TT[:].rearrange("p t c i -> p t (c i)")[:, :, 0:C * C:C + 1], 1.0).then_inc(unit, 1)

        @block.vector
        def _(dve):
            dve.wait_ge(unit, 2)
            dve.wait_ge(al, 16 * G * CT * J)
            for i in range(1, C):
                buf = tmp[i % 2][:, :, 0:i, 0:i]
                if i >= 2:
                    dve.wait_ge(row, i - 1)
                nc.vector.tensor_tensor(buf, AF[:, :, i:i + 1, 0:i].broadcast_to([P, J, i, i]), TT[:, :, 0:i, 0:i],
                                        ALU.mult).then_inc(prod, 1)
                dve.wait_ge(prod, i)
                nc.vector.tensor_reduce(TT[:, :, 0:i, i], buf, AX.X, ALU.add).then_inc(row, 1)


def delta_rule(nc, k, d, sem, gam, o_all, kn_dram, vk_dram, qk_dram, tt_dram):
    DF = Steps("atm", "QE", "MT", back=2)
    DT = Steps("S_0", "S_1", "S_2", "S_3", back=2)
    AF_ = Steps("UW", "B", back=2)
    AT = Steps("O", back=2)
    MF = Steps("at", "uw", "qe", "mt", "b", back=2)
    MT_ = Steps("ob", "rec_0", "rec_1", "rec_2", "rec_3", "o", back=2)
    LB = 11
    with ExitStack() as st:
        def sb(n, s, t=F32):
            return st.enter_context(nc.sbuf_tensor(f"delta_{n}", s, t))
        def ps(n, s, t=F32):
            return st.enter_context(nc.psum_tensor(f"delta_{n}", s, t))
        KN = [sb(f"KN{b}", [P, HB, DK]) for b in range(2)]
        KBD = [sb(f"KBD{b}", [P, HB, CT, DK]) for b in range(2)]
        VK = [sb(f"VK{b}", [P, HB, 2 * DK]) for b in range(2)]
        QK = [sb(f"QK{b}", [P, 2, 2, P]) for b in range(2)]
        TTb = [sb(f"TTb{b}", [P, HB, P]) for b in range(2)]
        UW = [sb(f"UW{b}", [P, HB, 2 * DK]) for b in range(2)]
        UBD = [sb(f"UBD{b}", [P, HB, CT, DK]) for b in range(2)]
        atm = [sb(f"atm{b}", [P, HB, P]) for b in range(2)]
        QE = [sb(f"QE{b}", [P, 2, P]) for b in range(2)]
        MTb = [sb(f"MTb{b}", [P, 2, CT, P]) for b in range(2)]
        BB = [sb(f"BB{b}", [P, 2, CT, P]) for b in range(2)]
        gI = [sb(f"gI{b}", [P, 2, CT, DK]) for b in range(2)]
        SB = sb("SB", [P, CT, 2, P])
        GM = sb("GM", [P, T, 2, CT, 2]); gall = sb("gall", [P, T * CT * 2])
        causal = sb("causal", [P, P]); id64 = sb("id64", [P, DK]); chunk = sb("chunk", [P, CT])
        atp = ps("atp", [P, 2, 512]); uwp = ps("uwp", [P, 512]); qep = ps("qep", [P, 512])
        mtp = ps("mtp", [P, 512]); bp = ps("bp", [P, 512]); op = ps("op", [P, 512]); rp = ps("rp", [P, 512])
        wl, gm_done, gm_mm, gm_cp = sem("w5_loaded"), sem("gm_done"), sem("gm_mm"), sem("gm_copied")
        cleared = sem("delta_cleared")
        loaded = [sem(f"tile_loaded{b}") for b in range(2)]
        df, dt_, af, at_, mf, mt_, gi = (sem(n) for n in ("dve_front", "dve_tail", "act_front", "act_tail",
                                                          "pe_front", "pe_tail", "gI_done"))
        held, sheld, aheld = sem("p5_pool_held"), sem("p5_sp_held"), sem("p5_act_held")
        block = st.enter_context(nc.Block())

        @block.sync
        def _(sp):
            sp.dma_start(causal[:], d["c_causal"]).then_inc(wl, 16)
            sp.dma_start(id64[:], d["c_id64"]).then_inc(wl, 16)
            sp.dma_start(chunk[:], d["c_chunk"]).then_inc(wl, 16)
            sp.wait_ge(cleared, 1)

            def load(t, b):
                one = bass.ds(t, 1)
                q = loaded[b]
                sp.dma_start(KN[b][:].rearrange("p h c -> p (h c)"), kn_dram[:, one, :]).then_inc(q, 16)
                sp.dma_start(VK[b][:].rearrange("p h c -> p (h c)"), vk_dram[:, one, :]).then_inc(q, 16)
                sp.dma_start(QK[b][:].rearrange("p a b c -> p (a b c)"), qk_dram[:, one, :]).then_inc(q, 16)
                for c in range(CT):
                    r = slice(C * c, C * c + C)
                    sp.dma_start(KBD[b][r, :, c, :], kn_dram[r, one, :].rearrange("p o (h c) -> p (o h) c", h=HB))\
                        .then_inc(q, 16)
                    sp.dma_start(TTb[b][r, :, r], tt_dram[one, HB * c:HB * c + HB, :]
                                 .rearrange("o h (x i) -> x (o h) i", i=C)).then_inc(q, 16)
            load(0, 0)
            load(1, 1)
            with sp.Fori(0, T // 2 - 1) as i:
                for b in range(2):
                    t = 2 * i + b
                    sp.wait_ge(mf, MF(t, "b"))
                    sp.wait_ge(df, DF(t, "QE"))
                    sp.sem_inc(sheld, 1)
                    load(t + 2, b)

        @block.gpsimd
        def _(pool):
            for b in range(2):
                for buf in (KBD, UBD, TTb, MTb, BB):
                    nc.gpsimd.memset(buf[b][:], 0.0)
            nc.gpsimd.memset(SB[:], 0.0).then_inc(cleared, 1)
            pool.wait_ge(gm_cp, 1)

            def gi_of(t, b):
                pool.wait_ge(df, DF(t - 2, "MT"))
                pool.sem_inc(held, 1)
                gv = gall[:, bass.ds(t * CT * 2, CT * 2)].rearrange("p (c a o) -> p a c o", c=CT, o=1)
                nc.gpsimd.tensor_tensor(gI[b][:], id64[:].rearrange("p (a b c) -> p a b c", a=1, b=1)
                                        .broadcast_to([P, 2, CT, DK]), gv.broadcast_to([P, 2, CT, DK]),
                                        ALU.mult).then_inc(gi, 1)
            with pool.Fori(0, T // 2) as i:
                for b in range(2):
                    gi_of(2 * i + b, b)

        @block.scalar
        def _(act):
            act.wait_ge(cleared, 1)
            act.sem_inc(af, AF_.primed)
            act.sem_inc(at_, AT.primed)

            def front_uw(t, b):
                act.wait_ge(mf, MF(t, "uw"))
                act.wait_ge(mt_, MT_(t - 2, "ob"))
                nc.scalar.activation(UW[b][:].rearrange("p h c -> p (h c)"), uwp[:], ACT.Copy)
                for c in range(CT):
                    r = slice(C * c, C * c + C)
                    last = nc.scalar.activation(UBD[b][r, :, c, :],
                                                uwp[r, :].rearrange("p (h c) -> p h c", h=HB)[:, :, 0:DK], ACT.Copy)
                last.then_inc(af, 1)

            def front_b(t, b):
                act.wait_ge(mf, MF(t, "b"))
                act.wait_ge(dt_, DT(t - 2, "S_3"))
                for q in range(2):
                    r = slice(DK * q, DK * q + DK)
                    last = nc.scalar.activation(BB[b][r, :, :, r],
                                                bp[r, :].rearrange("p (a c x) -> p a c x", a=2, c=CT), ACT.Copy)
                last.then_inc(af, 1)

            def tail(t, b):
                act.wait_ge(mt_, MT_(t, "o"))
                act.sem_inc(aheld, 1)
                nc.scalar.activation(o_all[:, bass.ds(t, 1), :].rearrange("p o c -> p (o c)"), op[:, 0:E],
                                     ACT.Copy).then_inc(at_, 1)

            def both(t, b):
                front_uw(t, b)
                tail(t - 1, 1 - b)
                front_b(t, b)
            front_uw(0, 0)
            front_b(0, 0)
            with act.Fori(0, T // 2 - 1) as i:
                for b in (1, 0):
                    both(2 * i + 2 - b, b)
            both(T - 1, 1)
            tail(T - 1, 1)

        @block.vector
        def _(dve):
            dve.wait_ge(wl, 48)
            for par in range(2):
                nc.vector.tensor_tensor(GM[:, :, par, :, :].rearrange("p t c a -> p t c a"),
                                        gam[:, :, par::2].rearrange("p t (o a) -> p t o a", o=1)
                                        .broadcast_to([P, T, CT, 2]),
                                        chunk[:].rearrange("p (o c q) -> p o c q", o=1, q=1)
                                        .broadcast_to([P, T, CT, 2]), ALU.mult).then_inc(gm_done, 1)
            dve.wait_ge(gm_mm, 1)
            nc.vector.tensor_copy(gall[:], rp[:, 0:T * CT * 2]).then_inc(gm_cp, 1)
            dve.wait_ge(cleared, 1)
            dve.sem_inc(df, DF.primed)
            dve.sem_inc(dt_, DT.primed)

            def f_at(t, b):
                dve.wait_ge(mf, MF(t, "at"))
                dve.wait_ge(mt_, MT_(t - 2, "ob"))
                nc.vector.tensor_tensor(atm[b][:].rearrange("p (a b) c -> p b a c", b=2),
                                        atp[:, :, 0:2 * P].rearrange("p b (a c) -> p b a c", a=2),
                                        causal[:].rearrange("p (a b c) -> p a b c", a=1, b=1)
                                        .broadcast_to([P, 2, 2, P]), ALU.mult).then_inc(df, 1)

            def f_qe(t, b):
                dve.wait_ge(mf, MF(t, "qe"))
                dve.wait_ge(mt_, MT_(t - 2, "o"))
                nc.vector.tensor_tensor(QE[b][:], QK[b][:, :, 1, :], qep[:, 0:2 * P]
                                        .rearrange("p (a c) -> p a c", a=2), ALU.subtract).then_inc(df, 1)

            def f_mt(t, b):
                dve.wait_ge(mf, MF(t, "mt"))
                dve.wait_ge(mt_, MT_(t - 2, "rec_3"))
                dve.wait_ge(gi, t + 1)
                for q in range(2):
                    r = slice(DK * q, DK * q + DK)
                    last = nc.vector.tensor_tensor(MTb[b][r, :, :, r], gI[b][r, :, :, :],
                                                   mtp[r, :].rearrange("p (a c x) -> p a c x", a=2, c=CT),
                                                   ALU.subtract)
                last.then_inc(df, 1)

            def t_s(t, b, c):
                dve.wait_ge(mt_, MT_(t, f"rec_{c}"))
                if c == 0:
                    dve.wait_ge(af, AF_(t, "B"))
                nc.vector.tensor_tensor(SB[:, (c + 1) % CT, :, :], BB[b][:, :, c, :],
                                        rp[:, 0:2 * P].rearrange("p (a c) -> p a c", a=2), ALU.add).then_inc(dt_, 1)

            def both(t, b):
                f_at(t, b)
                t_s(t - 1, 1 - b, 0)
                t_s(t - 1, 1 - b, 1)
                f_qe(t, b)
                t_s(t - 1, 1 - b, 2)
                f_mt(t, b)
                t_s(t - 1, 1 - b, 3)
            f_at(0, 0)
            f_qe(0, 0)
            f_mt(0, 0)
            with dve.Fori(0, T // 2 - 1) as i:
                for b in (1, 0):
                    both(2 * i + 2 - b, b)
            both(T - 1, 1)
            for c in range(CT):
                t_s(T - 1, 1, c)

        @block.tensor
        def _(pe):
            pe.wait_ge(gm_done, 2)
            for par in range(2):
                last = nc.tensor.matmul(rp[DK * par:DK * par + DK, 0:T * CT * 2], k["ones"][:, 0:DK],
                                        GM[:, :, par, :, :], start=True, stop=True)
            last.then_inc(gm_mm, 1)
            pe.wait_ge(gm_cp, 1)
            pe.wait_ge(cleared, 1)
            pe.sem_inc(mf, MF.primed)
            pe.sem_inc(mt_, MT_.primed)

            def f_at(t, b, turn):
                pe.wait_ge(loaded[b], 16 * LB * (turn + 1))
                pe.wait_ge(df, DF(t - 1, "atm"))
                for h in range(HB):
                    r = slice(DK * (h % 2), DK * (h % 2) + DK)
                    last = nc.tensor.matmul(atp[:, h % 2, (h // 2) * P:(h // 2) * P + P], QK[b][r, h // 2, 0, :],
                                            QK[b][r, h // 2, 1, :], start=True, stop=True)
                last.then_inc(mf, 1)

            def f_uw(t, b):
                pe.wait_ge(af, AF_(t - 1, "UW"))
                for h in range(HB):
                    last = nc.tensor.matmul(uwp[:, h * P:(h + 1) * P], TTb[b][:, h, :], VK[b][:, h, :],
                                            start=True, stop=True)
                last.then_inc(mf, 1)

            def f_qe(t, b):
                pe.wait_ge(af, AF_(t, "UW"))
                pe.wait_ge(df, DF(t, "atm"))
                for h in range(HB):
                    r = slice(DK * (h % 2), DK * (h % 2) + DK)
                    last = nc.tensor.matmul(qep[r, (h // 2) * P:(h // 2) * P + P], UW[b][:, h, DK:], atm[b][:, h, :],
                                            start=True, stop=True)
                last.then_inc(mf, 1)

            def f_mt(t, b):
                pe.wait_ge(df, DF(t - 1, "MT"))
                for h in range(HB):
                    r = slice(DK * (h % 2), DK * (h % 2) + DK)
                    o = (h // 2) * 2 * P
                    last = nc.tensor.matmul(mtp[r, o:o + 2 * P], UW[b][:, h, DK:], KBD[b][:, h, :, :],
                                            start=True, stop=True)
                last.then_inc(mf, 1)

            def f_b(t, b):
                pe.wait_ge(af, AF_(t - 1, "B"))
                for h in range(HB):
                    r = slice(DK * (h % 2), DK * (h % 2) + DK)
                    o = (h // 2) * 2 * P
                    last = nc.tensor.matmul(bp[r, o:o + 2 * P], KN[b][:, h, :], UBD[b][:, h, :, :],
                                            start=True, stop=True)
                last.then_inc(mf, 1)

            def t_ob(t, b):
                pe.wait_ge(at_, AT(t - 1, "O"))
                for h in range(HB):
                    last = nc.tensor.matmul(op[:, h * DK:(h + 1) * DK], atm[b][:, h, :], UW[b][:, h, 0:DK],
                                            start=(h == 0), stop=False, skip_group_check=True)
                last.then_inc(mt_, 1)

            def t_rec(t, b, c):
                pe.wait_ge(dt_, DT(t, f"S_{c - 1}") if c else DT(t - 1, "S_3"))
                if c == 0:
                    pe.wait_ge(df, DF(t, "MT"))
                for a in range(2):
                    last = nc.tensor.matmul(rp[:, a * P:(a + 1) * P], MTb[b][:, a, c, :], SB[:, c, a, :],
                                            start=True, stop=True)
                last.then_inc(mt_, 1)
                for a in range(2):
                    last = nc.tensor.matmul(op[C * c:C * c + C, a * P:(a + 1) * P], QE[b][:, a, C * c:C * c + C],
                                            SB[:, c, a, :], start=False, stop=True, skip_group_check=True)
                if c == CT - 1:
                    last.then_inc(mt_, 1)

            def both(t, b, turn):
                f_at(t, b, turn)
                t_ob(t - 1, 1 - b)
                t_rec(t - 1, 1 - b, 0)
                f_uw(t, b)
                t_rec(t - 1, 1 - b, 1)
                f_qe(t, b)
                t_rec(t - 1, 1 - b, 2)
                f_mt(t, b)
                t_rec(t - 1, 1 - b, 3)
                f_b(t, b)
            f_at(0, 0, 0)
            f_uw(0, 0)
            f_qe(0, 0)
            f_mt(0, 0)
            f_b(0, 0)
            with pe.Fori(0, T // 2 - 1) as i:
                both(2 * i + 1, 1, i)
                both(2 * i + 2, 0, i + 1)
            both(T - 1, 1, T // 2 - 1)
            t_ob(T - 1, 1)
            for c in range(CT):
                t_rec(T - 1, 1, c)


MAGIC = 1.5 * 2.0 ** 23


def layer1_back(nc, k, d, sem, x_res, o_all, out):
    V = Steps("ss", "rr", "on", "x3", "stats", "aggr", "rstd", "xn", "amax", "xs", "ri", "qr", "q", "qT", "y", "out")
    A = Steps("sq", "ostd", "oT", "std")
    M = Steps("otp", "wo", "qtp", "lin")
    O = Steps("hm", "ha", "x3b")
    with ExitStack() as st:
        def sb(n, s, t=F32):
            return st.enter_context(nc.sbuf_tensor(f"back_{n}", s, t))
        def ps(n, s, t=F32):
            return st.enter_context(nc.psum_tensor(f"back_{n}", s, t))
        wo = sb("wo1", [P, EH, E]); w8 = sb("w8", [P, EH, E // 4], mybir.dt.int32); wq = sb("wq8", [P, EH, E], BF16)
        w8b = sb("w8b", [P, EH, E], BF16)
        onw = sb("onw", [P, 1]); ws = sb("ws", [P, E]); bi = sb("bi", [P, E]); eps = sb("eps", [P, 1])
        SQ = sb("SQ", [P, J, E]); ss = sb("ss", [P, J * HB]); osd = sb("osd", [P, J * HB]); rr = sb("rr", [P, J * HB, 1])
        on = sb("on", [P, J, E]); oT = sb("oT", [P, EH, 512])
        st6 = sb("st6", [P, J, 6]); mv = sb("mv", [P, J, 2]); sd = sb("sd", [P, J]); rs = sb("rs", [P, J])
        xn = sb("xn", [P, J, E]); h4 = sb("h4", [P, J, E])
        am = sb("am", [P, J]); xs = sb("xs", [P, J]); ri = sb("ri", [P, J])
        q32 = sb("q32", [P, J, E]); qb = sb("qb", [P, J, E], BF16); qT = sb("qT", [P, EH, 512], BF16)
        x3b = sb("x3b", [P, J, E]); y = sb("y", [P, J, E])
        otp = ps("otp", [P, EH, 512]); wop = ps("wop", [P, 2, 512]); qtp = ps("qtp", [P, EH, 512], BF16)
        lin = ps("lin", [P, 2, 512])
        wl, wready, eps_set, out_sent = sem("w6_loaded"), sem("w6_ready"), sem("eps6_set"), sem("out_sent")
        vd, ad, md, od = sem("p6_dve"), sem("p6_act"), sem("p6_pe"), sem("p6_pool")
        held, held2, sheld, aheld = (sem(f"p6_{n}_held") for n in ("dve", "pool", "sp", "act"))
        wcast, wturned = sem("wq_cast"), sem("wq_turned")
        block = st.enter_context(nc.Block())
        out_v = out.rearrange("o (t p) c -> p (o t) c", p=P)

        @block.sync
        def _(sp):
            sp.dma_start(wo[:], d["L1_attn_Wo"].rearrange("(h p) n -> p h n", p=P)).then_inc(wl, 16)
            sp.dma_start(w8[:], d["L1_ffn_weight_q"].rearrange("(h p) n -> p h n", p=P)).then_inc(wl, 16)
            for h in range(2):
                sp.dma_start(onw[DK * h:DK * h + DK, :], d["L1_attn_o_norm_w"].rearrange("(c o) -> c o", o=1))\
                    .then_inc(wl, 16)
            sp.dma_start(ws[:], bcast(d["L1_ffn_weight_scale"], P)).then_inc(wl, 16)
            sp.dma_start(bi[:], bcast(d["L1_ffn_bias"], P)).then_inc(wl, 16)
            sp.sem_inc(out_sent, 16)
            with sp.Fori(0, G) as g:
                sp.wait_ge(vd, V(g, "out"))
                sp.sem_inc(sheld, 1)
                sp.dma_start(out_v[:, bass.ds(g * J, J), :], y[:]).then_inc(out_sent, 16)
            sp.wait_ge(out_sent, 16 * G + 16)

        @block.gpsimd
        def _(pool):
            nc.gpsimd.memset(eps[:], LN_EPS).then_inc(eps_set, 1)
            row = lambda a: a[:].rearrange("p (o c) -> p o c", o=1).broadcast_to([P, J, E])
            pool.wait_ge(wready, 2)
            pool.sem_inc(od, O.primed)
            with pool.Fori(0, G) as g:
                pool.wait_ge(vd, V(g, "xn"))
                nc.gpsimd.tensor_tensor(h4[:], xn[:], row(k["cb1"]), ALU.mult).then_inc(od, 1)
                pool.wait_ge(od, O(g, "hm"))
                nc.gpsimd.tensor_tensor(h4[:], h4[:], row(k["sb1"]), ALU.add).then_inc(od, 1)
                pool.wait_ge(vd, V(g - 1, "out"))
                pool.sem_inc(held2, 1)
                nc.gpsimd.tensor_tensor(x3b[:], x_res[:, bass.ds(g * J, J), :], row(bi), ALU.add).then_inc(od, 1)

        @block.scalar
        def _(act):
            act.wait_ge(wl, 16 * 6)
            act.wait_ge(eps_set, 1)
            act.sem_inc(ad, A.primed)
            with act.Fori(0, G) as g:
                act.wait_ge(vd, V(g - 1, "ss"))
                act.sem_inc(aheld, 1)
                nc.scalar.activation(SQ[:], o_all[:, bass.ds(g * J, J), :], ACT.Square).then_inc(ad, 1)
                act.wait_ge(vd, V(g, "ss"))
                nc.scalar.activation(osd[:], ss[:], ACT.Sqrt, bias=eps[:], scale=1.0 / DK).then_inc(ad, 1)
                act.wait_ge(md, M(g, "otp"))
                nc.scalar.activation(oT[:], otp[:], ACT.Copy, scale=onw[:]).then_inc(ad, 1)
                act.wait_ge(vd, V(g, "aggr"))
                nc.scalar.activation(sd[:], mv[:, :, 1], ACT.Sqrt, bias=eps[:]).then_inc(ad, 1)

        @block.vector
        def _(dve):
            dve.wait_ge(wl, 16 * 6)
            nc.vector.tensor_tensor(wo[:], wo[:], k["ga1"][:].rearrange("p (o c) -> p o c", o=1)
                                    .broadcast_to([P, EH, E]), ALU.mult)
            nc.vector.tensor_copy(w8b[:], w8[:].bitcast(mybir.dt.int8)).then_inc(wcast, 1)
            nc.vector.tensor_tensor(ws[:], ws[:], k["gb1"][:], ALU.mult)
            nc.vector.tensor_tensor(bi[:], bi[:], k["gb1"][:], ALU.mult).then_inc(wready, 1)
            dve.wait_ge(wturned, 1)
            nc.vector.tensor_copy(wq[:], qtp[:, :, 0:E]).then_inc(wready, 1)
            dve.wait_ge(wready, 2)
            dve.sem_inc(vd, V.primed)
            with dve.Fori(0, G) as g:
                xt = x_res[:, bass.ds(g * J, J), :]
                ot = o_all[:, bass.ds(g * J, J), :]
                dve.wait_ge(ad, A(g, "sq"))
                nc.vector.tensor_reduce(ss[:], SQ[:].rearrange("p j (h c) -> p (j h) c", c=DK), AX.X,
                                        ALU.add).then_inc(vd, 1)
                dve.wait_ge(ad, A(g, "ostd"))
                nc.vector.reciprocal(rr[:, :, 0], osd[:]).then_inc(vd, 1)
                dve.wait_ge(vd, V(g, "rr"))
                nc.vector.tensor_tensor(on[:].rearrange("p j (h c) -> p (j h) c", c=DK),
                                        ot.rearrange("p j (h c) -> p (j h) c", c=DK),
                                        rr[:].broadcast_to([P, J * HB, DK]), ALU.mult).then_inc(vd, 1)
                dve.wait_ge(md, M(g, "wo"))
                for a in range(2):
                    last = nc.vector.tensor_tensor(xt[:, 2 * a:2 * a + 2, :], xt[:, 2 * a:2 * a + 2, :],
                                                   wop[:, a, :].rearrange("p (j c) -> p j c", j=2), ALU.add)
                last.then_inc(vd, 1)
                dve.wait_ge(vd, V(g, "x3"))
                dve.sem_inc(held, 1)
                for j in range(J):
                    last = nc.vector.bn_stats(st6[:, j, :], xt[:, j, :])
                last.then_inc(vd, 1)
                dve.wait_ge(vd, V(g, "stats"))
                dve.sem_inc(held, 1)
                for j in range(J):
                    last = nc.vector.bn_aggr(mv[:, j, :], st6[:, j, :])
                last.then_inc(vd, 1)
                dve.wait_ge(ad, A(g, "std"))
                nc.vector.reciprocal(rs[:], sd[:]).then_inc(vd, 1)
                dve.wait_ge(vd, V(g, "rstd"))
                for j in range(J):
                    last = nc.vector.tensor_scalar(xn[:, j, :], xt[:, j, :], mv[:, j, 0:1], rs[:, j:j + 1],
                                                   ALU.subtract, ALU.mult)
                last.then_inc(vd, 1)
                dve.wait_ge(od, O(g, "ha"))
                nc.vector.tensor_reduce(am[:], h4[:], AX.X, ALU.max, apply_absolute_value=True).then_inc(vd, 1)
                dve.wait_ge(vd, V(g, "amax"))
                nc.vector.tensor_scalar(xs[:], am[:], 1e-6, 1.0 / 127.0, ALU.max, ALU.mult).then_inc(vd, 1)
                dve.wait_ge(vd, V(g, "xs"))
                nc.vector.reciprocal(ri[:], xs[:]).then_inc(vd, 1)
                dve.wait_ge(vd, V(g, "ri"))
                for j in range(J):
                    last = nc.vector.tensor_scalar(q32[:, j, :], h4[:, j, :], ri[:, j:j + 1], MAGIC,
                                                   ALU.mult, ALU.add)
                last.then_inc(vd, 1)
                dve.wait_ge(vd, V(g, "qr"))
                nc.vector.tensor_scalar(qb[:], q32[:], -MAGIC, 127.0, ALU.add, ALU.min).then_inc(vd, 1)
                dve.wait_ge(md, M(g, "qtp"))
                nc.vector.tensor_scalar(qT[:], qtp[:], -128.0, None, ALU.max).then_inc(vd, 1)
                dve.wait_ge(md, M(g, "lin"))
                dve.wait_ge(out_sent, 16 * g + 16)
                for j in range(J):
                    last = nc.vector.scalar_tensor_tensor(y[:, j, :], lin[:, j // 2, (j % 2) * E:(j % 2) * E + E],
                                                          xs[:, j:j + 1], ws[:], ALU.mult, ALU.mult)
                last.then_inc(vd, 1)
                dve.wait_ge(vd, V(g, "y"))
                dve.wait_ge(od, O(g, "x3b"))
                nc.vector.tensor_tensor(y[:], y[:], x3b[:], ALU.add).then_inc(vd, 1)

        @block.tensor
        def _(pe):
            pe.wait_ge(wcast, 1)
            for h in range(EH):
                for o in range(EH):
                    last = nc.tensor.transpose(qtp[:, h, o * P:(o + 1) * P], w8b[:, o, h * P:(h + 1) * P],
                                               k["identb"][:])
            last.then_inc(wturned, 1)
            pe.wait_ge(wready, 2)
            pe.sem_inc(md, M.primed)
            with pe.Fori(0, G) as g:
                pe.wait_ge(vd, V(g, "on"))
                for h in range(EH):
                    for j in range(J):
                        last = nc.tensor.transpose(otp[:, h, j * P:(j + 1) * P], on[:, j, h * P:(h + 1) * P],
                                                   k["ident"][:])
                last.then_inc(md, 1)
                pe.wait_ge(ad, A(g, "oT"))
                for j in range(J):
                    for h in range(EH):
                        last = nc.tensor.matmul(wop[:, j // 2, (j % 2) * E:(j % 2) * E + E],
                                                oT[:, h, j * P:(j + 1) * P], wo[:, h, :], start=(h == 0), stop=(h == 1))
                last.then_inc(md, 1)
                pe.wait_ge(vd, V(g, "q"))
                for h in range(EH):
                    for j in range(J):
                        last = nc.tensor.transpose(qtp[:, h, j * P:(j + 1) * P], qb[:, j, h * P:(h + 1) * P],
                                                   k["identb"][:])
                last.then_inc(md, 1)
                pe.wait_ge(vd, V(g, "qT"))
                for j in range(J):
                    for h in range(EH):
                        last = nc.tensor.matmul(lin[:, j // 2, (j % 2) * E:(j % 2) * E + E],
                                                qT[:, h, j * P:(j + 1) * P], wq[:, h, :], start=(h == 0), stop=(h == 1))
                last.then_inc(md, 1)


def build(nc, d, out):
    qk_parts = nc.dram_tensor("qk_parts", [3, 2 * E, S], BF16, kind="Internal").ap()
    ot = nc.dram_tensor("attn_out", [H * (DH + 1), S], F32, kind="Internal").ap()
    kn = nc.dram_tensor("k_natural", [P, T, E], F32, kind="Internal").ap()
    vk = nc.dram_tensor("vk_beta", [P, T, 2 * E], F32, kind="Internal").ap()
    qk = nc.dram_tensor("kq_transposed", [P, T, 2 * E], F32, kind="Internal").ap()
    am = nc.dram_tensor("a_blocks", [P, T, P], F32, kind="Internal").ap()
    tt = nc.dram_tensor("t_blocks", [T, CT * HB, C * C], F32, kind="Internal").ap()
    with ExitStack() as st:
        def sb(n, s, t):
            return st.enter_context(nc.sbuf_tensor(n, s, t))

        def sem(n):
            return st.enter_context(nc.semaphore(n))

        k = {}
        setup(nc, k, d, sb, sem)
        x_res = sb("x_res", [P, T, E], F32)
        with nc.sbuf_tensor("v17", [P, T, H, DH + 1], F32) as v17:
            project(nc, k, d, sem, x_res, v17, [qk_parts[i] for i in range(3)])
            attention(nc, k, d, sem, v17, [qk_parts[i] for i in range(3)], ot)
        layer0_out(nc, k, d, sem, x_res, ot)
        gam = sb("gam", [P, T, HB], F32)
        layer1_front(nc, k, d, sem, x_res, gam, kn, vk, am, qk)
        solve_chunks(nc, k, d, sem, am, tt)
        o_all = sb("o_all", [P, T, E], F32)
        delta_rule(nc, k, d, sem, gam, o_all, kn, vk, qk, tt)
        layer1_back(nc, k, d, sem, x_res, o_all, out)


def constants():
    import numpy as np
    i = np.arange(P)
    late = (i[None, :] > i[:, None]).astype(np.float32) * np.float32(NEG)
    inv = (np.float32(1.0) / np.float32(10000.0) ** (np.arange(0, DK, 2, dtype=np.float32) / np.float32(DK)))
    ang = np.arange(S, dtype=np.float32)[:, None] * inv.astype(np.float32)[None, :]
    same = i[:, None] // C == i[None, :] // C
    return {
        "c_ident": np.eye(P, dtype=np.float32),
        "c_mask": np.stack([late, late.T]),
        "c_lower": np.tril(np.ones((NEXP, NEXP), np.float32), -1),
        "c_cos": np.cos(ang).astype(np.float32),
        "c_sin": np.sin(ang).astype(np.float32),
        "c_trim": -(i[:, None] % C > np.arange(C)[None, :]).astype(np.float32),
        "c_causal": (same & (i[:, None] <= i[None, :])).astype(np.float32),
        "c_id64": (i[:, None] % DK == np.arange(DK)[None, :]).astype(np.float32),
        "c_chunk": (i[:, None] // C == np.arange(CT)[None, :]).astype(np.float32) / C,
    }


def kernel(**inputs):
    import numpy as _np
    import concourse.bacc as _bacc
    from concourse import mybir as _mybir
    from concourse.bass_utils import run_bass_kernel_spmd as _run

    nc = _bacc.Bacc("TRN2", target_bir_lowering=False, num_devices=1)
    given = {n: _np.asarray(a) for n, a in inputs.items()}
    given["L1_ffn_weight_q"] = _np.ascontiguousarray(given["L1_ffn_weight_q"]).view(_np.int32)
    given.update(constants())
    arrays, d = {}, {}
    for name, a in given.items():
        a = _np.ascontiguousarray(a)
        arrays[f"in_{name}_dram"] = a
        d[name] = nc.dram_tensor(f"in_{name}_dram", a.shape, _mybir.dt.from_np(a.dtype), kind="ExternalInput").ap()
    out = nc.dram_tensor("out_0_dram", (1, S, E), _mybir.dt.float32, kind="ExternalOutput").ap()
    build(nc, d, out)
    r = _run(nc, [arrays], core_ids=[0])
    return r.results[0]["out_0_dram"]
```

```python
import concourse.bass as bass
from concourse import mybir
from contextlib import ExitStack


F32 = mybir.dt.float32
BF16 = mybir.dt.bfloat16
ACT = mybir.ActivationFunctionType
ALU = mybir.AluOpType
AX = mybir.AxisListType

P = 128
S, E = 4096, 256
T = S // P
G = S // 512
J = 4
EH = E // P
H, DH = 16, 16
HID = 128
GW = 16
LN_EPS = 1e-5
NEG = -1e30


class Steps:

    def __init__(self, *names, back=1):
        self.primed = back * len(names)
        self.at = {n: i + 1 for i, n in enumerate(names)}
        self.n = len(names)

    def __call__(self, turn, name):
        return turn * self.n + self.primed + self.at[name]


def bcast(ap, n):
    return ap.rearrange("(o c) -> o c", o=1).broadcast_to([n, ap.shape[0]])


def setup(nc, k, d, sb, sem):
    ld = sem("loaded_weights")
    n_ld = [0]

    def load(q, dst, src):
        q.dma_start(dst, src, allow_slow_non_contiguous=True).then_inc(ld, 16)
        n_ld[0] += 16

    for l in (0, 1):
        k[f"silu{l}"] = sb(f"silu{l}", [P, EH], F32)
        k[f"silubc{l}"] = sb(f"silubc{l}", [P, EH, P], F32)
        k[f"mod{l}"] = sb(f"mod{l}", [P, 12], F32)
        k[f"ga{l}"] = sb(f"ga{l}", [P, E], F32)
        k[f"gb{l}"] = sb(f"gb{l}", [P, E], F32)
    k["cb1"] = sb("cb1", [P, E], F32)
    k["sb1"] = sb("sb1", [P, E], F32)
    k["ident"] = sb("ident", [P, P], F32)
    k["identb"] = sb("identb", [P, P], BF16)
    k["ones"] = sb("ones", [P, P], F32)

    with ExitStack() as st:
        c = [st.enter_context(nc.sbuf_tensor(f"c{l}", [P, EH], F32)) for l in (0, 1)]
        wm = [st.enter_context(nc.sbuf_tensor(f"wm{l}", [P, EH, 6 * E], F32)) for l in (0, 1)]
        tmp = st.enter_context(nc.sbuf_tensor("sgn", [P, 4, E], F32))
        raw = st.enter_context(nc.sbuf_tensor("rawrow", [P, 4, E], F32))
        colp = st.enter_context(nc.psum_tensor("colp", [P, 2, 512], F32))
        rowp = st.enter_context(nc.psum_tensor("rowp", [P, 6, 512], F32))
        silu_done, mm_done, v_done, id_done = sem("silu_done"), sem("modmm_done"), sem("mod_done"), sem("id_done")
        block = st.enter_context(nc.Block())
        rows = [(0, 2), (0, 5), (1, 2), (1, 5), (1, 4), (1, 3)]

        @block.sync
        def _(sp):
            for l in (0, 1):
                load(sp, c[l][:], d[f"L{l}_c"].rearrange("o (h p) -> p (o h)", p=P))
                load(sp, wm[l][:], d[f"L{l}_wmod"].rearrange("(h p) n -> p h n", p=P))
            load(sp, k["ident"][:], d["c_ident"])

        @block.gpsimd
        def _(pool):
            nc.gpsimd.memset(k["ones"][:], 1.0).then_inc(id_done, 1)

        @block.scalar
        def _(act):
            act.wait_ge(ld, 16 * 5)
            for l in (0, 1):
                last = nc.scalar.activation(k[f"silu{l}"][:], c[l][:], ACT.Silu)
            last.then_inc(silu_done, 1)

        @block.vector
        def _(dve):
            dve.wait_ge(ld, 16 * 5)
            nc.vector.tensor_copy(k["identb"][:], k["ident"][:]).then_inc(id_done, 1)
            dve.wait_ge(silu_done, 1)
            dve.wait_ge(id_done, 2)
            for l in (0, 1):
                for h in range(EH):
                    last = nc.vector.tensor_scalar(k[f"silubc{l}"][:, h, :], k["ones"][:],
                                                   k[f"silu{l}"][:, h:h + 1], None, ALU.mult)
            last.then_inc(v_done, 1)
            dve.wait_ge(mm_done, 1)
            for l in (0, 1):
                nc.vector.tensor_copy(k[f"mod{l}"][:], colp[:, l, 0:12])
            for i in range(4):
                nc.vector.tensor_copy(raw[:, i, :], rowp[:, i, 0:E])
            nc.vector.tensor_scalar(k["cb1"][:], rowp[:, 4, 0:E], 1.0, None, ALU.add)
            nc.vector.tensor_copy(k["sb1"][:], rowp[:, 5, 0:E]).then_inc(v_done, 1)
            dve.wait_ge(v_done, 2)
            for l in (0, 1):
                for w in (1, 4):
                    nc.vector.tensor_scalar(k[f"mod{l}"][:, 2 * w:2 * w + 2], k[f"mod{l}"][:, 2 * w:2 * w + 2],
                                            1.0, None, ALU.add)
            nc.vector.tensor_scalar(tmp[:], raw[:], 0.0, 2.0, ALU.is_ge, ALU.mult).then_inc(v_done, 1)
            dve.wait_ge(v_done, 3)
            nc.vector.scalar_tensor_tensor(raw[:], raw[:], -1.0, raw[:], ALU.mult, ALU.max)
            nc.vector.tensor_scalar(tmp[:], tmp[:], -1.0, None, ALU.add).then_inc(v_done, 1)
            dve.wait_ge(v_done, 4)
            for i, name in enumerate(("ga0", "gb0", "ga1", "gb1")):
                last = nc.vector.scalar_tensor_tensor(k[name][:], raw[:, i, :], 0.25, tmp[:, i, :], ALU.max, ALU.mult)
            last.then_inc(v_done, 1)

        @block.tensor
        def _(pe):
            pe.wait_ge(v_done, 1)
            for l in (0, 1):
                for m in range(12):
                    for h in range(EH):
                        nc.tensor.matmul(colp[:, l, m:m + 1], wm[l][:, h, m * P:(m + 1) * P],
                                         k[f"silu{l}"][:, h:h + 1], start=(h == 0), stop=(h == 1))
            for i, (l, w) in enumerate(rows):
                for h in range(EH):
                    last = nc.tensor.matmul(rowp[:, i, 0:E], k[f"silubc{l}"][:, h, :],
                                            wm[l][:, h, w * E:(w + 1) * E], start=(h == 0), stop=(h == 1))
            last.then_inc(mm_done, 1)


def project(nc, k, d, sem, x_res, v17, qk_dram):
    V = Steps("stats", "aggr", "rstd", "xn", "r1_0", "r1_1", "r1_2", "r1_3", "v", "haggr", "hrstd", "hn")
    A = Steps("std", "hT", "hi_0", "mid_0", "hi_1", "mid_1", "hi_2", "mid_2", "hi_3", "mid_3", "hstd")
    M = Steps("tp", "qk_0", "qk_1", "qk_2", "qk_3", "vh_01", "vh_23")
    with ExitStack() as st:
        def sb(n, s, t=F32):
            return st.enter_context(nc.sbuf_tensor(f"project_{n}", s, t))
        def ps(n, s, t=F32):
            return st.enter_context(nc.psum_tensor(f"project_{n}", s, t))
        wqk = sb("wqk", [P, EH, 2, E])
        wvh = sb("wvh", [P, EH, E + HID])
        bqk = sb("bqk", [P, 4])
        bvh = sb("bvh", [1, E + HID])
        rows = sb("rows", [P, 3, HID])
        grow = sb("grow", [P, 3, GW])
        g2 = sb("g2", [P, 2])
        st6 = sb("st6", [P, J, 6]); mv = sb("mv", [P, J, 2]); sd = sb("sd", [P, J]); rs = sb("rs", [P, J])
        hs6 = sb("hs6", [P, J, 6]); hmv = sb("hmv", [P, J, 2]); hsd = sb("hsd", [P, J]); hrs = sb("hrs", [P, J])
        xn = sb("xn", [P, J, E])
        hT = sb("hT", [P, EH, 512])
        hi = sb("hi", [P, 4, 512], BF16); mid = sb("mid", [P, 4, 512], BF16); lo = sb("lo", [P, 4, 512], BF16)
        r1 = sb("r1", [P, 4, 512])
        HD = sb("HD", [P, T, HID])
        G1 = sb("G1", [P, T, GW])
        drift = sb("drift", [P, T]); gate = sb("gate", [P, T])
        eps = sb("eps", [P, 1])
        tp = ps("tp", [P, EH, 512]); qkp = ps("qkp", [P, 4, 512]); vhp = ps("vhp", [P, 2, 512])
        xl, wl = sem("x_loaded"), sem("w1_loaded")
        vd, ad, md, pd = sem("p1_dve"), sem("p1_act"), sem("p1_pe"), sem("p1_pool")
        hi_out, mid_out, lo_out = sem("hi_out"), sem("mid_out"), sem("lo_out")
        vd2, ad2, held = sem("p1b_dve"), sem("p1b_act"), sem("aggr_held")
        sheld = sem("project_sp_held")
        block = st.enter_context(nc.Block())
        qk_out = [part.rearrange("(m p) n -> p m n", p=P) for part in qk_dram]

        @block.sync
        def _(sp):
            for h in range(1):
                sp.dma_start(wqk[:, :, 0, :], d["L0_attn_Wq"].rearrange("(h p) n -> p h n", p=P)).then_inc(wl, 16)
                sp.dma_start(wqk[:, :, 1, :], d["L0_attn_Wk"].rearrange("(h p) n -> p h n", p=P)).then_inc(wl, 16)
                sp.dma_start(wvh[:, :, 0:E], d["L0_attn_Wv"].rearrange("(h p) n -> p h n", p=P)).then_inc(wl, 16)
                sp.dma_start(wvh[:, :, E:], d["L0_attn_dp_w1"].rearrange("(h p) n -> p h n", p=P)).then_inc(wl, 16)
            sp.dma_start(bqk[:, 0:2], d["L0_attn_bq"].rearrange("(h p) -> p h", p=P), allow_slow_non_contiguous=True).then_inc(wl, 16)
            sp.dma_start(bqk[:, 2:4], d["L0_attn_bk"].rearrange("(h p) -> p h", p=P), allow_slow_non_contiguous=True).then_inc(wl, 16)
            sp.dma_start(bvh[:, 0:E], d["L0_attn_bv"].rearrange("(o n) -> o n", o=1)).then_inc(wl, 16)
            sp.dma_start(bvh[:, E:], d["L0_attn_dp_b1"].rearrange("(o n) -> o n", o=1)).then_inc(wl, 16)
            for i, n in enumerate(("ln_g", "ln_b")):
                sp.dma_start(rows[:, i, :], bcast(d[f"L0_attn_{n}"], P)).then_inc(wl, 16)
            sp.dma_start(rows[:, 2, :], bcast(d["L0_attn_dp_w2"].rearrange("a o -> (a o)"), P)).then_inc(wl, 16)
            sp.dma_start(grow[:, 0, :], bcast(d["L0_attn_g_w1"].rearrange("o a -> (o a)"), P)).then_inc(wl, 16)
            sp.dma_start(grow[:, 1, :], bcast(d["L0_attn_g_b1"], P)).then_inc(wl, 16)
            sp.dma_start(grow[:, 2, :], bcast(d["L0_attn_g_w2"].rearrange("a o -> (a o)"), P)).then_inc(wl, 16)
            sp.dma_start(g2[:, 0:1], bcast(d["L0_attn_dp_b2"], P)).then_inc(wl, 16)
            sp.dma_start(g2[:, 1:2], bcast(d["L0_attn_g_b2"], P)).then_inc(wl, 16)
            for out in (hi_out, mid_out, lo_out):
                sp.sem_inc(out, 16)
            with sp.Fori(0, G) as g:
                cols = bass.ds(g * 512, 512)
                sp.wait_ge(ad, A(g, "hi_3"))
                sp.sem_inc(sheld, 1)
                sp.dma_start(qk_out[0][:, :, cols], hi[:]).then_inc(hi_out, 16)
                sp.wait_ge(ad, A(g, "mid_3"))
                sp.dma_start(qk_out[1][:, :, cols], mid[:]).then_inc(mid_out, 16)
                sp.wait_ge(pd, 4 * g + 8)
                sp.dma_start(qk_out[2][:, :, cols], lo[:]).then_inc(lo_out, 16)
            sp.wait_ge(hi_out, 16 * G + 16)
            sp.wait_ge(mid_out, 16 * G + 16)
            sp.wait_ge(lo_out, 16 * G + 16)

        @block.scalar
        def _(act):
            xv = d["L0_attn_x"].rearrange("o (t p) c -> p (o t) c", p=P)
            for g in range(G):
                act.dma_start(x_res[:, J * g:J * g + J, :], xv[:, J * g:J * g + J, :]).then_inc(xl, 16)
            act.wait_ge(wl, 16 * 16)
            act.wait_ge(pd, 4)
            act.sem_inc(ad, A.primed)
            with act.Fori(0, G) as g:
                act.wait_ge(vd, V(g, "aggr"))
                nc.scalar.activation(sd[:], mv[:, :, 1], ACT.Sqrt, bias=eps[:]).then_inc(ad, 1)
                act.wait_ge(md, M(g, "tp"))
                for h in range(EH):
                    last = nc.scalar.activation(hT[:, h, :], tp[:, h, :], ACT.Identity,
                                                bias=k["mod0"][:, h:h + 1], scale=k["mod0"][:, 2 + h:3 + h])
                last.then_inc(ad, 1)
                for m in range(4):
                    act.wait_ge(md, M(g, f"qk_{m}"))
                    act.wait_ge(hi_out, 16 * g + 16)
                    nc.scalar.activation(hi[:, m, :], qkp[:, m, :], ACT.Identity, bias=bqk[:, m:m + 1]).then_inc(ad, 1)
                    act.wait_ge(vd, V(g, f"r1_{m}"))
                    act.wait_ge(mid_out, 16 * g + 16)
                    nc.scalar.activation(mid[:, m, :], r1[:, m, :], ACT.Copy).then_inc(ad, 1)
                act.wait_ge(vd, V(g, "haggr"))
                nc.scalar.activation(hsd[:], hmv[:, :, 1], ACT.Sqrt, bias=eps[:]).then_inc(ad, 1)
            act.wait_ge(vd2, 2)
            nc.scalar.activation(HD[:], HD[:], ACT.Gelu).then_inc(ad2, 1)
            act.wait_ge(vd2, 6)
            nc.scalar.activation(G1[:], G1[:], ACT.Gelu).then_inc(ad2, 1)
            act.wait_ge(vd2, 8)
            nc.scalar.activation(gate[:], gate[:], ACT.Tanh, bias=g2[:, 1:2]).then_inc(ad2, 1)

        @block.gpsimd
        def _(pool):
            nc.gpsimd.memset(eps[:], LN_EPS)
            nc.gpsimd.memset(v17[:, :, :, DH:DH + 1], 1.0).then_inc(pd, 4)
            with pool.Fori(0, G) as g:
                for m in range(4):
                    pool.wait_ge(ad, A(g, f"mid_{m}"))
                    pool.wait_ge(lo_out, 16 * g + 16)
                    nc.gpsimd.tensor_tensor(lo[:, m, :], r1[:, m, :], mid[:, m, :], ALU.subtract).then_inc(pd, 1)

        @block.vector
        def _(dve):
            dve.sem_inc(vd, V.primed)
            with dve.Fori(0, G) as g:
                xt = x_res[:, bass.ds(g * J, J), :]
                dve.wait_ge(xl, 16 * G)
                for j in range(J):
                    last = nc.vector.bn_stats(st6[:, j, :], xt[:, j, :])
                last.then_inc(vd, 1)
                dve.wait_ge(vd, V(g, "stats"))
                dve.wait_ge(ad, A(g - 1, "std"))
                dve.sem_inc(held, 1)
                for j in range(J):
                    last = nc.vector.bn_aggr(mv[:, j, :], st6[:, j, :])
                last.then_inc(vd, 1)
                dve.wait_ge(ad, A(g, "std"))
                nc.vector.reciprocal(rs[:], sd[:]).then_inc(vd, 1)
                dve.wait_ge(vd, V(g, "rstd"))
                dve.wait_ge(md, M(g - 1, "tp"))
                for j in range(J):
                    last = nc.vector.tensor_scalar(xn[:, j, :], xt[:, j, :], mv[:, j, 0:1], rs[:, j:j + 1],
                                                   ALU.subtract, ALU.mult)
                last.then_inc(vd, 1)
                for m in range(4):
                    dve.wait_ge(ad, A(g, f"hi_{m}"))
                    dve.wait_ge(pd, 4 * g + m + 1)
                    nc.vector.scalar_tensor_tensor(r1[:, m, :], qkp[:, m, :], bqk[:, m:m + 1], hi[:, m, :],
                                                   ALU.add, ALU.subtract).then_inc(vd, 1)
                for j in range(J):
                    if j % 2 == 0:
                        dve.wait_ge(md, M(g, "vh_01" if j == 0 else "vh_23"))
                    src = vhp[:, j % 2, :] if j < 2 else tp[:, j % 2, :]
                    nc.vector.tensor_copy(v17[:, bass.ds(g * J + j, 1), :, 0:DH],
                                          src[:, 0:E].rearrange("p (o h c) -> p o h c", o=1, c=DH))
                    last = nc.vector.bn_stats(hs6[:, j, :], src[:, E:E + HID])
                last.then_inc(vd, 1)
                dve.wait_ge(vd, V(g, "v"))
                dve.sem_inc(held, 1)
                for j in range(J):
                    last = nc.vector.bn_aggr(hmv[:, j, :], hs6[:, j, :])
                last.then_inc(vd, 1)
                dve.wait_ge(ad, A(g, "hstd"))
                nc.vector.reciprocal(hrs[:], hsd[:]).then_inc(vd, 1)
                dve.wait_ge(vd, V(g, "hrstd"))
                for j in range(J):
                    src = vhp[:, j % 2, :] if j < 2 else tp[:, j % 2, :]
                    last = nc.vector.tensor_scalar(HD[:, bass.ds(g * J + j, 1), :],
                                                   src[:, E:E + HID].rearrange("p (o c) -> p o c", o=1),
                                                   hmv[:, j, 0:1], hrs[:, j:j + 1], ALU.subtract, ALU.mult)
                last.then_inc(vd, 1)
            row = lambda i: rows[:, i:i + 1, :].broadcast_to([P, T, HID])
            wide = lambda i: grow[:, i:i + 1, :].broadcast_to([P, T, GW])
            dve.wait_ge(vd, V(G - 1, "hn"))
            nc.vector.tensor_tensor(HD[:], HD[:], row(0), ALU.mult).then_inc(vd2, 1)
            dve.wait_ge(vd2, 1)
            nc.vector.tensor_tensor(HD[:], HD[:], row(1), ALU.add).then_inc(vd2, 1)
            dve.wait_ge(ad2, 1)
            nc.vector.tensor_tensor(HD[:], HD[:], row(2), ALU.mult).then_inc(vd2, 1)
            dve.wait_ge(vd2, 3)
            nc.vector.tensor_reduce(drift[:], HD[:], AX.X, ALU.add).then_inc(vd2, 1)
            dve.wait_ge(vd2, 4)
            dr = drift[:].rearrange("p (t o) -> p t o", o=1).broadcast_to([P, T, GW])
            nc.vector.scalar_tensor_tensor(G1[:], dr, g2[:, 0:1], wide(0), ALU.add, ALU.mult).then_inc(vd2, 1)
            dve.wait_ge(vd2, 5)
            nc.vector.tensor_tensor(G1[:], G1[:], wide(1), ALU.add).then_inc(vd2, 1)
            dve.wait_ge(ad2, 2)
            nc.vector.tensor_tensor(G1[:], G1[:], wide(2), ALU.mult).then_inc(vd2, 1)
            dve.wait_ge(vd2, 7)
            nc.vector.tensor_reduce(gate[:], G1[:], AX.X, ALU.add).then_inc(vd2, 1)
            dve.wait_ge(ad2, 3)
            vv = v17[:, :, :, 0:DH]
            nc.vector.tensor_tensor(vv, vv, gate[:].rearrange("p (t o c) -> p t o c", o=1, c=1)
                                    .broadcast_to([P, T, H, DH]), ALU.mult).then_inc(vd2, 1)

        @block.tensor
        def _(pe):
            pe.wait_ge(wl, 16 * 16)
            pe.sem_inc(md, M.primed)
            with pe.Fori(0, G) as g:
                pe.wait_ge(vd, V(g, "xn"))
                pe.wait_ge(vd, V(g - 1, "hn"))
                for h in range(EH):
                    for j in range(J):
                        last = nc.tensor.transpose(tp[:, h, j * P:(j + 1) * P], xn[:, j, h * P:(h + 1) * P],
                                                   k["ident"][:])
                last.then_inc(md, 1)
                pe.wait_ge(ad, A(g, "hT"))
                for m in range(4):
                    pe.wait_ge(vd, V(g - 1, f"r1_{m}"))
                    for h in range(EH):
                        last = nc.tensor.matmul(qkp[:, m, :], wqk[:, h, m // 2, (m % 2) * P:(m % 2) * P + P],
                                                hT[:, h, :], start=(h == 0), stop=(h == 1))
                    last.then_inc(md, 1)
                for j in range(J):
                    dst = (vhp if j < 2 else tp)[:, j % 2, 0:E + HID]
                    nc.tensor.matmul(dst, k["ones"][0:1, :], bvh[:], start=True, stop=False)
                    for h in range(EH):
                        last = nc.tensor.matmul(dst, hT[:, h, j * P:(j + 1) * P], wvh[:, h, :],
                                                start=False, stop=(h == 1))
                    if j % 2:
                        last.then_inc(md, 1)


def attention(nc, k, d, sem, v17, qk_dram, ot_dram):
    ROWS = 6 * DH
    MAXR = ROWS + 3
    KPARTS = (0, 0, 0, 1, 1, 2)
    QPARTS = (0, 1, 2, 0, 1, 0)
    BLK = 1024
    NPT = 4
    units = []
    for s in range(2):
        for kt in range(16 * s + 16):
            for b in range(2):
                q0, q1 = 2048 * s + BLK * b, 2048 * s + BLK * b + BLK
                if kt * P < q1:
                    units.append((s, kt, max(q0, kt * P), q1))
    NE = len(units)
    last_of = [max(i for i, u in enumerate(units) if u[0] == s) for s in range(2)]
    pieces = [(i, c, min(512, P * (i + 1) - 512 * c)) for i in range(T) for c in range(i // 4 + 1)]
    NM = len(pieces) + 1
    SLACK = 10
    share = [min(NM, -(-NM * (u + 1) // (NE - SLACK))) for u in range(NE)]
    LAG = 2
    LOADS = 12 * 16
    NB = 3
    TURNS = H // NB

    with ExitStack() as st:
        def sb(n, s, t=F32):
            return st.enter_context(nc.sbuf_tensor(f"attn_{n}", s, t))
        def ps(n, s, t=F32):
            return st.enter_context(nc.psum_tensor(f"attn_{n}", s, t))
        KX = [sb(f"KX{b}", [P, S], BF16) for b in range(NB)]
        QX = [sb(f"QX{b}", [P, S], BF16) for b in range(NB)]
        VH = [sb(f"VH{b}", [P, T, DH + 1]) for b in range(NB)]
        PT = [sb(f"PT{b}", [P, BLK]) for b in range(NPT)]
        OS = [sb(f"OS{b}", [P, 512]) for b in range(2)]
        maskf = sb("maskf", [P, 2, P]); maskb = sb("maskb", [P, 2, P], BF16)
        pm = sb("pm", [P, T, 8]); nm = sb("nm", [P, T])
        nmT = sb("nmT", [32, P]); rT = sb("rT", [32, P])
        parts = sb("parts", [32, 3, P], BF16)
        ES = [ps(f"ES{b}", [P, BLK]) for b in range(2)]
        MS = [ps(f"MS{b}", [P, 512]) for b in range(3)]
        OP = ps("OP", [P, 512])
        held = sem("pool_held")
        mask_in, ready = sem("mask_in"), sem("attn_ready")
        loaded = [sem(f"qk_loaded{b}") for b in range(NB)]
        max_scores, max_taken, negmax = sem("max_scores"), sem("max_taken"), sem("negmax")
        split, v_copied, max_rows = sem("max_split"), sem("v_copied"), sem("max_rows")
        exp_scores, exp_done, pv_done = sem("exp_scores"), sem("exp_done"), sem("pv_done")
        o_evac, o_out = sem("o_evac"), [sem(f"o_out{s}") for s in range(2)]
        sheld = sem("attn_sp_held")
        block = st.enter_context(nc.Block())

        @block.sync
        def _(sp):
            sp.dma_start(maskf[:], d["c_mask"].rearrange("a p n -> p a n")).then_inc(mask_in, 16)

            def load(h, b):
                for r in range(6):
                    sp.dma_start(KX[b][DH * r:DH * r + DH, :],
                                 qk_dram[KPARTS[r]][bass.ds(E + h * DH, DH), :]).then_inc(loaded[b], 16)
                    sp.dma_start(QX[b][DH * r:DH * r + DH, :],
                                 qk_dram[QPARTS[r]][bass.ds(h * DH, DH), :]).then_inc(loaded[b], 16)

            def store(h, s):
                sp.wait_ge(o_evac, 2 * h + s + 3)
                sp.sem_inc(sheld, 1)
                for j in range(4):
                    sp.dma_start(ot_dram[bass.ds(h * (DH + 1), DH + 1), 2048 * s + 512 * j:2048 * s + 512 * j + 512],
                                 OS[s][32 * j:32 * j + DH + 1, :]).then_inc(o_out[s], 16)

            def turn(h, b, more):
                store(h, 0)
                if more:
                    sp.wait_ge(exp_scores, NE * h + NE)
                    sp.sem_inc(sheld, 1)
                    load(h + NB, b)
                store(h, 1)

            for s in range(2):
                sp.sem_inc(o_out[s], 64 + 64 * s)
            for b in range(NB):
                load(b, b)
            with sp.Fori(0, TURNS - 1) as i:
                for b in range(NB):
                    turn(NB * i + b, b, True)
            for h in range(H - 1 - NB, H):
                turn(h, h % NB, h + NB < H)
            for s in range(2):
                sp.wait_ge(o_out[s], 64 * H + 64 + 64 * s)

        @block.gpsimd
        def _(pool):
            for b in range(NB):
                nc.gpsimd.memset(KX[b][ROWS:MAXR, :], 1.0).then_inc(ready, 1)

            def split_max(h, b):
                pool.wait_ge(pv_done, NE * h + NE)
                nc.gpsimd.tensor_copy(VH[b][:].rearrange("p t (o c) -> p t o c", o=1),
                                      v17[:, :, bass.ds(h, 1), :]).then_inc(v_copied, 1)
                pool.wait_ge(max_taken, NM * h + NM)
                pool.sem_inc(held, 1)
                nc.gpsimd.tensor_scalar(parts[:, 0, :], nmT[:], 1.0, None, ALU.mult).then_inc(split, 1)
                pool.wait_ge(split, 4 * h + 5)
                nc.gpsimd.tensor_tensor(rT[:], nmT[:], parts[:, 0, :], ALU.subtract).then_inc(split, 1)
                pool.wait_ge(split, 4 * h + 6)
                pool.sem_inc(held, 1)
                nc.gpsimd.tensor_scalar(parts[:, 1, :], rT[:], 1.0, None, ALU.mult).then_inc(split, 1)
                pool.wait_ge(split, 4 * h + 7)
                nc.gpsimd.tensor_tensor(parts[:, 2, :], rT[:], parts[:, 1, :], ALU.subtract).then_inc(split, 1)
                pool.wait_ge(split, 4 * h + 8)
                pool.sem_inc(held, 1)
                for r in range(3):
                    pool.dma_start(QX[b][ROWS + r:ROWS + r + 1, :].rearrange("o (t c) -> o t c", c=P),
                                   parts[:, r, :]).then_inc(max_rows, 16)
            pool.sem_inc(split, 4)
            with pool.Fori(0, TURNS) as i:
                for b in range(NB):
                    split_max(NB * i + b, b)
            split_max(H - 1, (H - 1) % NB)

        @block.scalar
        def _(act):
            def take_out(e, pv_count, out_count):
                act.wait_ge(pv_done, pv_count)
                act.wait_ge(o_out[e], out_count)
                nc.scalar.activation(OS[e][:], OP[:], ACT.Copy).then_inc(o_evac, 1)

            act.sem_inc(o_evac, 1)
            with act.Fori(0, H) as h:
                for u, (s, kt, q0, q1) in enumerate(units):
                    w = q1 - q0
                    act.wait_ge(exp_scores, NE * h + u + 1)
                    act.wait_ge(pv_done, NE * h + u - NPT + 1 + 3 * NE)
                    nc.scalar.activation(PT[u % NPT][:, BLK - w:], ES[u % 2][:, BLK - w:], ACT.Exp,
                                         scale=DH ** -0.5).then_inc(exp_done, 1)
                    if u == 1:
                        take_out(1, NE * h + 3 * NE, 64 * h + 64)
                    if u == last_of[0] + LAG:
                        take_out(0, NE * h + last_of[0] + 1 + 3 * NE, 64 * h + 64)
            take_out(1, NE * H + 3 * NE, 64 * H + 64)

        @block.vector
        def _(dve):
            dve.wait_ge(mask_in, 16)
            nc.vector.tensor_copy(maskb[:], maskf[:])
            nc.vector.memset(OP[:], 0.0)
            nc.vector.memset(pm[:], NEG).then_inc(ready, 1)

            with dve.Fori(0, H) as h:
                for n, (i, c, w) in enumerate(pieces):
                    dve.wait_ge(max_scores, NM * h + n + 1)
                    nc.vector.tensor_reduce(pm[:, i, c:c + 1], MS[n % 3][:, 0:w], AX.X, ALU.max).then_inc(max_taken, 1)
                dve.wait_ge(max_taken, NM * h + NM - 1)
                nc.vector.tensor_reduce(nm[:], pm[:], AX.X, ALU.max, negate=True).then_inc(negmax, 1)
                dve.wait_ge(max_scores, NM * h + NM)
                dve.wait_ge(split, 4 * h + 4)
                nc.vector.tensor_copy(nmT[:], MS[(NM - 1) % 3][0:T, 0:P]).then_inc(max_taken, 1)

        @block.tensor
        def _(pe):
            def max_piece(h, b, n):
                if n < 3:
                    if not (isinstance(h, int) and h == 0):
                        pe.wait_ge(max_taken, NM * h)
                else:
                    pe.wait_ge(max_taken, NM * h + n - 2)
                if n == NM - 1:
                    pe.wait_ge(negmax, h + 1)
                    nc.tensor.transpose(MS[n % 3][0:T, 0:P], nm[:], k["ident"][:]).then_inc(max_scores, 1)
                    return
                i, c, w = pieces[n]
                diag = c == i // 4
                if diag:
                    nc.tensor.matmul(MS[n % 3][:, w - P:w], k["identb"][:], maskb[:, 0, :],
                                     start=True, stop=False, skip_group_check=True)
                last = nc.tensor.matmul(MS[n % 3][:, 0:w], QX[b][0:ROWS, i * P:(i + 1) * P],
                                        KX[b][0:ROWS, 512 * c:512 * c + w], start=not diag, stop=True,
                                        skip_group_check=True)
                last.then_inc(max_scores, 1)

            def scores(h, b, u):
                s, kt, q0, q1 = units[u]
                if u == 0:
                    pe.wait_ge(max_rows, 48 * h + 48)
                if u < 2:
                    if not (isinstance(h, int) and h == 0):
                        pe.wait_ge(exp_done, NE * h)
                else:
                    pe.wait_ge(exp_done, NE * h + u - 1)
                for c in (q1 - BLK, q1 - 512):
                    a = max(c, q0)
                    if a >= c + 512:
                        continue
                    o = a - (q1 - BLK)
                    diag = c <= kt * P
                    if diag:
                        nc.tensor.matmul(ES[u % 2][:, o:o + P], k["identb"][:], maskb[:, 1, :],
                                         start=True, stop=False, skip_group_check=True)
                    last = nc.tensor.matmul(ES[u % 2][:, o:o + c + 512 - a], KX[b][0:MAXR, kt * P:(kt + 1) * P],
                                            QX[b][0:MAXR, a:c + 512], start=not diag, stop=True,
                                            skip_group_check=True)
                last.then_inc(exp_scores, 1)

            def pv(h, b, u):
                s, kt, q0, q1 = units[u]
                if u == 0:
                    pe.wait_ge(v_copied, h + 1)
                    pe.wait_ge(o_evac, 2 * h + 2)
                if u == last_of[0] + 1:
                    pe.wait_ge(o_evac, 2 * h + 3)
                pe.wait_ge(exp_done, NE * h + u + 1)
                for c in (q1 - BLK, q1 - 512):
                    a = max(c, q0)
                    if a >= c + 512:
                        continue
                    j = c // 512 % 4
                    last = nc.tensor.matmul(OP[32 * j:32 * j + DH + 1, a - c:512], VH[b][:, kt, :],
                                            PT[u % NPT][:, a - (q1 - BLK):c + 512 - (q1 - BLK)],
                                            start=(kt == 0), stop=(kt >= c // P), skip_group_check=True)
                last.then_inc(pv_done, 1)

            pe.wait_ge(ready, NB + 1)
            pe.sem_inc(pv_done, 3 * NE)
            pe.wait_ge(loaded[0], LOADS)
            for n in range(NM):
                max_piece(0, 0, n)
            scores(0, 0, 0)
            scores(0, 0, 1)

            def turn(h, i, b):
                more = b is not None
                b = b or 0
                if more:
                    pe.wait_ge(loaded[(b + 1) % NB], LOADS * (i + 1 + (b + 1) // NB))
                for u in range(NE):
                    if more:
                        for n in range(share[u - 1] if u else 0, share[u]):
                            max_piece(h + 1, (b + 1) % NB, n)
                    if u + 2 < NE:
                        scores(h, b, u + 2)
                    elif more:
                        scores(h + 1, (b + 1) % NB, u + 2 - NE)
                    if u >= LAG:
                        pv(h, b, u - LAG)
                for u in range(NE - LAG, NE):
                    pv(h, b, u)
            with pe.Fori(0, TURNS) as i:
                for b in range(NB):
                    turn(NB * i + b, i, b)
            turn(H - 1, TURNS, None)


NEXP = 8


def layer0_out(nc, k, d, sem, x_res, ot_dram):
    FV = Steps("rl_0", "rl_1", "att", "x1", "stats", "aggr", "rstd", "xn", back=0)
    FA = Steps("std", "hT", back=0)
    FM = Steps("wo", "tp", back=0)
    V = Steps("lmax", "lsub", "esum", "erec", "p", "gt", "eq", "eqm", "cnt", "rank", "w", "s_0", "s_1", "s_2", "s_3",
              *[f"acc_{j}_{e}" for j in range(J) for e in range(NEXP + 1)])
    A = Steps("exp", "sg_0", "sg_1", "sg_2", "sg_3")
    M = Steps("lg", "ab_0", "ab_1", "ab_2", "ab_3",
              *[n for j in range(J) for n in (f"sh_{j}", *[f"ex_{j}_{e}" for e in range(NEXP // 2)])])
    with ExitStack() as st:
        def sb(n, s, t=F32):
            return st.enter_context(nc.sbuf_tensor(f"l0out_{n}", s, t))
        def ps(n, s, t=F32):
            return st.enter_context(nc.psum_tensor(f"l0out_{n}", s, t))
        wo = sb("wo", [P, EH, E]); bo = sb("bo", [1, E])
        w_in = sb("w_in", [P, EH, 2, 2 * E]); w_so = sb("w_so", [P, EH, E]); w2 = sb("w2", [P, EH, NEXP, E])
        wg = sb("wg", [P, EH, NEXP]); bg = sb("bg", [1, NEXP])
        lower = sb("lower", [P, NEXP, NEXP])
        OTg = sb("OTg", [P, EH, 512]); LB = sb("LB", [P, EH, 512])
        st6 = sb("st6", [P, J, 6]); mv = sb("mv", [P, J, 2]); sd = sb("sd", [P, J]); rs = sb("rs", [P, J])
        eps = sb("eps", [P, 1])
        xn = sb("xn", [P, J, E]); hT = sb("hT", [P, EH, 512])
        sg = sb("sg", [P, 2, 512]); sT = sb("sT", [P, 4, 512])
        lm = sb("lm", [P, J, 1]); lx = sb("lx", [P, J, NEXP]); es = sb("es", [P, J, 1]); er = sb("er", [P, J, 1])
        p = sb("p", [P, J, NEXP]); gt = sb("gt", [P, J, NEXP, NEXP]); eq = sb("eq", [P, J, NEXP, NEXP])
        rank = sb("rank", [P, J, NEXP]); w = sb("w", [P, J, NEXP])
        tp = ps("tp", [P, EH, 512]); ring = ps("ring", [P, 4, 512]); shp = ps("shp", [P, 512]); lgp = ps("lgp", [P, 512])
        wl, scaled, eps_set = sem("w3_loaded"), sem("w3_scaled"), sem("eps_set")
        ol = sem("attn_loaded")
        vd, ad, md, held = sem("p3_dve"), sem("p3_act"), sem("p3_pe"), sem("p3_held")
        fvd, fad, fmd = sem("p3_front_dve"), sem("p3_front_act"), sem("p3_front_pe")
        sheld = sem("l0out_sp_held")
        block = st.enter_context(nc.Block())
        NWL = 16 * 10
        ot3 = ot_dram.rearrange("(h r) q -> h r q", r=DH + 1)

        @block.sync
        def _(sp):
            def w(dst, src):
                sp.dma_start(dst, src).then_inc(wl, 16)
            w(wo[:], d["L0_attn_Wo"].rearrange("(h p) n -> p h n", p=P))
            w(bo[:], d["L0_attn_bo"].rearrange("(o n) -> o n", o=1))
            w(w_in[:, :, 0, :], d["L0_ffn_w_shared_in"].rearrange("(h p) n -> p h n", p=P))
            w(w_in[:, :, 1, :], d["L0_ffn_w1_shared"].rearrange("(h p) n -> p h n", p=P))
            w(w_so[:], d["L0_ffn_w_shared_out"].rearrange("(h p) n -> p h n", p=P))
            for h in range(EH):
                w(w2[:, h, :, :], d["L0_ffn_w2"][:, h * P:(h + 1) * P, :].rearrange("e p n -> p e n"))
            w(wg[:], d["L0_ffn_w_gate"].rearrange("(h p) n -> p h n", p=P))
            w(bg[:], d["L0_ffn_gate_bias"].rearrange("(o n) -> o n", o=1))
            w(lower[:], d["c_lower"].rearrange("(o a) b -> o a b", o=1).broadcast_to([P, NEXP, NEXP]))

            def load(g):
                cols = bass.ds(g * 512, 512)
                for h in range(EH):
                    hs = slice(8 * h, 8 * h + 8)
                    sp.dma_start(OTg[:, h, :], ot3[hs, 0:DH, cols]).then_inc(ol, 16)
                    sp.dma_start(LB[:, h, :], ot3[hs, DH:DH + 1, cols].broadcast_to([8, DH, 512])).then_inc(ol, 16)
            load(0)
            with sp.Fori(1, G) as g:
                sp.wait_ge(fmd, FM(g - 1, "wo"))
                sp.sem_inc(sheld, 1)
                load(g)

        @block.gpsimd
        def _(pool):
            nc.gpsimd.memset(eps[:], LN_EPS).then_inc(eps_set, 1)

        @block.scalar
        def _(act):
            act.wait_ge(eps_set, 1)
            def front(g):
                act.wait_ge(fvd, FV(g, "aggr"))
                nc.scalar.activation(sd[:], mv[:, :, 1], ACT.Sqrt, bias=eps[:]).then_inc(fad, 1)
                act.wait_ge(fmd, FM(g, "tp"))
                for h in range(EH):
                    last = nc.scalar.activation(hT[:, h, :], tp[:, h, :], ACT.Identity,
                                                bias=k["mod0"][:, 6 + h:7 + h], scale=k["mod0"][:, 8 + h:9 + h])
                last.then_inc(fad, 1)

            def network(g):
                act.wait_ge(vd, V(g, "lsub"))
                nc.scalar.activation(lx[:], lx[:], ACT.Exp).then_inc(ad, 1)
                for i in range(4):
                    act.wait_ge(md, M(g, f"ab_{i}"))
                    if i < 2:
                        act.wait_ge(vd, V(g - 1, f"s_{i + 2}"))
                    else:
                        act.wait_ge(vd, V(g, f"s_{i - 2}"))
                    nc.scalar.activation(sg[:, i % 2, :], ring[:, 2 * (i % 2), :], ACT.Silu).then_inc(ad, 1)

            act.sem_inc(ad, A.primed)
            front(0)
            with act.Fori(0, G - 1) as g:
                network(g)
                front(g + 1)
            network(G - 1)

        @block.vector
        def _(dve):
            dve.wait_ge(wl, NWL)
            nc.vector.tensor_tensor(wo[:], wo[:], k["ga0"][:].rearrange("p (o c) -> p o c", o=1)
                                    .broadcast_to([P, EH, E]), ALU.mult)
            nc.vector.tensor_tensor(bo[:], bo[:], k["ga0"][0:1, :], ALU.mult)
            nc.vector.tensor_tensor(w_so[:], w_so[:], k["gb0"][:].rearrange("p (o c) -> p o c", o=1)
                                    .broadcast_to([P, EH, E]), ALU.mult)
            for h in range(EH):
                last = nc.vector.tensor_tensor(w2[:, h, :, :], w2[:, h, :, :],
                                               k["gb0"][:].rearrange("p (o c) -> p o c", o=1)
                                               .broadcast_to([P, NEXP, E]), ALU.mult)
            last.then_inc(scaled, 1)
            def divide(g, part):
                if part < 2:
                    dve.wait_ge(ol, 64 * g + 64)
                    nc.vector.reciprocal(LB[:, part, :], LB[:, part, :]).then_inc(fvd, 1)
                else:
                    dve.wait_ge(fvd, FV(g, "rl_1"))
                    nc.vector.tensor_tensor(OTg[:], OTg[:], LB[:], ALU.mult).then_inc(fvd, 1)

            def residual(g):
                xt = x_res[:, bass.ds(g * J, J), :]
                dve.wait_ge(fmd, FM(g, "wo"))
                for a in range(2):
                    last = nc.vector.tensor_tensor(xt[:, 2 * a:2 * a + 2, :], xt[:, 2 * a:2 * a + 2, :],
                                                   tp[:, a, :].rearrange("p (j c) -> p j c", j=2), ALU.add)
                last.then_inc(fvd, 1)
                dve.wait_ge(fvd, FV(g, "x1"))
                dve.sem_inc(held, 1)
                for j in range(J):
                    last = nc.vector.bn_stats(st6[:, j, :], xt[:, j, :])
                last.then_inc(fvd, 1)
                dve.wait_ge(fvd, FV(g, "stats"))
                dve.sem_inc(held, 1)
                for j in range(J):
                    last = nc.vector.bn_aggr(mv[:, j, :], st6[:, j, :])
                last.then_inc(fvd, 1)

            def normalise(g):
                xt = x_res[:, bass.ds(g * J, J), :]
                dve.wait_ge(fad, FA(g, "std"))
                nc.vector.reciprocal(rs[:], sd[:]).then_inc(fvd, 1)
                dve.wait_ge(fvd, FV(g, "rstd"))
                for j in range(J):
                    last = nc.vector.tensor_scalar(xn[:, j, :], xt[:, j, :], mv[:, j, 0:1], rs[:, j:j + 1],
                                                   ALU.subtract, ALU.mult)
                last.then_inc(fvd, 1)

            def route(g):
                dve.wait_ge(md, M(g, "lg"))
                lg = lgp[:, 0:J * NEXP].rearrange("p (j e) -> p j e", e=NEXP)
                nc.vector.tensor_reduce(lm[:, :, 0], lg, AX.X, ALU.max).then_inc(vd, 1)
                dve.wait_ge(vd, V(g, "lmax"))
                nc.vector.tensor_tensor(lx[:], lg, lm[:].broadcast_to([P, J, NEXP]), ALU.subtract).then_inc(vd, 1)
                dve.wait_ge(ad, A(g, "exp"))
                nc.vector.tensor_reduce(es[:, :, 0], lx[:], AX.X, ALU.add).then_inc(vd, 1)
                dve.wait_ge(vd, V(g, "esum"))
                nc.vector.reciprocal(er[:], es[:]).then_inc(vd, 1)
                dve.wait_ge(vd, V(g, "erec"))
                nc.vector.tensor_tensor(p[:], lx[:], er[:].broadcast_to([P, J, NEXP]), ALU.mult).then_inc(vd, 1)
                dve.wait_ge(vd, V(g, "p"))
                pj = p[:].rearrange("p j (o e) -> p j o e", o=1).broadcast_to([P, J, NEXP, NEXP])
                pe_ = p[:].rearrange("p j (e o) -> p j e o", o=1).broadcast_to([P, J, NEXP, NEXP])
                nc.vector.tensor_tensor(gt[:], pj, pe_, ALU.is_gt).then_inc(vd, 1)
                nc.vector.tensor_tensor(eq[:], pj, pe_, ALU.is_equal).then_inc(vd, 1)
                dve.wait_ge(vd, V(g, "eq"))
                nc.vector.tensor_tensor(eq[:], eq[:], lower[:].rearrange("p (o a) b -> p o a b", o=1)
                                        .broadcast_to([P, J, NEXP, NEXP]), ALU.mult).then_inc(vd, 1)
                dve.wait_ge(vd, V(g, "eqm"))
                nc.vector.tensor_tensor(gt[:], gt[:], eq[:], ALU.add).then_inc(vd, 1)
                dve.wait_ge(vd, V(g, "cnt"))
                nc.vector.tensor_reduce(rank[:], gt[:], AX.X, ALU.add).then_inc(vd, 1)
                dve.wait_ge(vd, V(g, "rank"))
                nc.vector.scalar_tensor_tensor(w[:], rank[:], 1.5, p[:], ALU.is_lt, ALU.mult).then_inc(vd, 1)

            def gate_hidden(g, i):
                dve.wait_ge(ad, A(g, f"sg_{i}"))
                nc.vector.tensor_tensor(sT[:, i, :], ring[:, 2 * (i % 2) + 1, :], sg[:, i % 2, :],
                                        ALU.mult).then_inc(vd, 1)

            def experts(g, j):
                xt = x_res[:, bass.ds(g * J, J), :]
                dve.wait_ge(md, M(g, f"sh_{j}"))
                nc.vector.tensor_tensor(xt[:, j, :], xt[:, j, :], (shp, lgp)[j % 2][:, 0:E],
                                        ALU.add).then_inc(vd, 1)
                for e in range(NEXP):
                    if e % 2 == 0:
                        dve.wait_ge(md, M(g, f"ex_{j}_{e // 2}"))
                    dve.wait_ge(vd, V(g, f"acc_{j}_{e}"))
                    nc.vector.scalar_tensor_tensor(xt[:, j, :], ring[:, e // 2, (e % 2) * E:(e % 2) * E + E],
                                                   w[:, j, e:e + 1], xt[:, j, :], ALU.mult, ALU.add).then_inc(vd, 1)

            dve.sem_inc(vd, V.primed)
            for part in range(3):
                divide(0, part)
            residual(0)
            normalise(0)
            with dve.Fori(0, G - 1) as g:
                route(g)
                for i in range(4):
                    gate_hidden(g, i)
                    if i < 3:
                        divide(g + 1, i)
                experts(g, 0)
                residual(g + 1)
                experts(g, 1)
                normalise(g + 1)
                experts(g, 2)
                experts(g, 3)
            route(G - 1)
            for i in range(4):
                gate_hidden(G - 1, i)
            for j in range(J):
                experts(G - 1, j)

        @block.tensor
        def _(pe):
            pe.wait_ge(scaled, 1)
            def project(g, first=False):
                if not first:
                    pe.wait_ge(fad, FA(g - 1, "hT"))
                pe.wait_ge(fvd, FV(g, "att"))
                for j in range(J):
                    dst = tp[:, j // 2, (j % 2) * E:(j % 2) * E + E]
                    nc.tensor.matmul(dst, k["ones"][0:1, :], bo[:], start=True, stop=False)
                    for h in range(EH):
                        last = nc.tensor.matmul(dst, OTg[:, h, j * P:(j + 1) * P], wo[:, h, :],
                                                start=False, stop=(h == 1))
                last.then_inc(fmd, 1)

            def turn_over(g):
                pe.wait_ge(fvd, FV(g, "xn"))
                for h in range(EH):
                    for j in range(J):
                        last = nc.tensor.transpose(tp[:, h, j * P:(j + 1) * P], xn[:, j, h * P:(h + 1) * P],
                                                   k["ident"][:])
                last.then_inc(fmd, 1)

            def network(g):
                pe.wait_ge(fad, FA(g, "hT"))
                pe.wait_ge(vd, V(g - 1, f"acc_{J - 1}_0"))
                for j in range(J):
                    dst = lgp[:, j * NEXP:(j + 1) * NEXP]
                    nc.tensor.matmul(dst, k["ones"][0:1, :], bg[:], start=True, stop=False)
                    for h in range(EH):
                        last = nc.tensor.matmul(dst, hT[:, h, j * P:(j + 1) * P], wg[:, h, :],
                                                start=False, stop=(h == 1))
                last.then_inc(md, 1)
                for i in range(4):
                    if i < 2:
                        pe.wait_ge(vd, V(g - 1, f"acc_{J - 1}_{NEXP}"))
                    else:
                        pe.wait_ge(vd, V(g, f"s_{i - 2}"))
                    for ab in range(2):
                        for h in range(EH):
                            o = ab * E + (i % 2) * P
                            last = nc.tensor.matmul(ring[:, 2 * (i % 2) + ab, :], w_in[:, h, i // 2, o:o + P],
                                                    hT[:, h, :], start=(h == 0), stop=(h == 1))
                    last.then_inc(md, 1)

            def experts(g, j):
                if j == 0:
                    pe.wait_ge(vd, V(g, "s_3"))
                if j == 1:
                    pe.wait_ge(vd, V(g, "lsub"))
                if j >= 2:
                    pe.wait_ge(vd, V(g, f"acc_{j - 2}_0"))
                for h in range(EH):
                    last = nc.tensor.matmul((shp, lgp)[j % 2][:, 0:E], sT[:, h, j * P:(j + 1) * P],
                                            w_so[:, h, :], start=(h == 0), stop=(h == 1))
                last.then_inc(md, 1)
                for e in range(NEXP // 2):
                    if j:
                        pe.wait_ge(vd, V(g, f"acc_{j - 1}_{2 * e + 2}"))
                    for h in range(EH):
                        last = nc.tensor.matmul(ring[:, e, :], sT[:, 2 + h, j * P:(j + 1) * P],
                                                w2[:, h, 2 * e:2 * e + 2, :].rearrange("p a b -> p (a b)"),
                                                start=(h == 0), stop=(h == 1))
                    last.then_inc(md, 1)

            pe.sem_inc(md, M.primed)
            project(0, True)
            turn_over(0)
            with pe.Fori(0, G - 1) as g:
                network(g)
                experts(g, 0)
                project(g + 1)
                experts(g, 1)
                turn_over(g + 1)
                experts(g, 2)
                experts(g, 3)
            network(G - 1)
            for j in range(J):
                experts(G - 1, j)


HB, DK = 4, 64
C = 32
CT = P // C
TAPS = 4


def layer1_front(nc, k, d, sem, x_res, gam, kn_dram, vk_dram, a_dram, qk_dram):
    AV = Steps("stats", "aggr", "rstd", "xn", *[f"fr_{h}_{t}" for t in range(5) for h in range(2)],
               *[f"cv_{m}_{t}" for a in (0, 2, 4) for t in range(TAPS) for m in (a, a + 1)], "frr", "frg", "frx")
    BV = Steps(*[f"vb_{j}" for j in range(J)], "t1", "t2", "t3", "t4", "ra", "rb", "sc", "ro", "ss", "rr", "nrm",
               *[f"A_{j}" for j in range(J)])
    AA = Steps("std", "halo", "hT", *[f"pre_{m}" for m in range(6)], "sig", *[f"silu_{m}" for m in range(6)], "fstd")
    BA = Steps(*[f"X_{j}" for j in range(J)], "sq", "sstd", *[f"qkT_{j}" for j in range(J)])
    AM = Steps("tp", *[f"pr_{m}" for m in range(6)], "lg", "ftp")
    BM = Steps(*[f"nat_{j}" for j in range(J)], *[n for j in range(J) for n in (f"qkT_{j}", f"G_{j}")])
    AO = Steps("fx")
    BO = Steps("bt", "cm", "sm", "t1", "t2", "t3", "t4", "ra", "rb", "sc", "ro", "m2", "kb")
    with ExitStack() as st:
        def sb(n, s, t=F32):
            return st.enter_context(nc.sbuf_tensor(f"front_{n}", s, t))
        def ps(n, s, t=F32):
            return st.enter_context(nc.psum_tensor(f"front_{n}", s, t))
        wq = sb("wqkv", [P, EH, 3, E]); wl9 = sb("wl9", [P, EH, 9]); b9 = sb("b9", [1, 9])
        cw = sb("cw", [P, 6, TAPS]); fw = sb("fw", [P, EH, 4, 2]); f1 = sb("f1", [P, EH]); mw = sb("mw", [P, E])
        mix = sb("mix", [P, HB]); omx = sb("omx", [P, HB]); trim = sb("trim", [P, C])
        st6 = sb("st6", [P, J, 6]); mv = sb("mv", [P, J, 2]); sd = sb("sd", [P, J]); rs = sb("rs", [P, J])
        eps = sb("eps", [P, 2])
        xn = sb("xn", [P, J, E]); hT = sb("hT", [P, EH, 8 + 512])
        fr = sb("fr", [P, 2, EH, 512])
        pre = sb("pre", [P, 6, 3 + 512]); acc = sb("acc", [P, 2, 6, 512])
        lg = sb("lg", [P, J, 9]); bt4 = sb("bt4", [P, J, HB])
        X = sb("X", [P, J, 2, HB, DK]); XR = sb("XR", [P, J, 2, HB, DK]); SQ = sb("SQ", [P, J, 2, HB, DK])
        cs = sb("cs", [P, 2, J, 32]); csm = sb("csm", [P, 2, J, HB, 32])
        tq = [sb(f"tq{i}", [P, J, HB, 32]) for i in range(4)]
        tk = [sb(f"tk{i}", [P, J, HB, 32]) for i in range(4)]
        ss = sb("ss", [P, J, 2, HB]); ssd = sb("ssd", [P, J, 2, HB]); rr = sb("rr", [P, J, 2, HB, 1])
        vk = sb("vk", [P, J, HB, 2 * DK]); m2 = sb("m2", [P, J, HB, C]); AB = sb("AB", [P, J, HB, C])
        fss = sb("fss", [P, J]); fsd = sb("fsd", [P, J]); frr = sb("frr", [P, J]); frg = sb("frg", [P, J])
        qkG = sb("qkG", [P, J, 4 * P])
        fx = sb("fx", [P, J, E]); junk = sb("junk", [P, E])
        tp = ps("tp", [P, EH, 512]); pr = ps("pr", [P, 2, 512]); nat = ps("nat", [P, 2, 512]); gp = ps("gp", [P, 2, 512])
        wl, csl, xout = sem("w4_loaded"), sem("cs_loaded"), [sem("kn_out"), sem("vk_out"), sem("a_out"), sem("qkT_out")]
        avd, aad, amd, aod = (sem(f"front_a_{e}") for e in ("dve", "act", "pe", "pool"))
        bvd, bad, bmd, bod = (sem(f"front_b_{e}") for e in ("dve", "act", "pe", "pool"))
        held, sheld, pheld, sw = sem("p4_held"), sem("p4_sp_held"), sem("p4_pool_held"), sem("trim_loaded")
        sw2, fsq, cleared, mixed, coef = sem("w4_sum"), sem("frac_squares"), sem("cleared"), sem("mixed"), sem("coefs")
        block = st.enter_context(nc.Block())
        NWL = 16 * 20
        cos_v = d["c_cos"].rearrange("(t p) f -> p t f", p=P)
        sin_v = d["c_sin"].rearrange("(t p) f -> p t f", p=P)

        @block.sync
        def _(sp):
            def w(dst, src):
                sp.dma_start(dst, src, allow_slow_non_contiguous=True).then_inc(wl, 16)
            for i, n in enumerate(("Wq", "Wk", "Wv")):
                w(wq[:, :, i, :], d[f"L1_attn_{n}"].rearrange("(h p) n -> p h n", p=P))
            w(wl9[:, :, 0:4], d["L1_attn_Wb"].rearrange("(h p) n -> p h n", p=P))
            w(wl9[:, :, 4:8], d["L1_attn_Wgamma"].rearrange("(h p) n -> p h n", p=P))
            w(wl9[:, :, 8:9], d["L1_attn_frac_gate_w"].rearrange("(h p) n -> p h n", p=P))
            w(b9[:, 8:9], d["L1_attn_frac_gate_b"].rearrange("(o n) -> o n", o=1))
            for i, n in enumerate(("conv_q", "conv_k", "conv_v")):
                w(cw[:, 2 * i:2 * i + 2, :], d[f"L1_attn_{n}"].rearrange("(h p) n -> p h n", p=P))
            for i in range(4):
                for h in range(EH):
                    w(fw[:, h, i, :], d["L1_attn_frac_conv_w"][i, h * P:(h + 1) * P, :])
            w(mw[:], bcast(d["L1_attn_mixer_norm_w"], P))
            w(mix[:], bcast(d["L1_attn_rot_logit"], P))
            for s in xout:
                sp.sem_inc(s, 16)
            def load(g):
                tiles = bass.ds(g * J, J)
                sp.dma_start(cs[:, 0, :, :], cos_v[:, tiles, :]).then_inc(csl, 16)
                sp.dma_start(cs[:, 1, :, :], sin_v[:, tiles, :]).then_inc(csl, 16)

            def store(g):
                tiles = bass.ds(g * J, J)
                sp.wait_ge(bvd, BV(g, "nrm"))
                sp.dma_start(kn_dram[:, tiles, :], XR[:, :, 1, :, :].rearrange("p j h c -> p j (h c)"))\
                    .then_inc(xout[0], 16)
                sp.wait_ge(bod, BO(g, "kb"))
                sp.sem_inc(sheld, 1)
                sp.wait_ge(bvd, BV(g, f"vb_{J - 1}"))
                sp.dma_start(vk_dram[:, tiles, :], vk[:].rearrange("p j h c -> p j (h c)")).then_inc(xout[1], 16)
                sp.wait_ge(bvd, BV(g, f"A_{J - 1}"))
                sp.dma_start(a_dram[:, tiles, :], AB[:].rearrange("p j h c -> p j (h c)")).then_inc(xout[2], 16)
                sp.wait_ge(bad, BA(g, f"qkT_{J - 1}"))
                sp.dma_start(qk_dram[:, tiles, :], qkG[:]).then_inc(xout[3], 16)

            load(0)
            with sp.Fori(0, G - 1) as g:
                sp.wait_ge(bod, BO(g, "sm"))
                sp.sem_inc(sheld, 1)
                load(g + 1)
                store(g)
            store(G - 1)
            for s in xout:
                sp.wait_ge(s, 16 * G + 16)

        @block.gpsimd
        def _(pool):
            nc.gpsimd.memset(eps[:, 0:1], LN_EPS)
            nc.gpsimd.memset(eps[:, 1:2], 1e-6)
            nc.gpsimd.memset(hT[:], 0.0)
            nc.gpsimd.memset(b9[:, 0:8], 0.0)
            nc.gpsimd.memset(pre[:], 0.0).then_inc(cleared, 1)
            pool.dma_start(trim[:], d["c_trim"]).then_inc(sw, 16)
            pool.wait_ge(sw, 16)
            pool.wait_ge(coef, 1)
            def heads(g):
                pool.wait_ge(aad, AA(g, "sig"))
                pool.wait_ge(bvd, BV(g - 1, "vb_3"))
                pool.wait_ge(bod, BO(g - 1, "kb"))
                pool.sem_inc(pheld, 1)
                nc.gpsimd.tensor_copy(bt4[:], lg[:, :, 0:4]).then_inc(bod, 1)
                mb = mix[:].rearrange("p (o h c) -> p o h c", o=1, c=1).broadcast_to([P, J, HB, 32])
                ob = omx[:].rearrange("p (o h c) -> p o h c", o=1, c=1).broadcast_to([P, J, HB, DK])
                pool.wait_ge(csl, 32 * g + 32)
                pool.wait_ge(bvd, BV(g - 1, "t4"))
                pool.wait_ge(bod, BO(g - 1, "t4"))
                for i in range(2):
                    nc.gpsimd.tensor_tensor(csm[:, i, :, :, :], cs[:, i, :, :].rearrange("p j (o c) -> p j o c", o=1)
                                            .broadcast_to([P, J, HB, 32]), mb, ALU.mult).then_inc(bod, 1)
                pool.wait_ge(bad, BA(g, "X_3"))
                pool.wait_ge(bod, BO(g, "sm"))
                c_, s_ = csm[:, 0, :, :, :], csm[:, 1, :, :, :]
                x1, x2 = X[:, :, 1, :, 0:DK:2], X[:, :, 1, :, 1:DK:2]
                for o_, a_, b_ in ((0, x1, c_), (1, x2, s_), (2, x1, s_), (3, x2, c_)):
                    nc.gpsimd.tensor_tensor(tk[o_][:], a_, b_, ALU.mult).then_inc(bod, 1)
                pool.wait_ge(bod, BO(g, "t4"))
                nc.gpsimd.tensor_tensor(tk[0][:], tk[0][:], tk[1][:], ALU.subtract).then_inc(bod, 1)
                nc.gpsimd.tensor_tensor(tk[2][:], tk[2][:], tk[3][:], ALU.add).then_inc(bod, 1)
                nc.gpsimd.tensor_tensor(X[:, :, 1, :, :], X[:, :, 1, :, :], ob, ALU.mult).then_inc(bod, 1)
                pool.wait_ge(bod, BO(g, "sc"))
                pool.wait_ge(bmd, BM(g - 1, "qkT_3"))
                pool.wait_ge(xout[0], 16 * g + 16)
                nc.gpsimd.tensor_tensor(XR[:, :, 1, :, 0:32], X[:, :, 1, :, 0:32], tk[0][:], ALU.add)
                nc.gpsimd.tensor_tensor(XR[:, :, 1, :, 32:64], X[:, :, 1, :, 32:64], tk[2][:], ALU.add).then_inc(bod, 1)
                bt = bt4[:].rearrange("p j (h o) -> p j h o", o=1)
                nc.gpsimd.tensor_tensor(m2[:], trim[:].rearrange("p (a b c) -> p a b c", a=1, b=1)
                                        .broadcast_to([P, J, HB, C]), bt.broadcast_to([P, J, HB, C]),
                                        ALU.mult).then_inc(bod, 1)
                pool.wait_ge(bvd, BV(g, "nrm"))
                nc.gpsimd.tensor_tensor(vk[:, :, :, DK:], XR[:, :, 1, :, :], bt.broadcast_to([P, J, HB, DK]),
                                        ALU.mult).then_inc(bod, 1)

            def mixer(g):
                pool.wait_ge(avd, AV(g, "frx"))
                pool.sem_inc(pheld, 1)
                xt = x_res[:, bass.ds(g * J, J), :]
                nc.gpsimd.tensor_tensor(xt, xt, fx[:], ALU.add).then_inc(aod, 1)

            pool.sem_inc(bod, BO.primed)
            pool.sem_inc(aod, AO.primed)
            mixer(0)
            with pool.Fori(1, G) as g:
                heads(g - 1)
                mixer(g)
            heads(G - 1)

        @block.scalar
        def _(act):
            act.wait_ge(wl, NWL)
            nc.scalar.activation(mix[:], mix[:], ACT.Sigmoid).then_inc(mixed, 1)
            act.wait_ge(coef, 1)
            act.wait_ge(cleared, 1)
            def spread_and_halo(g):
                act.wait_ge(avd, AV(g, "aggr"))
                nc.scalar.activation(sd[:], mv[:, :, 1], ACT.Sqrt, bias=eps[:, 0:1]).then_inc(aad, 1)
                act.wait_ge(avd, AV(g - 1, "cv_5_3"))
                act.wait_ge(amd, AM(g - 1, "lg"))
                nc.scalar.activation(hT[:, :, 0:8], hT[:, :, 512:520], ACT.Copy)
                nc.scalar.activation(pre[:, :, 0:3], pre[:, :, 512:515], ACT.Copy).then_inc(aad, 1)

            def modulate(g):
                act.wait_ge(aad, AA(g, "halo"))
                act.wait_ge(amd, AM(g, "tp"))
                for h in range(EH):
                    last = nc.scalar.activation(hT[:, h, 8:], tp[:, h, :], ACT.Identity,
                                                bias=k["mod1"][:, h:h + 1], scale=k["mod1"][:, 2 + h:3 + h])
                last.then_inc(aad, 1)

            def take_projections(g):
                for m in range(6):
                    act.wait_ge(amd, AM(g, f"pr_{m}"))
                    nc.scalar.activation(pre[:, m, 3:], pr[:, m % 2, :], ACT.Copy).then_inc(aad, 1)

            def silu(g, m):
                act.wait_ge(avd, AV(g, f"cv_{m}_3"))
                nc.scalar.activation(acc[:, 0, m, :], acc[:, 1, m, :], ACT.Silu).then_inc(aad, 1)

            def rates(g):
                act.wait_ge(amd, AM(g, "lg"))
                act.wait_ge(bod, BO(g - 1, "bt"))
                nc.scalar.activation(lg[:], pr[:, 0, 0:J * 9].rearrange("p (j e) -> p j e", e=9), ACT.Sigmoid)
                nc.scalar.activation(gam[:, bass.ds(g * J, J), :],
                                     pr[:, 0, 0:J * 9].rearrange("p (j e) -> p j e", e=9)[:, :, 4:8],
                                     ACT.Sigmoid).then_inc(aad, 1)

            def mixer_squares(g):
                act.wait_ge(amd, AM(g, "ftp"))
                for j in range(J):
                    if j:
                        act.wait_ge(fsq, J * g + j + J)
                    nc.scalar.activation(junk[:], tp[:, j // 2, (j % 2) * E:(j % 2) * E + E], ACT.Square,
                                         accum_out=fss[:, j:j + 1]).then_inc(fsq, 1)

            def mixer_spread(g):
                act.wait_ge(fsq, J * g + 2 * J)
                nc.scalar.activation(fsd[:], fss[:], ACT.Sqrt, bias=eps[:, 0:1], scale=1.0 / E).then_inc(aad, 1)

            def take_heads(g, j):
                act.wait_ge(bmd, BM(g, f"nat_{j}"))
                nc.scalar.activation(X[:, j, :, :, :].rearrange("p a h c -> p (a h c)"), nat[:, 0, :],
                                     ACT.Copy).then_inc(bad, 1)

            def head_squares(g):
                act.wait_ge(bvd, BV(g, "ro"))
                act.wait_ge(bod, BO(g, "ro"))
                nc.scalar.activation(SQ[:], XR[:], ACT.Square).then_inc(bad, 1)

            def head_spread(g):
                act.wait_ge(bvd, BV(g, "ss"))
                nc.scalar.activation(ssd[:], ss[:], ACT.Sqrt, bias=eps[:, 1:2]).then_inc(bad, 1)

            def take_turned(g, j):
                act.wait_ge(bmd, BM(g, f"qkT_{j}"))
                act.wait_ge(xout[3], 16 * g + 16)
                nc.scalar.activation(qkG[:, j, :], pr[:, 0, :], ACT.Copy).then_inc(bad, 1)


            def turn(g, front, back):
                if front:
                    spread_and_halo(g)
                if back:
                    for j in range(J - 1):
                        take_heads(g - 1, j)
                if front:
                    modulate(g)
                if back:
                    take_heads(g - 1, J - 1)
                if front:
                    take_projections(g)
                if back:
                    head_squares(g - 1)
                    head_spread(g - 1)
                if front:
                    rates(g)
                for j in range(J):
                    if back:
                        take_turned(g - 1, j)
                    if front:
                        for m in ((0, 1), (2, 3), (4, 5), ())[j]:
                            silu(g, m)
                if front:
                    mixer_squares(g)
                    mixer_spread(g)

            act.sem_inc(aad, AA.primed)
            act.sem_inc(bad, BA.primed)
            act.sem_inc(fsq, J)
            turn(0, True, False)
            with act.Fori(1, G) as g:
                turn(g, True, True)
            turn(G, False, True)

        @block.vector
        def _(dve):
            dve.wait_ge(mixed, 1)
            dve.wait_ge(wl, NWL)
            nc.vector.tensor_scalar(omx[:], mix[:], -1.0, 1.0, ALU.mult, ALU.add)
            nc.vector.tensor_tensor(mw[:], mw[:], k["ga1"][:], ALU.mult)
            nc.vector.tensor_reduce(f1[:], fw[:, :, :, 1], AX.X, ALU.add).then_inc(sw2, 1)
            dve.wait_ge(sw2, 1)
            nc.vector.tensor_scalar(f1[:], f1[:], 2.0, None, ALU.add).then_inc(coef, 1)
            dve.wait_ge(coef, 1)
            def statistics(g):
                xt = x_res[:, bass.ds(g * J, J), :]
                for j in range(J):
                    last = nc.vector.bn_stats(st6[:, j, :], xt[:, j, :])
                last.then_inc(avd, 1)
                dve.wait_ge(avd, AV(g, "stats"))
                dve.sem_inc(held, 1)
                for j in range(J):
                    last = nc.vector.bn_aggr(mv[:, j, :], st6[:, j, :])
                last.then_inc(avd, 1)

            def normalise(g):
                xt = x_res[:, bass.ds(g * J, J), :]
                dve.wait_ge(aad, AA(g, "std"))
                nc.vector.reciprocal(rs[:], sd[:]).then_inc(avd, 1)
                dve.wait_ge(avd, AV(g, "rstd"))
                for j in range(J):
                    last = nc.vector.tensor_scalar(xn[:, j, :], xt[:, j, :], mv[:, j, 0:1], rs[:, j:j + 1],
                                                   ALU.subtract, ALU.mult)
                last.then_inc(avd, 1)

            def mixer_taps(g):
                dve.wait_ge(aad, AA(g, "hT"))
                for h in range(EH):
                    nc.vector.tensor_scalar(fr[:, 0, h, :], hT[:, h, 8:], f1[:, h:h + 1], None,
                                            ALU.mult).then_inc(avd, 1)
                for t in range(1, 5):
                    sh = 8 - 2 ** (t - 1)
                    for h in range(EH):
                        dve.wait_ge(avd, AV(g, f"fr_{h}_{t - 1}"))
                        nc.vector.scalar_tensor_tensor(fr[:, t % 2, h, :], hT[:, h, sh:sh + 512], fw[:, h, t - 1, 0:1],
                                                       fr[:, (t - 1) % 2, h, :], ALU.mult, ALU.add).then_inc(avd, 1)

            def convolve(g, a):
                for t in range(TAPS):
                    for m in (a, a + 1):
                        if t == 0:
                            dve.wait_ge(aad, AA(g, f"pre_{m}"))
                            dve.wait_ge(bmd, BM(g - 1, "nat_3"))
                            nc.vector.tensor_scalar(acc[:, 0, m, :], pre[:, m, 0:512], cw[:, m, 0:1], None,
                                                    ALU.mult).then_inc(avd, 1)
                        else:
                            dve.wait_ge(avd, AV(g, f"cv_{m}_{t - 1}"))
                            nc.vector.scalar_tensor_tensor(acc[:, t % 2, m, :], pre[:, m, t:t + 512],
                                                           cw[:, m, t:t + 1], acc[:, (t - 1) % 2, m, :],
                                                           ALU.mult, ALU.add).then_inc(avd, 1)

            def mixer_out(g):
                dve.wait_ge(aad, AA(g, "fstd"))
                nc.vector.reciprocal(frr[:], fsd[:]).then_inc(avd, 1)
                dve.wait_ge(avd, AV(g, "frr"))
                nc.vector.tensor_tensor(frg[:], frr[:], lg[:, :, 8], ALU.mult).then_inc(avd, 1)
                dve.wait_ge(avd, AV(g, "frg"))
                dve.wait_ge(aod, AO(g - 1, "fx"))
                for j in range(J):
                    last = nc.vector.scalar_tensor_tensor(fx[:, j, :], tp[:, j // 2, (j % 2) * E:(j % 2) * E + E],
                                                          frg[:, j:j + 1], mw[:], ALU.mult, ALU.mult)
                last.then_inc(avd, 1)

            def take_values(g, j):
                if j == 0:
                    dve.wait_ge(bod, BO(g, "bt"))
                    dve.wait_ge(xout[1], 16 * g + 16)
                dve.wait_ge(bmd, BM(g, f"nat_{j}"))
                nc.vector.tensor_tensor(vk[:, j, :, 0:DK], nat[:, 1, 0:E].rearrange("p (h c) -> p h c", h=HB),
                                        bt4[:, j, :].rearrange("p (h o) -> p h o", o=1)
                                        .broadcast_to([P, HB, DK]), ALU.mult).then_inc(bvd, 1)

            def rotate(g):
                ob = omx[:].rearrange("p (o h c) -> p o h c", o=1, c=1).broadcast_to([P, J, HB, DK])
                dve.wait_ge(bad, BA(g, "X_3"))
                dve.wait_ge(bod, BO(g, "sm"))
                c_, s_ = csm[:, 0, :, :, :], csm[:, 1, :, :, :]
                x1, x2 = X[:, :, 0, :, 0:DK:2], X[:, :, 0, :, 1:DK:2]
                for o_, a_, b_ in ((0, x1, c_), (1, x2, s_), (2, x1, s_), (3, x2, c_)):
                    nc.vector.tensor_tensor(tq[o_][:], a_, b_, ALU.mult).then_inc(bvd, 1)
                dve.wait_ge(bvd, BV(g, "t4"))
                nc.vector.tensor_tensor(tq[0][:], tq[0][:], tq[1][:], ALU.subtract).then_inc(bvd, 1)
                nc.vector.tensor_tensor(tq[2][:], tq[2][:], tq[3][:], ALU.add).then_inc(bvd, 1)
                nc.vector.tensor_tensor(X[:, :, 0, :, :], X[:, :, 0, :, :], ob, ALU.mult).then_inc(bvd, 1)
                dve.wait_ge(bvd, BV(g, "sc"))
                dve.wait_ge(bmd, BM(g - 1, "qkT_3"))
                nc.vector.tensor_tensor(XR[:, :, 0, :, 0:32], X[:, :, 0, :, 0:32], tq[0][:], ALU.add)
                nc.vector.tensor_tensor(XR[:, :, 0, :, 32:64], X[:, :, 0, :, 32:64], tq[2][:], ALU.add).then_inc(bvd, 1)

            def norms(g):
                dve.wait_ge(bad, BA(g, "sq"))
                nc.vector.tensor_reduce(ss[:], SQ[:], AX.X, ALU.add).then_inc(bvd, 1)
                dve.wait_ge(bad, BA(g, "sstd"))
                nc.vector.reciprocal(rr[:].rearrange("p j a h o -> p (j a h o)"),
                                     ssd[:].rearrange("p j a h -> p (j a h)")).then_inc(bvd, 1)
                dve.wait_ge(bvd, BV(g, "rr"))
                xf = XR[:].rearrange("p j a h c -> p (j a h) c")
                nc.vector.tensor_tensor(xf, xf, rr[:].rearrange("p j a h o -> p (j a h) o")
                                        .broadcast_to([P, J * 2 * HB, DK]), ALU.mult).then_inc(bvd, 1)

            def mask_products(g, j):
                if j == 0:
                    dve.wait_ge(bod, BO(g, "m2"))
                    dve.wait_ge(xout[2], 16 * g + 16)
                dve.wait_ge(bmd, BM(g, f"G_{j}"))
                for c in range(CT):
                    r = slice(C * c, C * c + C)
                    last = nc.vector.tensor_tensor(AB[r, j, :, :].rearrange("p (a b) c -> p b a c", b=2),
                                                   gp[r, :, 0:2 * P].rearrange("p b (a c) -> p b a c", a=2)[:, :, :, r],
                                                   m2[r, j, :, :].rearrange("p (a b) c -> p b a c", b=2), ALU.mult)
                last.then_inc(bvd, 1)


            def turn(g, front, back):
                if front:
                    statistics(g)
                if back:
                    take_values(g - 1, 0)
                    take_values(g - 1, 1)
                if front:
                    normalise(g)
                if back:
                    take_values(g - 1, 2)
                    take_values(g - 1, 3)
                    rotate(g - 1)
                if front:
                    mixer_taps(g)
                if back:
                    norms(g - 1)
                for i in range(3):
                    if front:
                        convolve(g, 2 * i)
                    if back:
                        for j in ((0,), (1, 2), (3,))[i]:
                            mask_products(g - 1, j)
                if front:
                    mixer_out(g)

            dve.sem_inc(avd, AV.primed)
            dve.sem_inc(bvd, BV.primed)
            turn(0, True, False)
            with dve.Fori(1, G) as g:
                turn(g, True, True)
            turn(G, False, True)

        @block.tensor
        def _(pe):
            pe.wait_ge(wl, NWL)
            pe.wait_ge(cleared, 1)
            def turn_over(g):
                pe.wait_ge(avd, AV(g, "xn"))
                for h in range(EH):
                    for j in range(J):
                        last = nc.tensor.transpose(tp[:, h, j * P:(j + 1) * P], xn[:, j, h * P:(h + 1) * P],
                                                   k["ident"][:])
                last.then_inc(amd, 1)

            def project(g):
                pe.wait_ge(aad, AA(g, "hT"))
                for m in range(6):
                    if m >= 2:
                        pe.wait_ge(aad, AA(g, f"pre_{m - 2}"))
                    for h in range(EH):
                        last = nc.tensor.matmul(pr[:, m % 2, :], wq[:, h, m // 2, (m % 2) * P:(m % 2) * P + P],
                                                hT[:, h, 8:], start=(h == 0), stop=(h == 1))
                    last.then_inc(amd, 1)

            def rates(g):
                pe.wait_ge(aad, AA(g, "pre_4"))
                for j in range(J):
                    dst = pr[:, 0, j * 9:j * 9 + 9]
                    nc.tensor.matmul(dst, k["ones"][0:1, :], b9[:], start=True, stop=False)
                    for h in range(EH):
                        last = nc.tensor.matmul(dst, hT[:, h, 8 + j * P:8 + (j + 1) * P], wl9[:, h, :],
                                                start=False, stop=(h == 1))
                last.then_inc(amd, 1)

            def turn_mixer(g):
                pe.wait_ge(avd, AV(g, "fr_1_4"))
                for j in range(J):
                    for h in range(EH):
                        o = (j % 2) * E + h * P
                        last = nc.tensor.transpose(tp[:, j // 2, o:o + P], fr[:, 0, h, j * P:(j + 1) * P],
                                                   k["ident"][:])
                last.then_inc(amd, 1)

            def turn_heads(g, j):
                if j == 0:
                    pe.wait_ge(aad, AA(g, "silu_5"))
                if j:
                    pe.wait_ge(bad, BA(g, f"X_{j - 1}"))
                    pe.wait_ge(bvd, BV(g, f"vb_{j - 1}"))
                for m in range(6):
                    last = nc.tensor.transpose(nat[:, m // 4, (m % 4) * P:(m % 4) * P + P],
                                               acc[:, 0, m, j * P:(j + 1) * P], k["ident"][:])
                last.then_inc(bmd, 1)

            def turn_and_square(g, j, last_group):
                if j == 0:
                    pe.wait_ge(bvd, BV(g, "nrm"))
                if j:
                    pe.wait_ge(bad, BA(g, f"qkT_{j - 1}"))
                elif last_group:
                    pe.wait_ge(bad, BA(g - 1, "qkT_3"))
                else:
                    pe.wait_ge(aad, AA(g + 1, "sig"))
                for pair in range(2):
                    for i, a in ((0, 1), (1, 0)):
                        last = nc.tensor.transpose(pr[:, 0, (2 * pair + i) * P:(2 * pair + i + 1) * P],
                                                   XR[:, j, a, 2 * pair:2 * pair + 2, :]
                                                   .rearrange("p h c -> p (h c)"), k["ident"][:])
                last.then_inc(bmd, 1)
                pe.wait_ge(bad, BA(g, f"qkT_{j}"))
                if j:
                    pe.wait_ge(bvd, BV(g, f"A_{j - 1}"))
                for h in range(HB):
                    r = slice(DK * (h % 2), DK * (h % 2) + DK)
                    kT = qkG[r, j, (h // 2) * 2 * P:(h // 2) * 2 * P + P]
                    last = nc.tensor.matmul(gp[:, h % 2, (h // 2) * P:(h // 2) * P + P], kT, kT, start=True, stop=True)
                last.then_inc(bmd, 1)


            def turn(g, front, back):
                if back:
                    for j in range(J - 1):
                        turn_heads(g - 1, j)
                if front:
                    turn_over(g)
                if back:
                    turn_heads(g - 1, J - 1)
                if front:
                    project(g)
                    rates(g)
                    turn_mixer(g)
                if back:
                    for j in range(J):
                        turn_and_square(g - 1, j, not front)

            pe.sem_inc(amd, AM.primed)
            pe.sem_inc(bmd, BM.primed)
            turn(0, True, False)
            with pe.Fori(1, G) as g:
                turn(g, True, True)
            turn(G, False, True)


def solve_chunks(nc, k, d, sem, a_dram, tt_dram):
    with ExitStack() as st:
        AF = st.enter_context(nc.sbuf_tensor("AF", [P, J, C, C], F32))
        TT = st.enter_context(nc.sbuf_tensor("TT", [P, J, C, C], F32))
        tmp = [st.enter_context(nc.sbuf_tensor(f"tmp{i}", [P, J, C - 1, C - 1], F32)) for i in range(2)]
        al, unit, prod, row, out = sem("a_loaded"), sem("unit_set"), sem("products"), sem("rows_done"), sem("tt_out")
        block = st.enter_context(nc.Block())

        @block.sync
        def _(sp):
            for g in range(G):
                for c in range(CT):
                    r = 16 * g + 4 * c
                    for j in range(J):
                        sp.dma_start(AF[r:r + HB, j, :, :],
                                     a_dram[C * c:C * c + C, J * g + j, :].rearrange("i (h j) -> h i j", h=HB))\
                            .then_inc(al, 16)
            sp.wait_ge(row, C - 1)
            for g in range(G):
                sp.dma_start(tt_dram[J * g:J * g + J, :, :].rearrange("t q x -> q t x"),
                             TT[16 * g:16 * g + 16, :, :, :].rearrange("p t c i -> p t (c i)")).then_inc(out, 16)
            sp.wait_ge(out, 16 * G)

        @block.gpsimd
        def _(pool):
            nc.gpsimd.memset(TT[:], 0.0).then_inc(unit, 1)
            pool.wait_ge(unit, 1)
            nc.gpsimd.memset(TT[:].rearrange("p t c i -> p t (c i)")[:, :, 0:C * C:C + 1], 1.0).then_inc(unit, 1)

        @block.vector
        def _(dve):
            dve.wait_ge(unit, 2)
            dve.wait_ge(al, 16 * G * CT * J)
            for i in range(1, C):
                buf = tmp[i % 2][:, :, 0:i, 0:i]
                if i >= 2:
                    dve.wait_ge(row, i - 1)
                nc.vector.tensor_tensor(buf, AF[:, :, i:i + 1, 0:i].broadcast_to([P, J, i, i]), TT[:, :, 0:i, 0:i],
                                        ALU.mult).then_inc(prod, 1)
                dve.wait_ge(prod, i)
                nc.vector.tensor_reduce(TT[:, :, 0:i, i], buf, AX.X, ALU.add).then_inc(row, 1)


def delta_rule(nc, k, d, sem, gam, o_all, kn_dram, vk_dram, qk_dram, tt_dram):
    DF = Steps("atm", "QE", "MT", back=2)
    DT = Steps("S_0", "S_1", "S_2", "S_3", back=2)
    AF_ = Steps("UW", "B", back=2)
    AT = Steps("O", back=2)
    MF = Steps("at", "uw", "qe", "mt", "b", back=2)
    MT_ = Steps("ob", "rec_0", "rec_1", "rec_2", "rec_3", "o", back=2)
    LB = 11
    with ExitStack() as st:
        def sb(n, s, t=F32):
            return st.enter_context(nc.sbuf_tensor(f"delta_{n}", s, t))
        def ps(n, s, t=F32):
            return st.enter_context(nc.psum_tensor(f"delta_{n}", s, t))
        KN = [sb(f"KN{b}", [P, HB, DK]) for b in range(2)]
        KBD = [sb(f"KBD{b}", [P, HB, CT, DK]) for b in range(2)]
        VK = [sb(f"VK{b}", [P, HB, 2 * DK]) for b in range(2)]
        QK = [sb(f"QK{b}", [P, 2, 2, P]) for b in range(2)]
        TTb = [sb(f"TTb{b}", [P, HB, P]) for b in range(2)]
        UW = [sb(f"UW{b}", [P, HB, 2 * DK]) for b in range(2)]
        UBD = [sb(f"UBD{b}", [P, HB, CT, DK]) for b in range(2)]
        atm = [sb(f"atm{b}", [P, HB, P]) for b in range(2)]
        QE = [sb(f"QE{b}", [P, 2, P]) for b in range(2)]
        MTb = [sb(f"MTb{b}", [P, 2, CT, P]) for b in range(2)]
        BB = [sb(f"BB{b}", [P, 2, CT, P]) for b in range(2)]
        gI = [sb(f"gI{b}", [P, 2, CT, DK]) for b in range(2)]
        SB = sb("SB", [P, CT, 2, P])
        GM = sb("GM", [P, T, 2, CT, 2]); gall = sb("gall", [P, T * CT * 2])
        causal = sb("causal", [P, P]); id64 = sb("id64", [P, DK]); chunk = sb("chunk", [P, CT])
        atp = ps("atp", [P, 2, 512]); uwp = ps("uwp", [P, 512]); qep = ps("qep", [P, 512])
        mtp = ps("mtp", [P, 512]); bp = ps("bp", [P, 512]); op = ps("op", [P, 512]); rp = ps("rp", [P, 512])
        wl, gm_done, gm_mm, gm_cp = sem("w5_loaded"), sem("gm_done"), sem("gm_mm"), sem("gm_copied")
        cleared = sem("delta_cleared")
        loaded = [sem(f"tile_loaded{b}") for b in range(2)]
        df, dt_, af, at_, mf, mt_, gi = (sem(n) for n in ("dve_front", "dve_tail", "act_front", "act_tail",
                                                          "pe_front", "pe_tail", "gI_done"))
        held, sheld, aheld = sem("p5_pool_held"), sem("p5_sp_held"), sem("p5_act_held")
        block = st.enter_context(nc.Block())

        @block.sync
        def _(sp):
            sp.dma_start(causal[:], d["c_causal"]).then_inc(wl, 16)
            sp.dma_start(id64[:], d["c_id64"]).then_inc(wl, 16)
            sp.dma_start(chunk[:], d["c_chunk"]).then_inc(wl, 16)
            sp.wait_ge(cleared, 1)

            def load(t, b):
                one = bass.ds(t, 1)
                q = loaded[b]
                sp.dma_start(KN[b][:].rearrange("p h c -> p (h c)"), kn_dram[:, one, :]).then_inc(q, 16)
                sp.dma_start(VK[b][:].rearrange("p h c -> p (h c)"), vk_dram[:, one, :]).then_inc(q, 16)
                sp.dma_start(QK[b][:].rearrange("p a b c -> p (a b c)"), qk_dram[:, one, :]).then_inc(q, 16)
                for c in range(CT):
                    r = slice(C * c, C * c + C)
                    sp.dma_start(KBD[b][r, :, c, :], kn_dram[r, one, :].rearrange("p o (h c) -> p (o h) c", h=HB))\
                        .then_inc(q, 16)
                    sp.dma_start(TTb[b][r, :, r], tt_dram[one, HB * c:HB * c + HB, :]
                                 .rearrange("o h (x i) -> x (o h) i", i=C)).then_inc(q, 16)
            load(0, 0)
            load(1, 1)
            with sp.Fori(0, T // 2 - 1) as i:
                for b in range(2):
                    t = 2 * i + b
                    sp.wait_ge(mf, MF(t, "b"))
                    sp.wait_ge(df, DF(t, "QE"))
                    sp.sem_inc(sheld, 1)
                    load(t + 2, b)

        @block.gpsimd
        def _(pool):
            for b in range(2):
                for buf in (KBD, UBD, TTb, MTb, BB):
                    nc.gpsimd.memset(buf[b][:], 0.0)
            nc.gpsimd.memset(SB[:], 0.0).then_inc(cleared, 1)
            pool.wait_ge(gm_cp, 1)

            def gi_of(t, b):
                pool.wait_ge(df, DF(t - 2, "MT"))
                pool.sem_inc(held, 1)
                gv = gall[:, bass.ds(t * CT * 2, CT * 2)].rearrange("p (c a o) -> p a c o", c=CT, o=1)
                nc.gpsimd.tensor_tensor(gI[b][:], id64[:].rearrange("p (a b c) -> p a b c", a=1, b=1)
                                        .broadcast_to([P, 2, CT, DK]), gv.broadcast_to([P, 2, CT, DK]),
                                        ALU.mult).then_inc(gi, 1)
            with pool.Fori(0, T // 2) as i:
                for b in range(2):
                    gi_of(2 * i + b, b)

        @block.scalar
        def _(act):
            act.wait_ge(cleared, 1)
            act.sem_inc(af, AF_.primed)
            act.sem_inc(at_, AT.primed)

            def front_uw(t, b):
                act.wait_ge(mf, MF(t, "uw"))
                act.wait_ge(mt_, MT_(t - 2, "ob"))
                nc.scalar.activation(UW[b][:].rearrange("p h c -> p (h c)"), uwp[:], ACT.Copy)
                for c in range(CT):
                    r = slice(C * c, C * c + C)
                    last = nc.scalar.activation(UBD[b][r, :, c, :],
                                                uwp[r, :].rearrange("p (h c) -> p h c", h=HB)[:, :, 0:DK], ACT.Copy)
                last.then_inc(af, 1)

            def front_b(t, b):
                act.wait_ge(mf, MF(t, "b"))
                act.wait_ge(dt_, DT(t - 2, "S_3"))
                for q in range(2):
                    r = slice(DK * q, DK * q + DK)
                    last = nc.scalar.activation(BB[b][r, :, :, r],
                                                bp[r, :].rearrange("p (a c x) -> p a c x", a=2, c=CT), ACT.Copy)
                last.then_inc(af, 1)

            def tail(t, b):
                act.wait_ge(mt_, MT_(t, "o"))
                act.sem_inc(aheld, 1)
                nc.scalar.activation(o_all[:, bass.ds(t, 1), :].rearrange("p o c -> p (o c)"), op[:, 0:E],
                                     ACT.Copy).then_inc(at_, 1)

            def both(t, b):
                front_uw(t, b)
                tail(t - 1, 1 - b)
                front_b(t, b)
            front_uw(0, 0)
            front_b(0, 0)
            with act.Fori(0, T // 2 - 1) as i:
                for b in (1, 0):
                    both(2 * i + 2 - b, b)
            both(T - 1, 1)
            tail(T - 1, 1)

        @block.vector
        def _(dve):
            dve.wait_ge(wl, 48)
            for par in range(2):
                nc.vector.tensor_tensor(GM[:, :, par, :, :].rearrange("p t c a -> p t c a"),
                                        gam[:, :, par::2].rearrange("p t (o a) -> p t o a", o=1)
                                        .broadcast_to([P, T, CT, 2]),
                                        chunk[:].rearrange("p (o c q) -> p o c q", o=1, q=1)
                                        .broadcast_to([P, T, CT, 2]), ALU.mult).then_inc(gm_done, 1)
            dve.wait_ge(gm_mm, 1)
            nc.vector.tensor_copy(gall[:], rp[:, 0:T * CT * 2]).then_inc(gm_cp, 1)
            dve.wait_ge(cleared, 1)
            dve.sem_inc(df, DF.primed)
            dve.sem_inc(dt_, DT.primed)

            def f_at(t, b):
                dve.wait_ge(mf, MF(t, "at"))
                dve.wait_ge(mt_, MT_(t - 2, "ob"))
                nc.vector.tensor_tensor(atm[b][:].rearrange("p (a b) c -> p b a c", b=2),
                                        atp[:, :, 0:2 * P].rearrange("p b (a c) -> p b a c", a=2),
                                        causal[:].rearrange("p (a b c) -> p a b c", a=1, b=1)
                                        .broadcast_to([P, 2, 2, P]), ALU.mult).then_inc(df, 1)

            def f_qe(t, b):
                dve.wait_ge(mf, MF(t, "qe"))
                dve.wait_ge(mt_, MT_(t - 2, "o"))
                nc.vector.tensor_tensor(QE[b][:], QK[b][:, :, 1, :], qep[:, 0:2 * P]
                                        .rearrange("p (a c) -> p a c", a=2), ALU.subtract).then_inc(df, 1)

            def f_mt(t, b):
                dve.wait_ge(mf, MF(t, "mt"))
                dve.wait_ge(mt_, MT_(t - 2, "rec_3"))
                dve.wait_ge(gi, t + 1)
                for q in range(2):
                    r = slice(DK * q, DK * q + DK)
                    last = nc.vector.tensor_tensor(MTb[b][r, :, :, r], gI[b][r, :, :, :],
                                                   mtp[r, :].rearrange("p (a c x) -> p a c x", a=2, c=CT),
                                                   ALU.subtract)
                last.then_inc(df, 1)

            def t_s(t, b, c):
                dve.wait_ge(mt_, MT_(t, f"rec_{c}"))
                if c == 0:
                    dve.wait_ge(af, AF_(t, "B"))
                nc.vector.tensor_tensor(SB[:, (c + 1) % CT, :, :], BB[b][:, :, c, :],
                                        rp[:, 0:2 * P].rearrange("p (a c) -> p a c", a=2), ALU.add).then_inc(dt_, 1)

            def both(t, b):
                f_at(t, b)
                t_s(t - 1, 1 - b, 0)
                t_s(t - 1, 1 - b, 1)
                f_qe(t, b)
                t_s(t - 1, 1 - b, 2)
                f_mt(t, b)
                t_s(t - 1, 1 - b, 3)
            f_at(0, 0)
            f_qe(0, 0)
            f_mt(0, 0)
            with dve.Fori(0, T // 2 - 1) as i:
                for b in (1, 0):
                    both(2 * i + 2 - b, b)
            both(T - 1, 1)
            for c in range(CT):
                t_s(T - 1, 1, c)

        @block.tensor
        def _(pe):
            pe.wait_ge(gm_done, 2)
            for par in range(2):
                last = nc.tensor.matmul(rp[DK * par:DK * par + DK, 0:T * CT * 2], k["ones"][:, 0:DK],
                                        GM[:, :, par, :, :], start=True, stop=True)
            last.then_inc(gm_mm, 1)
            pe.wait_ge(gm_cp, 1)
            pe.wait_ge(cleared, 1)
            pe.sem_inc(mf, MF.primed)
            pe.sem_inc(mt_, MT_.primed)

            def f_at(t, b, turn):
                pe.wait_ge(loaded[b], 16 * LB * (turn + 1))
                pe.wait_ge(df, DF(t - 1, "atm"))
                for h in range(HB):
                    r = slice(DK * (h % 2), DK * (h % 2) + DK)
                    last = nc.tensor.matmul(atp[:, h % 2, (h // 2) * P:(h // 2) * P + P], QK[b][r, h // 2, 0, :],
                                            QK[b][r, h // 2, 1, :], start=True, stop=True)
                last.then_inc(mf, 1)

            def f_uw(t, b):
                pe.wait_ge(af, AF_(t - 1, "UW"))
                for h in range(HB):
                    last = nc.tensor.matmul(uwp[:, h * P:(h + 1) * P], TTb[b][:, h, :], VK[b][:, h, :],
                                            start=True, stop=True)
                last.then_inc(mf, 1)

            def f_qe(t, b):
                pe.wait_ge(af, AF_(t, "UW"))
                pe.wait_ge(df, DF(t, "atm"))
                for h in range(HB):
                    r = slice(DK * (h % 2), DK * (h % 2) + DK)
                    last = nc.tensor.matmul(qep[r, (h // 2) * P:(h // 2) * P + P], UW[b][:, h, DK:], atm[b][:, h, :],
                                            start=True, stop=True)
                last.then_inc(mf, 1)

            def f_mt(t, b):
                pe.wait_ge(df, DF(t - 1, "MT"))
                for h in range(HB):
                    r = slice(DK * (h % 2), DK * (h % 2) + DK)
                    o = (h // 2) * 2 * P
                    last = nc.tensor.matmul(mtp[r, o:o + 2 * P], UW[b][:, h, DK:], KBD[b][:, h, :, :],
                                            start=True, stop=True)
                last.then_inc(mf, 1)

            def f_b(t, b):
                pe.wait_ge(af, AF_(t - 1, "B"))
                for h in range(HB):
                    r = slice(DK * (h % 2), DK * (h % 2) + DK)
                    o = (h // 2) * 2 * P
                    last = nc.tensor.matmul(bp[r, o:o + 2 * P], KN[b][:, h, :], UBD[b][:, h, :, :],
                                            start=True, stop=True)
                last.then_inc(mf, 1)

            def t_ob(t, b):
                pe.wait_ge(at_, AT(t - 1, "O"))
                for h in range(HB):
                    last = nc.tensor.matmul(op[:, h * DK:(h + 1) * DK], atm[b][:, h, :], UW[b][:, h, 0:DK],
                                            start=(h == 0), stop=False, skip_group_check=True)
                last.then_inc(mt_, 1)

            def t_rec(t, b, c):
                pe.wait_ge(dt_, DT(t, f"S_{c - 1}") if c else DT(t - 1, "S_3"))
                if c == 0:
                    pe.wait_ge(df, DF(t, "MT"))
                for a in range(2):
                    last = nc.tensor.matmul(rp[:, a * P:(a + 1) * P], MTb[b][:, a, c, :], SB[:, c, a, :],
                                            start=True, stop=True)
                last.then_inc(mt_, 1)
                for a in range(2):
                    last = nc.tensor.matmul(op[C * c:C * c + C, a * P:(a + 1) * P], QE[b][:, a, C * c:C * c + C],
                                            SB[:, c, a, :], start=False, stop=True, skip_group_check=True)
                if c == CT - 1:
                    last.then_inc(mt_, 1)

            def both(t, b, turn):
                f_at(t, b, turn)
                t_ob(t - 1, 1 - b)
                t_rec(t - 1, 1 - b, 0)
                f_uw(t, b)
                t_rec(t - 1, 1 - b, 1)
                f_qe(t, b)
                t_rec(t - 1, 1 - b, 2)
                f_mt(t, b)
                t_rec(t - 1, 1 - b, 3)
                f_b(t, b)
            f_at(0, 0, 0)
            f_uw(0, 0)
            f_qe(0, 0)
            f_mt(0, 0)
            f_b(0, 0)
            with pe.Fori(0, T // 2 - 1) as i:
                both(2 * i + 1, 1, i)
                both(2 * i + 2, 0, i + 1)
            both(T - 1, 1, T // 2 - 1)
            t_ob(T - 1, 1)
            for c in range(CT):
                t_rec(T - 1, 1, c)


MAGIC = 1.5 * 2.0 ** 23


def layer1_back(nc, k, d, sem, x_res, o_all, out):
    V = Steps("ss", "rr", "on", "x3", "stats", "aggr", "rstd", "xn", "amax", "xs", "ri", "qr", "q", "qT", "y", "out")
    A = Steps("sq", "ostd", "oT", "std")
    M = Steps("otp", "wo", "qtp", "lin")
    O = Steps("hm", "ha", "x3b")
    with ExitStack() as st:
        def sb(n, s, t=F32):
            return st.enter_context(nc.sbuf_tensor(f"back_{n}", s, t))
        def ps(n, s, t=F32):
            return st.enter_context(nc.psum_tensor(f"back_{n}", s, t))
        wo = sb("wo1", [P, EH, E]); w8 = sb("w8", [P, EH, E // 4], mybir.dt.int32); wq = sb("wq8", [P, EH, E], BF16)
        w8b = sb("w8b", [P, EH, E], BF16)
        onw = sb("onw", [P, 1]); ws = sb("ws", [P, E]); bi = sb("bi", [P, E]); eps = sb("eps", [P, 1])
        SQ = sb("SQ", [P, J, E]); ss = sb("ss", [P, J * HB]); osd = sb("osd", [P, J * HB]); rr = sb("rr", [P, J * HB, 1])
        on = sb("on", [P, J, E]); oT = sb("oT", [P, EH, 512])
        st6 = sb("st6", [P, J, 6]); mv = sb("mv", [P, J, 2]); sd = sb("sd", [P, J]); rs = sb("rs", [P, J])
        xn = sb("xn", [P, J, E]); h4 = sb("h4", [P, J, E])
        am = sb("am", [P, J]); xs = sb("xs", [P, J]); ri = sb("ri", [P, J])
        q32 = sb("q32", [P, J, E]); qb = sb("qb", [P, J, E], BF16); qT = sb("qT", [P, EH, 512], BF16)
        x3b = sb("x3b", [P, J, E]); y = sb("y", [P, J, E])
        otp = ps("otp", [P, EH, 512]); wop = ps("wop", [P, 2, 512]); qtp = ps("qtp", [P, EH, 512], BF16)
        lin = ps("lin", [P, 2, 512])
        wl, wready, eps_set, out_sent = sem("w6_loaded"), sem("w6_ready"), sem("eps6_set"), sem("out_sent")
        vd, ad, md, od = sem("p6_dve"), sem("p6_act"), sem("p6_pe"), sem("p6_pool")
        held, held2, sheld, aheld = (sem(f"p6_{n}_held") for n in ("dve", "pool", "sp", "act"))
        wcast, wturned = sem("wq_cast"), sem("wq_turned")
        block = st.enter_context(nc.Block())
        out_v = out.rearrange("o (t p) c -> p (o t) c", p=P)

        @block.sync
        def _(sp):
            sp.dma_start(wo[:], d["L1_attn_Wo"].rearrange("(h p) n -> p h n", p=P)).then_inc(wl, 16)
            sp.dma_start(w8[:], d["L1_ffn_weight_q"].rearrange("(h p) n -> p h n", p=P)).then_inc(wl, 16)
            for h in range(2):
                sp.dma_start(onw[DK * h:DK * h + DK, :], d["L1_attn_o_norm_w"].rearrange("(c o) -> c o", o=1))\
                    .then_inc(wl, 16)
            sp.dma_start(ws[:], bcast(d["L1_ffn_weight_scale"], P)).then_inc(wl, 16)
            sp.dma_start(bi[:], bcast(d["L1_ffn_bias"], P)).then_inc(wl, 16)
            sp.sem_inc(out_sent, 16)
            with sp.Fori(0, G) as g:
                sp.wait_ge(vd, V(g, "out"))
                sp.sem_inc(sheld, 1)
                sp.dma_start(out_v[:, bass.ds(g * J, J), :], y[:]).then_inc(out_sent, 16)
            sp.wait_ge(out_sent, 16 * G + 16)

        @block.gpsimd
        def _(pool):
            nc.gpsimd.memset(eps[:], LN_EPS).then_inc(eps_set, 1)
            row = lambda a: a[:].rearrange("p (o c) -> p o c", o=1).broadcast_to([P, J, E])
            pool.wait_ge(wready, 2)
            pool.sem_inc(od, O.primed)
            with pool.Fori(0, G) as g:
                pool.wait_ge(vd, V(g, "xn"))
                nc.gpsimd.tensor_tensor(h4[:], xn[:], row(k["cb1"]), ALU.mult).then_inc(od, 1)
                pool.wait_ge(od, O(g, "hm"))
                nc.gpsimd.tensor_tensor(h4[:], h4[:], row(k["sb1"]), ALU.add).then_inc(od, 1)
                pool.wait_ge(vd, V(g - 1, "out"))
                pool.sem_inc(held2, 1)
                nc.gpsimd.tensor_tensor(x3b[:], x_res[:, bass.ds(g * J, J), :], row(bi), ALU.add).then_inc(od, 1)

        @block.scalar
        def _(act):
            act.wait_ge(wl, 16 * 6)
            act.wait_ge(eps_set, 1)
            act.sem_inc(ad, A.primed)
            with act.Fori(0, G) as g:
                act.wait_ge(vd, V(g - 1, "ss"))
                act.sem_inc(aheld, 1)
                nc.scalar.activation(SQ[:], o_all[:, bass.ds(g * J, J), :], ACT.Square).then_inc(ad, 1)
                act.wait_ge(vd, V(g, "ss"))
                nc.scalar.activation(osd[:], ss[:], ACT.Sqrt, bias=eps[:], scale=1.0 / DK).then_inc(ad, 1)
                act.wait_ge(md, M(g, "otp"))
                nc.scalar.activation(oT[:], otp[:], ACT.Copy, scale=onw[:]).then_inc(ad, 1)
                act.wait_ge(vd, V(g, "aggr"))
                nc.scalar.activation(sd[:], mv[:, :, 1], ACT.Sqrt, bias=eps[:]).then_inc(ad, 1)

        @block.vector
        def _(dve):
            dve.wait_ge(wl, 16 * 6)
            nc.vector.tensor_tensor(wo[:], wo[:], k["ga1"][:].rearrange("p (o c) -> p o c", o=1)
                                    .broadcast_to([P, EH, E]), ALU.mult)
            nc.vector.tensor_copy(w8b[:], w8[:].bitcast(mybir.dt.int8)).then_inc(wcast, 1)
            nc.vector.tensor_tensor(ws[:], ws[:], k["gb1"][:], ALU.mult)
            nc.vector.tensor_tensor(bi[:], bi[:], k["gb1"][:], ALU.mult).then_inc(wready, 1)
            dve.wait_ge(wturned, 1)
            nc.vector.tensor_copy(wq[:], qtp[:, :, 0:E]).then_inc(wready, 1)
            dve.wait_ge(wready, 2)
            dve.sem_inc(vd, V.primed)
            with dve.Fori(0, G) as g:
                xt = x_res[:, bass.ds(g * J, J), :]
                ot = o_all[:, bass.ds(g * J, J), :]
                dve.wait_ge(ad, A(g, "sq"))
                nc.vector.tensor_reduce(ss[:], SQ[:].rearrange("p j (h c) -> p (j h) c", c=DK), AX.X,
                                        ALU.add).then_inc(vd, 1)
                dve.wait_ge(ad, A(g, "ostd"))
                nc.vector.reciprocal(rr[:, :, 0], osd[:]).then_inc(vd, 1)
                dve.wait_ge(vd, V(g, "rr"))
                nc.vector.tensor_tensor(on[:].rearrange("p j (h c) -> p (j h) c", c=DK),
                                        ot.rearrange("p j (h c) -> p (j h) c", c=DK),
                                        rr[:].broadcast_to([P, J * HB, DK]), ALU.mult).then_inc(vd, 1)
                dve.wait_ge(md, M(g, "wo"))
                for a in range(2):
                    last = nc.vector.tensor_tensor(xt[:, 2 * a:2 * a + 2, :], xt[:, 2 * a:2 * a + 2, :],
                                                   wop[:, a, :].rearrange("p (j c) -> p j c", j=2), ALU.add)
                last.then_inc(vd, 1)
                dve.wait_ge(vd, V(g, "x3"))
                dve.sem_inc(held, 1)
                for j in range(J):
                    last = nc.vector.bn_stats(st6[:, j, :], xt[:, j, :])
                last.then_inc(vd, 1)
                dve.wait_ge(vd, V(g, "stats"))
                dve.sem_inc(held, 1)
                for j in range(J):
                    last = nc.vector.bn_aggr(mv[:, j, :], st6[:, j, :])
                last.then_inc(vd, 1)
                dve.wait_ge(ad, A(g, "std"))
                nc.vector.reciprocal(rs[:], sd[:]).then_inc(vd, 1)
                dve.wait_ge(vd, V(g, "rstd"))
                for j in range(J):
                    last = nc.vector.tensor_scalar(xn[:, j, :], xt[:, j, :], mv[:, j, 0:1], rs[:, j:j + 1],
                                                   ALU.subtract, ALU.mult)
                last.then_inc(vd, 1)
                dve.wait_ge(od, O(g, "ha"))
                nc.vector.tensor_reduce(am[:], h4[:], AX.X, ALU.max, apply_absolute_value=True).then_inc(vd, 1)
                dve.wait_ge(vd, V(g, "amax"))
                nc.vector.tensor_scalar(xs[:], am[:], 1e-6, 1.0 / 127.0, ALU.max, ALU.mult).then_inc(vd, 1)
                dve.wait_ge(vd, V(g, "xs"))
                nc.vector.reciprocal(ri[:], xs[:]).then_inc(vd, 1)
                dve.wait_ge(vd, V(g, "ri"))
                for j in range(J):
                    last = nc.vector.tensor_scalar(q32[:, j, :], h4[:, j, :], ri[:, j:j + 1], MAGIC,
                                                   ALU.mult, ALU.add)
                last.then_inc(vd, 1)
                dve.wait_ge(vd, V(g, "qr"))
                nc.vector.tensor_scalar(qb[:], q32[:], -MAGIC, 127.0, ALU.add, ALU.min).then_inc(vd, 1)
                dve.wait_ge(md, M(g, "qtp"))
                nc.vector.tensor_scalar(qT[:], qtp[:], -128.0, None, ALU.max).then_inc(vd, 1)
                dve.wait_ge(md, M(g, "lin"))
                dve.wait_ge(out_sent, 16 * g + 16)
                for j in range(J):
                    last = nc.vector.scalar_tensor_tensor(y[:, j, :], lin[:, j // 2, (j % 2) * E:(j % 2) * E + E],
                                                          xs[:, j:j + 1], ws[:], ALU.mult, ALU.mult)
                last.then_inc(vd, 1)
                dve.wait_ge(vd, V(g, "y"))
                dve.wait_ge(od, O(g, "x3b"))
                nc.vector.tensor_tensor(y[:], y[:], x3b[:], ALU.add).then_inc(vd, 1)

        @block.tensor
        def _(pe):
            pe.wait_ge(wcast, 1)
            for h in range(EH):
                for o in range(EH):
                    last = nc.tensor.transpose(qtp[:, h, o * P:(o + 1) * P], w8b[:, o, h * P:(h + 1) * P],
                                               k["identb"][:])
            last.then_inc(wturned, 1)
            pe.wait_ge(wready, 2)
            pe.sem_inc(md, M.primed)
            with pe.Fori(0, G) as g:
                pe.wait_ge(vd, V(g, "on"))
                for h in range(EH):
                    for j in range(J):
                        last = nc.tensor.transpose(otp[:, h, j * P:(j + 1) * P], on[:, j, h * P:(h + 1) * P],
                                                   k["ident"][:])
                last.then_inc(md, 1)
                pe.wait_ge(ad, A(g, "oT"))
                for j in range(J):
                    for h in range(EH):
                        last = nc.tensor.matmul(wop[:, j // 2, (j % 2) * E:(j % 2) * E + E],
                                                oT[:, h, j * P:(j + 1) * P], wo[:, h, :], start=(h == 0), stop=(h == 1))
                last.then_inc(md, 1)
                pe.wait_ge(vd, V(g, "q"))
                for h in range(EH):
                    for j in range(J):
                        last = nc.tensor.transpose(qtp[:, h, j * P:(j + 1) * P], qb[:, j, h * P:(h + 1) * P],
                                                   k["identb"][:])
                last.then_inc(md, 1)
                pe.wait_ge(vd, V(g, "qT"))
                for j in range(J):
                    for h in range(EH):
                        last = nc.tensor.matmul(lin[:, j // 2, (j % 2) * E:(j % 2) * E + E],
                                                qT[:, h, j * P:(j + 1) * P], wq[:, h, :], start=(h == 0), stop=(h == 1))
                last.then_inc(md, 1)


def build(nc, d, out):
    qk_parts = nc.dram_tensor("qk_parts", [3, 2 * E, S], BF16, kind="Internal").ap()
    ot = nc.dram_tensor("attn_out", [H * (DH + 1), S], F32, kind="Internal").ap()
    kn = nc.dram_tensor("k_natural", [P, T, E], F32, kind="Internal").ap()
    vk = nc.dram_tensor("vk_beta", [P, T, 2 * E], F32, kind="Internal").ap()
    qk = nc.dram_tensor("kq_transposed", [P, T, 2 * E], F32, kind="Internal").ap()
    am = nc.dram_tensor("a_blocks", [P, T, P], F32, kind="Internal").ap()
    tt = nc.dram_tensor("t_blocks", [T, CT * HB, C * C], F32, kind="Internal").ap()
    with ExitStack() as st:
        def sb(n, s, t):
            return st.enter_context(nc.sbuf_tensor(n, s, t))

        def sem(n):
            return st.enter_context(nc.semaphore(n))

        k = {}
        setup(nc, k, d, sb, sem)
        x_res = sb("x_res", [P, T, E], F32)
        with nc.sbuf_tensor("v17", [P, T, H, DH + 1], F32) as v17:
            project(nc, k, d, sem, x_res, v17, [qk_parts[i] for i in range(3)])
            attention(nc, k, d, sem, v17, [qk_parts[i] for i in range(3)], ot)
        layer0_out(nc, k, d, sem, x_res, ot)
        gam = sb("gam", [P, T, HB], F32)
        layer1_front(nc, k, d, sem, x_res, gam, kn, vk, am, qk)
        solve_chunks(nc, k, d, sem, am, tt)
        o_all = sb("o_all", [P, T, E], F32)
        delta_rule(nc, k, d, sem, gam, o_all, kn, vk, qk, tt)
        layer1_back(nc, k, d, sem, x_res, o_all, out)


def constants():
    import numpy as np
    i = np.arange(P)
    late = (i[None, :] > i[:, None]).astype(np.float32) * np.float32(NEG)
    inv = (np.float32(1.0) / np.float32(10000.0) ** (np.arange(0, DK, 2, dtype=np.float32) / np.float32(DK)))
    ang = np.arange(S, dtype=np.float32)[:, None] * inv.astype(np.float32)[None, :]
    same = i[:, None] // C == i[None, :] // C
    return {
        "c_ident": np.eye(P, dtype=np.float32),
        "c_mask": np.stack([late, late.T]),
        "c_lower": np.tril(np.ones((NEXP, NEXP), np.float32), -1),
        "c_cos": np.cos(ang).astype(np.float32),
        "c_sin": np.sin(ang).astype(np.float32),
        "c_trim": -(i[:, None] % C > np.arange(C)[None, :]).astype(np.float32),
        "c_causal": (same & (i[:, None] <= i[None, :])).astype(np.float32),
        "c_id64": (i[:, None] % DK == np.arange(DK)[None, :]).astype(np.float32),
        "c_chunk": (i[:, None] // C == np.arange(CT)[None, :]).astype(np.float32) / C,
    }


def kernel(**inputs):
    import numpy as _np
    import concourse.bacc as _bacc
    from concourse import mybir as _mybir
    from concourse.bass_utils import run_bass_kernel_spmd as _run

    nc = _bacc.Bacc("TRN2", target_bir_lowering=False, num_devices=1)
    given = {n: _np.asarray(a) for n, a in inputs.items()}
    given["L1_ffn_weight_q"] = _np.ascontiguousarray(given["L1_ffn_weight_q"]).view(_np.int32)
    given.update(constants())
    arrays, d = {}, {}
    for name, a in given.items():
        a = _np.ascontiguousarray(a)
        arrays[f"in_{name}_dram"] = a
        d[name] = nc.dram_tensor(f"in_{name}_dram", a.shape, _mybir.dt.from_np(a.dtype), kind="ExternalInput").ap()
    out = nc.dram_tensor("out_0_dram", (1, S, E), _mybir.dt.float32, kind="ExternalOutput").ap()
    build(nc, d, out)
    r = _run(nc, [arrays], core_ids=[0])
    return r.results[0]["out_0_dram"]
```

```python
import concourse.bass as bass
from concourse import mybir
from contextlib import ExitStack


F32 = mybir.dt.float32
BF16 = mybir.dt.bfloat16
ACT = mybir.ActivationFunctionType
ALU = mybir.AluOpType
AX = mybir.AxisListType

P = 128
S, E = 4096, 256
T = S // P
G = S // 512
J = 4
EH = E // P
H, DH = 16, 16
HID = 128
GW = 16
LN_EPS = 1e-5
NEG = -1e30


class Steps:

    def __init__(self, *names, back=1):
        self.primed = back * len(names)
        self.at = {n: i + 1 for i, n in enumerate(names)}
        self.n = len(names)

    def __call__(self, turn, name):
        return turn * self.n + self.primed + self.at[name]


def bcast(ap, n):
    return ap.rearrange("(o c) -> o c", o=1).broadcast_to([n, ap.shape[0]])


def setup(nc, k, d, sb, sem):
    ld = sem("loaded_weights")
    n_ld = [0]

    def load(q, dst, src):
        q.dma_start(dst, src, allow_slow_non_contiguous=True).then_inc(ld, 16)
        n_ld[0] += 16

    for l in (0, 1):
        k[f"silu{l}"] = sb(f"silu{l}", [P, EH], F32)
        k[f"silubc{l}"] = sb(f"silubc{l}", [P, EH, P], F32)
        k[f"mod{l}"] = sb(f"mod{l}", [P, 12], F32)
        k[f"ga{l}"] = sb(f"ga{l}", [P, E], F32)
        k[f"gb{l}"] = sb(f"gb{l}", [P, E], F32)
    k["cb1"] = sb("cb1", [P, E], F32)
    k["sb1"] = sb("sb1", [P, E], F32)
    k["ident"] = sb("ident", [P, P], F32)
    k["identb"] = sb("identb", [P, P], BF16)
    k["ones"] = sb("ones", [P, P], F32)

    with ExitStack() as st:
        c = [st.enter_context(nc.sbuf_tensor(f"c{l}", [P, EH], F32)) for l in (0, 1)]
        wm = [st.enter_context(nc.sbuf_tensor(f"wm{l}", [P, EH, 6 * E], F32)) for l in (0, 1)]
        tmp = st.enter_context(nc.sbuf_tensor("sgn", [P, 4, E], F32))
        raw = st.enter_context(nc.sbuf_tensor("rawrow", [P, 4, E], F32))
        colp = st.enter_context(nc.psum_tensor("colp", [P, 2, 512], F32))
        rowp = st.enter_context(nc.psum_tensor("rowp", [P, 6, 512], F32))
        silu_done, mm_done, v_done, id_done = sem("silu_done"), sem("modmm_done"), sem("mod_done"), sem("id_done")
        block = st.enter_context(nc.Block())
        rows = [(0, 2), (0, 5), (1, 2), (1, 5), (1, 4), (1, 3)]

        @block.sync
        def _(sp):
            for l in (0, 1):
                load(sp, c[l][:], d[f"L{l}_c"].rearrange("o (h p) -> p (o h)", p=P))
                load(sp, wm[l][:], d[f"L{l}_wmod"].rearrange("(h p) n -> p h n", p=P))
            load(sp, k["ident"][:], d["c_ident"])

        @block.gpsimd
        def _(pool):
            nc.gpsimd.memset(k["ones"][:], 1.0).then_inc(id_done, 1)

        @block.scalar
        def _(act):
            act.wait_ge(ld, 16 * 5)
            for l in (0, 1):
                last = nc.scalar.activation(k[f"silu{l}"][:], c[l][:], ACT.Silu)
            last.then_inc(silu_done, 1)

        @block.vector
        def _(dve):
            dve.wait_ge(ld, 16 * 5)
            nc.vector.tensor_copy(k["identb"][:], k["ident"][:]).then_inc(id_done, 1)
            dve.wait_ge(silu_done, 1)
            dve.wait_ge(id_done, 2)
            for l in (0, 1):
                for h in range(EH):
                    last = nc.vector.tensor_scalar(k[f"silubc{l}"][:, h, :], k["ones"][:],
                                                   k[f"silu{l}"][:, h:h + 1], None, ALU.mult)
            last.then_inc(v_done, 1)
            dve.wait_ge(mm_done, 1)
            for l in (0, 1):
                nc.vector.tensor_copy(k[f"mod{l}"][:], colp[:, l, 0:12])
            for i in range(4):
                nc.vector.tensor_copy(raw[:, i, :], rowp[:, i, 0:E])
            nc.vector.tensor_scalar(k["cb1"][:], rowp[:, 4, 0:E], 1.0, None, ALU.add)
            nc.vector.tensor_copy(k["sb1"][:], rowp[:, 5, 0:E]).then_inc(v_done, 1)
            dve.wait_ge(v_done, 2)
            for l in (0, 1):
                for w in (1, 4):
                    nc.vector.tensor_scalar(k[f"mod{l}"][:, 2 * w:2 * w + 2], k[f"mod{l}"][:, 2 * w:2 * w + 2],
                                            1.0, None, ALU.add)
            nc.vector.tensor_scalar(tmp[:], raw[:], 0.0, 2.0, ALU.is_ge, ALU.mult).then_inc(v_done, 1)
            dve.wait_ge(v_done, 3)
            nc.vector.scalar_tensor_tensor(raw[:], raw[:], -1.0, raw[:], ALU.mult, ALU.max)
            nc.vector.tensor_scalar(tmp[:], tmp[:], -1.0, None, ALU.add).then_inc(v_done, 1)
            dve.wait_ge(v_done, 4)
            for i, name in enumerate(("ga0", "gb0", "ga1", "gb1")):
                last = nc.vector.scalar_tensor_tensor(k[name][:], raw[:, i, :], 0.25, tmp[:, i, :], ALU.max, ALU.mult)
            last.then_inc(v_done, 1)

        @block.tensor
        def _(pe):
            pe.wait_ge(v_done, 1)
            for l in (0, 1):
                for m in range(12):
                    for h in range(EH):
                        nc.tensor.matmul(colp[:, l, m:m + 1], wm[l][:, h, m * P:(m + 1) * P],
                                         k[f"silu{l}"][:, h:h + 1], start=(h == 0), stop=(h == 1))
            for i, (l, w) in enumerate(rows):
                for h in range(EH):
                    last = nc.tensor.matmul(rowp[:, i, 0:E], k[f"silubc{l}"][:, h, :],
                                            wm[l][:, h, w * E:(w + 1) * E], start=(h == 0), stop=(h == 1))
            last.then_inc(mm_done, 1)


def project(nc, k, d, sem, x_res, v17, HD, qk_dram):
    FV = Steps("stats", "aggr", "rstd", "xn")
    FA = Steps("std", "hT")
    FM = Steps("tp")
    V = Steps("r1_0", "r1_1", "r1_2", "r1_3", "v", "haggr", "hrstd", "hn")
    A = Steps("hi_0", "mid_0", "hi_1", "mid_1", "hi_2", "mid_2", "hi_3", "mid_3", "hstd")
    M = Steps("qk_0", "qk_1", "qk_2", "qk_3", "vh_0", "vh_1", "vh_2", "vh_3")
    with ExitStack() as st:
        def sb(n, s, t=F32):
            return st.enter_context(nc.sbuf_tensor(f"project_{n}", s, t))
        def ps(n, s, t=F32):
            return st.enter_context(nc.psum_tensor(f"project_{n}", s, t))
        wqk = sb("wqk", [P, EH, 2, E])
        wvh = sb("wvh", [P, EH, E + HID])
        bqk = sb("bqk", [P, 4])
        bvh = sb("bvh", [1, E + HID])
        st6 = sb("st6", [P, J, 6]); mv = sb("mv", [P, J, 2]); sd = sb("sd", [P, J]); rs = sb("rs", [P, J])
        hs6 = sb("hs6", [P, J, 6]); hmv = sb("hmv", [P, J, 2]); hsd = sb("hsd", [P, J]); hrs = sb("hrs", [P, J])
        xn = sb("xn", [P, J, E])
        hT = sb("hT", [P, EH, 512])
        hi = sb("hi", [P, 4, 512], BF16); mid = sb("mid", [P, 4, 512], BF16); lo = sb("lo", [P, 4, 512], BF16)
        r1 = sb("r1", [P, 4, 512])
        eps = sb("eps", [P, 1])
        tp = ps("tp", [P, EH, 512]); qkp = ps("qkp", [P, 2, 512]); vhp = ps("vhp", [P, 4, 512])
        xl, wl = sem("x_loaded"), sem("w1_loaded")
        vd, ad, md, pd = sem("p1_dve"), sem("p1_act"), sem("p1_pe"), sem("p1_pool")
        hi_out, mid_out, lo_out = sem("hi_out"), sem("mid_out"), sem("lo_out")
        fvd, fad, fmd = sem("p1_front_dve"), sem("p1_front_act"), sem("p1_front_pe")
        held = sem("aggr_held")
        sheld = sem("project_sp_held")
        block = st.enter_context(nc.Block())
        qk_out = [part.rearrange("(m p) n -> p m n", p=P) for part in qk_dram]

        @block.sync
        def _(sp):
            for dst, name in ((wqk[:, :, 0, :], "Wq"), (wqk[:, :, 1, :], "Wk"), (wvh[:, :, 0:E], "Wv"),
                              (wvh[:, :, E:], "dp_w1")):
                sp.dma_start(dst, d[f"L0_attn_{name}"].rearrange("(h p) n -> p h n", p=P)).then_inc(wl, 16)
            sp.dma_start(bqk[:, 0:2], d["L0_attn_bq"].rearrange("(h p) -> p h", p=P), allow_slow_non_contiguous=True).then_inc(wl, 16)
            sp.dma_start(bqk[:, 2:4], d["L0_attn_bk"].rearrange("(h p) -> p h", p=P), allow_slow_non_contiguous=True).then_inc(wl, 16)
            sp.dma_start(bvh[:, 0:E], d["L0_attn_bv"].rearrange("(o n) -> o n", o=1)).then_inc(wl, 16)
            sp.dma_start(bvh[:, E:], d["L0_attn_dp_b1"].rearrange("(o n) -> o n", o=1)).then_inc(wl, 16)
            for out in (hi_out, mid_out, lo_out):
                sp.sem_inc(out, 16)
            with sp.Fori(0, G) as g:
                cols = bass.ds(g * 512, 512)
                sp.wait_ge(ad, A(g, "hi_3"))
                sp.sem_inc(sheld, 1)
                sp.dma_start(qk_out[0][:, :, cols], hi[:]).then_inc(hi_out, 16)
                sp.wait_ge(ad, A(g, "mid_3"))
                sp.dma_start(qk_out[1][:, :, cols], mid[:]).then_inc(mid_out, 16)
                sp.wait_ge(pd, 4 * g + 8)
                sp.dma_start(qk_out[2][:, :, cols], lo[:]).then_inc(lo_out, 16)
            sp.wait_ge(hi_out, 16 * G + 16)
            sp.wait_ge(mid_out, 16 * G + 16)
            sp.wait_ge(lo_out, 16 * G + 16)

        @block.scalar
        def _(act):
            xv = d["L0_attn_x"].rearrange("o (t p) c -> p (o t) c", p=P)
            for g in range(G):
                act.dma_start(x_res[:, J * g:J * g + J, :], xv[:, J * g:J * g + J, :]).then_inc(xl, 16)
            act.wait_ge(wl, 16 * 8)
            act.wait_ge(pd, 4)

            def spread(g):
                act.wait_ge(fvd, FV(g, "aggr"))
                nc.scalar.activation(sd[:], mv[:, :, 1], ACT.Sqrt, bias=eps[:]).then_inc(fad, 1)

            def modulate(g):
                act.wait_ge(fmd, FM(g, "tp"))
                for h in range(EH):
                    last = nc.scalar.activation(hT[:, h, :], tp[:, h, :], ACT.Identity,
                                                bias=k["mod0"][:, h:h + 1], scale=k["mod0"][:, 2 + h:3 + h])
                last.then_inc(fad, 1)

            def parts(g, more):
                for m in range(4):
                    if m == 2 and more:
                        spread(g + 1)
                    act.wait_ge(md, M(g, f"qk_{m}"))
                    act.wait_ge(hi_out, 16 * g + 16)
                    nc.scalar.activation(hi[:, m, :], qkp[:, m % 2, :], ACT.Identity, bias=bqk[:, m:m + 1])\
                        .then_inc(ad, 1)
                    act.wait_ge(vd, V(g, f"r1_{m}"))
                    act.wait_ge(mid_out, 16 * g + 16)
                    nc.scalar.activation(mid[:, m, :], r1[:, m, :], ACT.Copy).then_inc(ad, 1)
                act.wait_ge(vd, V(g, "haggr"))
                nc.scalar.activation(hsd[:], hmv[:, :, 1], ACT.Sqrt, bias=eps[:]).then_inc(ad, 1)

            act.sem_inc(ad, A.primed)
            act.sem_inc(fad, FA.primed)
            spread(0)
            modulate(0)
            with act.Fori(0, G - 1) as g:
                parts(g, True)
                modulate(g + 1)
            parts(G - 1, False)

        @block.gpsimd
        def _(pool):
            nc.gpsimd.memset(eps[:], LN_EPS)
            nc.gpsimd.memset(v17[:, :, :, DH:DH + 1], 1.0).then_inc(pd, 4)
            with pool.Fori(0, G) as g:
                for m in range(4):
                    pool.wait_ge(ad, A(g, f"mid_{m}"))
                    pool.wait_ge(lo_out, 16 * g + 16)
                    nc.gpsimd.tensor_tensor(lo[:, m, :], r1[:, m, :], mid[:, m, :], ALU.subtract).then_inc(pd, 1)

        @block.vector
        def _(dve):
            def normalise(g):
                xt = x_res[:, bass.ds(g * J, J), :]
                for j in range(J):
                    last = nc.vector.bn_stats(st6[:, j, :], xt[:, j, :])
                last.then_inc(fvd, 1)
                dve.wait_ge(fvd, FV(g, "stats"))
                dve.wait_ge(fad, FA(g - 1, "std"))
                dve.sem_inc(held, 1)
                for j in range(J):
                    last = nc.vector.bn_aggr(mv[:, j, :], st6[:, j, :])
                last.then_inc(fvd, 1)
                dve.wait_ge(fad, FA(g, "std"))
                nc.vector.reciprocal(rs[:], sd[:]).then_inc(fvd, 1)
                dve.wait_ge(fvd, FV(g, "rstd"))
                dve.wait_ge(fmd, FM(g - 1, "tp"))
                for j in range(J):
                    last = nc.vector.tensor_scalar(xn[:, j, :], xt[:, j, :], mv[:, j, 0:1], rs[:, j:j + 1],
                                                   ALU.subtract, ALU.mult)
                last.then_inc(fvd, 1)

            def rest(g, m):
                dve.wait_ge(ad, A(g, f"hi_{m}"))
                dve.wait_ge(pd, 4 * g + m + 1)
                nc.vector.scalar_tensor_tensor(r1[:, m, :], qkp[:, m % 2, :], bqk[:, m:m + 1], hi[:, m, :],
                                               ALU.add, ALU.subtract).then_inc(vd, 1)

            def values(g):
                for j in range(J):
                    dve.wait_ge(md, M(g, f"vh_{j}"))
                    nc.vector.tensor_copy(v17[:, bass.ds(g * J + j, 1), :, 0:DH],
                                          vhp[:, j, 0:E].rearrange("p (o h c) -> p o h c", o=1, c=DH))
                    last = nc.vector.bn_stats(hs6[:, j, :], vhp[:, j, E:E + HID])
                last.then_inc(vd, 1)
                dve.wait_ge(vd, V(g, "v"))
                dve.sem_inc(held, 1)
                for j in range(J):
                    last = nc.vector.bn_aggr(hmv[:, j, :], hs6[:, j, :])
                last.then_inc(vd, 1)
                dve.wait_ge(ad, A(g, "hstd"))
                nc.vector.reciprocal(hrs[:], hsd[:]).then_inc(vd, 1)
                dve.wait_ge(vd, V(g, "hrstd"))
                for j in range(J):
                    last = nc.vector.tensor_scalar(HD[:, bass.ds(g * J + j, 1), :],
                                                   vhp[:, j, E:E + HID].rearrange("p (o c) -> p o c", o=1),
                                                   hmv[:, j, 0:1], hrs[:, j:j + 1], ALU.subtract, ALU.mult)
                last.then_inc(vd, 1)

            dve.wait_ge(xl, 16 * G)
            dve.sem_inc(fvd, FV.primed)
            dve.sem_inc(vd, V.primed)
            normalise(0)
            with dve.Fori(0, G - 1) as g:
                for m in range(2):
                    rest(g, m)
                normalise(g + 1)
                for m in range(2, 4):
                    rest(g, m)
                values(g)
            for m in range(4):
                rest(G - 1, m)
            values(G - 1)

        @block.tensor
        def _(pe):
            def turn_over(g):
                pe.wait_ge(fvd, FV(g, "xn"))
                for h in range(EH):
                    for j in range(J):
                        last = nc.tensor.transpose(tp[:, h, j * P:(j + 1) * P], xn[:, j, h * P:(h + 1) * P],
                                                   k["ident"][:])
                last.then_inc(fmd, 1)

            def products(g):
                pe.wait_ge(fad, FA(g, "hT"))
                for m in range(4):
                    pe.wait_ge(vd, V(g, f"r1_{m - 2}") if m >= 2 else V(g - 1, f"r1_{m + 2}"))
                    for h in range(EH):
                        last = nc.tensor.matmul(qkp[:, m % 2, :], wqk[:, h, m // 2, (m % 2) * P:(m % 2) * P + P],
                                                hT[:, h, :], start=(h == 0), stop=(h == 1))
                    last.then_inc(md, 1)
                pe.wait_ge(vd, V(g - 1, "hn"))
                for j in range(J):
                    dst = vhp[:, j, 0:E + HID]
                    nc.tensor.matmul(dst, k["ones"][0:1, :], bvh[:], start=True, stop=False)
                    for h in range(EH):
                        last = nc.tensor.matmul(dst, hT[:, h, j * P:(j + 1) * P], wvh[:, h, :],
                                                start=False, stop=(h == 1))
                    last.then_inc(md, 1)

            pe.wait_ge(wl, 16 * 8)
            pe.sem_inc(md, M.primed)
            pe.sem_inc(fmd, FM.primed)
            turn_over(0)
            with pe.Fori(0, G - 1) as g:
                products(g)
                turn_over(g + 1)
            products(G - 1)


class Gate:

    def __init__(self, nc, d, sb, sem, v17, HD):
        self.nc, self.d, self.v17, self.HD = nc, d, v17, HD
        self.rows = sb("gate_rows", [P, 3, HID])
        self.grow = sb("gate_grow", [P, 3, GW])
        self.g2 = sb("gate_g2", [P, 2])
        self.G1 = sb("gate_G1", [P, T, GW])
        self.gate = sb("gate_gate", [P, T])
        self.wl, self.pd, self.ad = sem("gate_loaded"), sem("gate_pool"), sem("gate_act")

    def load(self, sp):
        d, wl = self.d, self.wl
        for i, n in enumerate(("ln_g", "ln_b")):
            sp.dma_start(self.rows[:, i, :], bcast(d[f"L0_attn_{n}"], P)).then_inc(wl, 16)
        sp.dma_start(self.rows[:, 2, :], bcast(d["L0_attn_dp_w2"].rearrange("a o -> (a o)"), P)).then_inc(wl, 16)
        sp.dma_start(self.grow[:, 0, :], bcast(d["L0_attn_g_w1"].rearrange("o a -> (o a)"), P)).then_inc(wl, 16)
        sp.dma_start(self.grow[:, 1, :], bcast(d["L0_attn_g_b1"], P)).then_inc(wl, 16)
        sp.dma_start(self.grow[:, 2, :], bcast(d["L0_attn_g_w2"].rearrange("a o -> (a o)"), P)).then_inc(wl, 16)
        sp.dma_start(self.g2[:, 0:1], bcast(d["L0_attn_dp_b2"], P)).then_inc(wl, 16)
        sp.dma_start(self.g2[:, 1:2], bcast(d["L0_attn_g_b2"], P)).then_inc(wl, 16)

    def on_act(self, act):
        act.wait_ge(self.pd, 2)
        self.nc.scalar.activation(self.HD[:], self.HD[:], ACT.Gelu).then_inc(self.ad, 1)
        act.wait_ge(self.pd, 13)
        self.nc.scalar.activation(self.G1[:], self.G1[:], ACT.Gelu).then_inc(self.ad, 1)
        act.wait_ge(self.pd, 18)
        self.nc.scalar.activation(self.gate[:], self.G1[:, :, 0], ACT.Tanh, bias=self.g2[:, 1:2]).then_inc(self.ad, 1)

    def on_pool(self, pool):
        nc, HD, G1, pd = self.nc, self.HD, self.G1, self.pd
        row = lambda i: self.rows[:, i:i + 1, :].broadcast_to([P, T, HID])
        wide = lambda i: self.grow[:, i:i + 1, :].broadcast_to([P, T, GW])

        def sum_over(a, width, done):
            while width > 1:
                width //= 2
                nc.gpsimd.tensor_tensor(a[:, :, 0:width], a[:, :, 0:width], a[:, :, width:2 * width],
                                        ALU.add).then_inc(pd, 1)
                done += 1
                pool.wait_ge(pd, done)

        pool.wait_ge(self.wl, 16 * 8)
        nc.gpsimd.tensor_tensor(HD[:], HD[:], row(0), ALU.mult).then_inc(pd, 1)
        pool.wait_ge(pd, 1)
        nc.gpsimd.tensor_tensor(HD[:], HD[:], row(1), ALU.add).then_inc(pd, 1)
        pool.wait_ge(self.ad, 1)
        nc.gpsimd.tensor_tensor(HD[:], HD[:], row(2), ALU.mult).then_inc(pd, 1)
        pool.wait_ge(pd, 3)
        sum_over(HD, HID, 3)
        nc.gpsimd.tensor_scalar(HD[:, :, 0:1], HD[:, :, 0:1], self.g2[:, 0:1], None, ALU.add).then_inc(pd, 1)
        pool.wait_ge(pd, 11)
        nc.gpsimd.tensor_tensor(G1[:], HD[:, :, 0:1].broadcast_to([P, T, GW]), wide(0), ALU.mult).then_inc(pd, 1)
        pool.wait_ge(pd, 12)
        nc.gpsimd.tensor_tensor(G1[:], G1[:], wide(1), ALU.add).then_inc(pd, 1)
        pool.wait_ge(self.ad, 2)
        nc.gpsimd.tensor_tensor(G1[:], G1[:], wide(2), ALU.mult).then_inc(pd, 1)
        pool.wait_ge(pd, 14)
        sum_over(G1, GW, 14)
        pool.wait_ge(self.ad, 3)
        vv = self.v17[:, :, :, 0:DH]
        nc.gpsimd.tensor_tensor(vv, vv, self.gate[:].rearrange("p (t o c) -> p t o c", o=1, c=1)
                                .broadcast_to([P, T, H, DH]), ALU.mult).then_inc(pd, 1)
        pool.wait_ge(pd, 19)


def attention(nc, k, d, sem, v17, qk_dram, ot_dram, gate=None, later_loads=None):
    ROWS = 6 * DH
    MAXR = ROWS + 3
    KPARTS = (0, 0, 0, 1, 1, 2)
    QPARTS = (0, 1, 2, 0, 1, 0)
    BLK = 1024
    NPT = 4
    units = []
    for s in range(2):
        for kt in range(16 * s + 16):
            for b in range(2):
                q0, q1 = 2048 * s + BLK * b, 2048 * s + BLK * b + BLK
                if kt * P < q1:
                    units.append((s, kt, max(q0, kt * P), q1))
    NE = len(units)
    last_of = [max(i for i, u in enumerate(units) if u[0] == s) for s in range(2)]
    pieces = [(i, c, min(512, P * (i + 1) - 512 * c)) for i in range(T) for c in range(i // 4 + 1)]
    NM = len(pieces) + 1
    SLACK = 9
    cost_u = [q1 - q0 + 200 for _, _, q0, q1 in units]
    cost_p = [w + 60 for _, _, w in pieces] + [P]
    goal = [sum(cost_u[:u + 1]) / sum(cost_u[:NE - SLACK]) * sum(cost_p) for u in range(NE)]
    share = [sum(sum(cost_p[:n + 1]) <= g + 1 for n in range(NM)) for g in goal]
    LAG = 2
    LOADS = 12 * 16
    NB = 3
    TURNS = H // NB

    with ExitStack() as st:
        def sb(n, s, t=F32):
            return st.enter_context(nc.sbuf_tensor(f"attn_{n}", s, t))
        def ps(n, s, t=F32):
            return st.enter_context(nc.psum_tensor(f"attn_{n}", s, t))
        KX = [sb(f"KX{b}", [P, S], BF16) for b in range(NB)]
        QX = [sb(f"QX{b}", [P, S], BF16) for b in range(NB)]
        VH = [sb(f"VH{b}", [P, T, DH + 1]) for b in range(NB)]
        PT = [sb(f"PT{b}", [P, BLK]) for b in range(NPT)]
        OS = [sb(f"OS{b}", [P, 512]) for b in range(2)]
        maskf = sb("maskf", [P, 2, P]); maskb = sb("maskb", [P, 2, P], BF16)
        pm = sb("pm", [P, T, 8]); nm = sb("nm", [P, T])
        nmT = sb("nmT", [32, P]); rT = sb("rT", [32, P])
        parts = sb("parts", [32, 3, P], BF16)
        ES = [ps(f"ES{b}", [P, BLK]) for b in range(2)]
        MS = [ps(f"MS{b}", [P, 512]) for b in range(3)]
        OP = ps("OP", [P, 512])
        held = sem("pool_held")
        mask_in, ready = sem("mask_in"), sem("attn_ready")
        loaded = [sem(f"qk_loaded{b}") for b in range(NB)]
        max_scores, max_taken, negmax = sem("max_scores"), sem("max_taken"), sem("negmax")
        split, v_copied, max_rows = sem("max_split"), sem("v_copied"), sem("max_rows")
        exp_scores, exp_done, pv_done = sem("exp_scores"), sem("exp_done"), sem("pv_done")
        o_evac, o_out = sem("o_evac"), [sem(f"o_out{s}") for s in range(2)]
        sheld = sem("attn_sp_held")
        block = st.enter_context(nc.Block())

        @block.sync
        def _(sp):
            sp.dma_start(maskf[:], d["c_mask"].rearrange("a p n -> p a n")).then_inc(mask_in, 16)
            if gate:
                gate.load(sp)

            def load(h, b):
                for r in range(6):
                    sp.dma_start(KX[b][DH * r:DH * r + DH, :],
                                 qk_dram[KPARTS[r]][bass.ds(E + h * DH, DH), :]).then_inc(loaded[b], 16)
                    sp.dma_start(QX[b][DH * r:DH * r + DH, :],
                                 qk_dram[QPARTS[r]][bass.ds(h * DH, DH), :]).then_inc(loaded[b], 16)

            def store(h, s):
                sp.wait_ge(o_evac, 2 * h + s + 3)
                sp.sem_inc(sheld, 1)
                for j in range(4):
                    sp.dma_start(ot_dram[bass.ds(h * (DH + 1), DH + 1), 2048 * s + 512 * j:2048 * s + 512 * j + 512],
                                 OS[s][32 * j:32 * j + DH + 1, :]).then_inc(o_out[s], 16)

            def turn(h, b, more):
                store(h, 0)
                if more:
                    sp.wait_ge(exp_scores, NE * h + NE)
                    sp.sem_inc(sheld, 1)
                    load(h + NB, b)
                store(h, 1)

            for s in range(2):
                sp.sem_inc(o_out[s], 64 + 64 * s)
            for b in range(NB):
                load(b, b)
            if later_loads:
                later_loads(sp)
            with sp.Fori(0, TURNS - 1) as i:
                for b in range(NB):
                    turn(NB * i + b, b, True)
            for h in range(H - 1 - NB, H):
                turn(h, h % NB, h + NB < H)
            for s in range(2):
                sp.wait_ge(o_out[s], 64 * H + 64 + 64 * s)

        @block.gpsimd
        def _(pool):
            for b in range(NB):
                nc.gpsimd.memset(KX[b][ROWS:MAXR, :], 1.0).then_inc(ready, 1)

            def split_max(h, b):
                pool.wait_ge(pv_done, NE * h + NE)
                nc.gpsimd.tensor_copy(VH[b][:].rearrange("p t (o c) -> p t o c", o=1),
                                      v17[:, :, bass.ds(h, 1), :]).then_inc(v_copied, 1)
                pool.wait_ge(max_taken, NM * h + NM)
                pool.sem_inc(held, 1)
                nc.gpsimd.tensor_scalar(parts[:, 0, :], nmT[:], 1.0, None, ALU.mult).then_inc(split, 1)
                pool.wait_ge(split, 4 * h + 5)
                nc.gpsimd.tensor_tensor(rT[:], nmT[:], parts[:, 0, :], ALU.subtract).then_inc(split, 1)
                pool.wait_ge(split, 4 * h + 6)
                pool.sem_inc(held, 1)
                nc.gpsimd.tensor_scalar(parts[:, 1, :], rT[:], 1.0, None, ALU.mult).then_inc(split, 1)
                pool.wait_ge(split, 4 * h + 7)
                nc.gpsimd.tensor_tensor(parts[:, 2, :], rT[:], parts[:, 1, :], ALU.subtract).then_inc(split, 1)
                pool.wait_ge(split, 4 * h + 8)
                pool.sem_inc(held, 1)
                for r in range(3):
                    pool.dma_start(QX[b][ROWS + r:ROWS + r + 1, :].rearrange("o (t c) -> o t c", c=P),
                                   parts[:, r, :]).then_inc(max_rows, 16)
            if gate:
                pool.wait_ge(ready, NB + 1)
                gate.on_pool(pool)
            pool.sem_inc(split, 4)
            with pool.Fori(0, TURNS) as i:
                for b in range(NB):
                    split_max(NB * i + b, b)
            split_max(H - 1, (H - 1) % NB)

        @block.scalar
        def _(act):
            def take_out(e, pv_count, out_count):
                act.wait_ge(pv_done, pv_count)
                act.wait_ge(o_out[e], out_count)
                nc.scalar.activation(OS[e][:], OP[:], ACT.Copy).then_inc(o_evac, 1)

            if gate:
                gate.on_act(act)
            act.sem_inc(o_evac, 1)
            with act.Fori(0, H) as h:
                for u, (s, kt, q0, q1) in enumerate(units):
                    w = q1 - q0
                    act.wait_ge(exp_scores, NE * h + u + 1)
                    act.wait_ge(pv_done, NE * h + u - NPT + 1 + 3 * NE)
                    nc.scalar.activation(PT[u % NPT][:, BLK - w:], ES[u % 2][:, BLK - w:], ACT.Exp,
                                         scale=DH ** -0.5).then_inc(exp_done, 1)
                    if u == 1:
                        take_out(1, NE * h + 3 * NE, 64 * h + 64)
                    if u == last_of[0] + LAG:
                        take_out(0, NE * h + last_of[0] + 1 + 3 * NE, 64 * h + 64)
            take_out(1, NE * H + 3 * NE, 64 * H + 64)

        @block.vector
        def _(dve):
            dve.wait_ge(mask_in, 16)
            nc.vector.tensor_copy(maskb[:], maskf[:])
            nc.vector.memset(OP[:], 0.0)
            nc.vector.memset(pm[:], NEG).then_inc(ready, 1)

            with dve.Fori(0, H) as h:
                for n, (i, c, w) in enumerate(pieces):
                    dve.wait_ge(max_scores, NM * h + n + 1)
                    nc.vector.tensor_reduce(pm[:, i, c:c + 1], MS[n % 3][:, 0:w], AX.X, ALU.max).then_inc(max_taken, 1)
                dve.wait_ge(max_taken, NM * h + NM - 1)
                nc.vector.tensor_reduce(nm[:], pm[:], AX.X, ALU.max, negate=True).then_inc(negmax, 1)
                dve.wait_ge(max_scores, NM * h + NM)
                dve.wait_ge(split, 4 * h + 4)
                nc.vector.tensor_copy(nmT[:], MS[(NM - 1) % 3][0:T, 0:P]).then_inc(max_taken, 1)

        @block.tensor
        def _(pe):
            def max_piece(h, b, n):
                if n < 3:
                    if not (isinstance(h, int) and h == 0):
                        pe.wait_ge(max_taken, NM * h)
                else:
                    pe.wait_ge(max_taken, NM * h + n - 2)
                if n == NM - 1:
                    pe.wait_ge(negmax, h + 1)
                    nc.tensor.transpose(MS[n % 3][0:T, 0:P], nm[:], k["ident"][:]).then_inc(max_scores, 1)
                    return
                i, c, w = pieces[n]
                diag = c == i // 4
                if diag:
                    nc.tensor.matmul(MS[n % 3][:, w - P:w], k["identb"][:], maskb[:, 0, :],
                                     start=True, stop=False, skip_group_check=True)
                last = nc.tensor.matmul(MS[n % 3][:, 0:w], QX[b][0:ROWS, i * P:(i + 1) * P],
                                        KX[b][0:ROWS, 512 * c:512 * c + w], start=not diag, stop=True,
                                        skip_group_check=True)
                last.then_inc(max_scores, 1)

            def scores(h, b, u):
                s, kt, q0, q1 = units[u]
                if u == 0:
                    pe.wait_ge(max_rows, 48 * h + 48)
                if u < 2:
                    if not (isinstance(h, int) and h == 0):
                        pe.wait_ge(exp_done, NE * h)
                else:
                    pe.wait_ge(exp_done, NE * h + u - 1)
                for c in (q1 - BLK, q1 - 512):
                    a = max(c, q0)
                    if a >= c + 512:
                        continue
                    o = a - (q1 - BLK)
                    diag = c <= kt * P
                    if diag:
                        nc.tensor.matmul(ES[u % 2][:, o:o + P], k["identb"][:], maskb[:, 1, :],
                                         start=True, stop=False, skip_group_check=True)
                    last = nc.tensor.matmul(ES[u % 2][:, o:o + c + 512 - a], KX[b][0:MAXR, kt * P:(kt + 1) * P],
                                            QX[b][0:MAXR, a:c + 512], start=not diag, stop=True,
                                            skip_group_check=True)
                last.then_inc(exp_scores, 1)

            def pv(h, b, u):
                s, kt, q0, q1 = units[u]
                if u == 0:
                    pe.wait_ge(v_copied, h + 1)
                    pe.wait_ge(o_evac, 2 * h + 2)
                if u == last_of[0] + 1:
                    pe.wait_ge(o_evac, 2 * h + 3)
                pe.wait_ge(exp_done, NE * h + u + 1)
                for c in (q1 - BLK, q1 - 512):
                    a = max(c, q0)
                    if a >= c + 512:
                        continue
                    j = c // 512 % 4
                    last = nc.tensor.matmul(OP[32 * j:32 * j + DH + 1, a - c:512], VH[b][:, kt, :],
                                            PT[u % NPT][:, a - (q1 - BLK):c + 512 - (q1 - BLK)],
                                            start=(kt == 0), stop=(kt >= c // P), skip_group_check=True)
                last.then_inc(pv_done, 1)

            pe.wait_ge(ready, NB + 1)
            pe.sem_inc(pv_done, 3 * NE)
            pe.wait_ge(loaded[0], LOADS)
            for n in range(NM):
                max_piece(0, 0, n)
            scores(0, 0, 0)
            scores(0, 0, 1)

            def turn(h, i, b):
                more = b is not None
                b = b or 0
                if more:
                    pe.wait_ge(loaded[(b + 1) % NB], LOADS * (i + 1 + (b + 1) // NB))
                for u in range(NE):
                    todo = list(range(share[u - 1] if u else 0, share[u])) if more else []
                    if todo:
                        max_piece(h + 1, (b + 1) % NB, todo.pop(0))
                    if u >= LAG:
                        pv(h, b, u - LAG)
                    while todo:
                        max_piece(h + 1, (b + 1) % NB, todo.pop(0))
                    if u + 2 < NE:
                        scores(h, b, u + 2)
                    elif more:
                        scores(h + 1, (b + 1) % NB, u + 2 - NE)
                for u in range(NE - LAG, NE):
                    pv(h, b, u)
            with pe.Fori(0, TURNS) as i:
                for b in range(NB):
                    turn(NB * i + b, i, b)
            turn(H - 1, TURNS, None)


NEXP = 8


def layer0_weights(nc, d, sb, sem):
    wo = sb("l0out_wo", [P, EH, E], F32); bo = sb("l0out_bo", [1, E], F32)
    w_in = sb("l0out_w_in", [P, EH, 2, 2 * E], F32); w_so = sb("l0out_w_so", [P, EH, E], F32); w2 = sb("l0out_w2", [P, EH, NEXP, E], F32)
    wg = sb("l0out_wg", [P, EH, NEXP], F32); bg = sb("l0out_bg", [1, NEXP], F32)
    lower = sb("l0out_lower", [P, NEXP, NEXP], F32)
    wl = sem("w3_loaded")

    def issue(sp):
        def w(dst, src):
            sp.dma_start(dst, src).then_inc(wl, 16)
        w(wo[:], d["L0_attn_Wo"].rearrange("(h p) n -> p h n", p=P))
        w(bo[:], d["L0_attn_bo"].rearrange("(o n) -> o n", o=1))
        w(w_in[:, :, 0, :], d["L0_ffn_w_shared_in"].rearrange("(h p) n -> p h n", p=P))
        w(w_in[:, :, 1, :], d["L0_ffn_w1_shared"].rearrange("(h p) n -> p h n", p=P))
        w(w_so[:], d["L0_ffn_w_shared_out"].rearrange("(h p) n -> p h n", p=P))
        for h in range(EH):
            w(w2[:, h, :, :], d["L0_ffn_w2"][:, h * P:(h + 1) * P, :].rearrange("e p n -> p e n"))
        w(wg[:], d["L0_ffn_w_gate"].rearrange("(h p) n -> p h n", p=P))
        w(bg[:], d["L0_ffn_gate_bias"].rearrange("(o n) -> o n", o=1))
        w(lower[:], d["c_lower"].rearrange("(o a) b -> o a b", o=1).broadcast_to([P, NEXP, NEXP]))

    return (wo, bo, w_in, w_so, w2, wg, bg, lower, wl), issue


def layer0_out(nc, k, d, sem, x_res, ot_dram, weights, later_loads=None):
    FV = Steps("rl_0", "rl_1", "att", "x1", "stats", "aggr", "rstd", "xn", back=0)
    FA = Steps("std", "hT", back=0)
    FM = Steps("wo", "tp", back=0)
    V = Steps("lmax", "lsub", "esum", "erec", "p", "gt", "eq", "eqm", "cnt", "rank", "w", "s_0", "s_1", "s_2", "s_3",
              *[f"acc_{j}_{e}" for j in range(J) for e in range(NEXP + 1)])
    A = Steps("exp", "sg_0", "sg_1", "sg_2", "sg_3")
    M = Steps("lg", "ab_0", "ab_1", "ab_2", "ab_3",
              *[n for j in range(J) for n in (f"sh_{j}", *[f"ex_{j}_{e}" for e in range(NEXP // 2)])])
    with ExitStack() as st:
        def sb(n, s, t=F32):
            return st.enter_context(nc.sbuf_tensor(f"l0out_{n}", s, t))
        def ps(n, s, t=F32):
            return st.enter_context(nc.psum_tensor(f"l0out_{n}", s, t))
        wo, bo, w_in, w_so, w2, wg, bg, lower, wl = weights
        OTg = sb("OTg", [P, EH, 512]); LB = sb("LB", [P, EH, 512])
        st6 = sb("st6", [P, J, 6]); mv = sb("mv", [P, J, 2]); sd = sb("sd", [P, J]); rs = sb("rs", [P, J])
        eps = sb("eps", [P, 1])
        xn = sb("xn", [P, J, E]); hT = sb("hT", [P, EH, 512])
        sg = sb("sg", [P, 2, 512]); sT = sb("sT", [P, 4, 512])
        lm = sb("lm", [P, J, 1]); lx = sb("lx", [P, J, NEXP]); es = sb("es", [P, J, 1]); er = sb("er", [P, J, 1])
        p = sb("p", [P, J, NEXP]); gt = sb("gt", [P, J, NEXP, NEXP]); eq = sb("eq", [P, J, NEXP, NEXP])
        rank = sb("rank", [P, J, NEXP]); w = sb("w", [P, J, NEXP])
        tp = ps("tp", [P, EH, 512]); ring = ps("ring", [P, 4, 512]); shp = ps("shp", [P, 512]); lgp = ps("lgp", [P, 512])
        scaled, eps_set = sem("w3_scaled"), sem("eps_set")
        ol = sem("attn_loaded")
        vd, ad, md, held = sem("p3_dve"), sem("p3_act"), sem("p3_pe"), sem("p3_held")
        fvd, fad, fmd = sem("p3_front_dve"), sem("p3_front_act"), sem("p3_front_pe")
        sheld = sem("l0out_sp_held")
        block = st.enter_context(nc.Block())
        NWL = 16 * 10
        ot3 = ot_dram.rearrange("(h r) q -> h r q", r=DH + 1)

        @block.sync
        def _(sp):
            def load(g):
                cols = bass.ds(g * 512, 512)
                for h in range(EH):
                    hs = slice(8 * h, 8 * h + 8)
                    sp.dma_start(OTg[:, h, :], ot3[hs, 0:DH, cols]).then_inc(ol, 16)
                    sp.dma_start(LB[:, h, :], ot3[hs, DH:DH + 1, cols].broadcast_to([8, DH, 512])).then_inc(ol, 16)
            load(0)
            if later_loads:
                later_loads(sp)
            with sp.Fori(1, G) as g:
                sp.wait_ge(fmd, FM(g - 1, "wo"))
                sp.sem_inc(sheld, 1)
                load(g)

        @block.gpsimd
        def _(pool):
            nc.gpsimd.memset(eps[:], LN_EPS).then_inc(eps_set, 1)

        @block.scalar
        def _(act):
            act.wait_ge(eps_set, 1)

            def front(g):
                act.wait_ge(fvd, FV(g, "aggr"))
                nc.scalar.activation(sd[:], mv[:, :, 1], ACT.Sqrt, bias=eps[:]).then_inc(fad, 1)
                act.wait_ge(fmd, FM(g, "tp"))
                for h in range(EH):
                    last = nc.scalar.activation(hT[:, h, :], tp[:, h, :], ACT.Identity,
                                                bias=k["mod0"][:, 6 + h:7 + h], scale=k["mod0"][:, 8 + h:9 + h])
                last.then_inc(fad, 1)

            def network(g):
                act.wait_ge(vd, V(g, "lsub"))
                nc.scalar.activation(lx[:], lx[:], ACT.Exp).then_inc(ad, 1)
                for i in range(4):
                    act.wait_ge(md, M(g, f"ab_{i}"))
                    if i < 2:
                        act.wait_ge(vd, V(g - 1, f"s_{i + 2}"))
                    else:
                        act.wait_ge(vd, V(g, f"s_{i - 2}"))
                    nc.scalar.activation(sg[:, i % 2, :], ring[:, 2 * (i % 2), :], ACT.Silu).then_inc(ad, 1)

            act.sem_inc(ad, A.primed)
            front(0)
            with act.Fori(0, G - 1) as g:
                network(g)
                front(g + 1)
            network(G - 1)

        @block.vector
        def _(dve):
            dve.wait_ge(wl, NWL)
            nc.vector.tensor_tensor(wo[:], wo[:], k["ga0"][:].rearrange("p (o c) -> p o c", o=1)
                                    .broadcast_to([P, EH, E]), ALU.mult)
            nc.vector.tensor_tensor(bo[:], bo[:], k["ga0"][0:1, :], ALU.mult)
            nc.vector.tensor_tensor(w_so[:], w_so[:], k["gb0"][:].rearrange("p (o c) -> p o c", o=1)
                                    .broadcast_to([P, EH, E]), ALU.mult)
            for h in range(EH):
                last = nc.vector.tensor_tensor(w2[:, h, :, :], w2[:, h, :, :],
                                               k["gb0"][:].rearrange("p (o c) -> p o c", o=1)
                                               .broadcast_to([P, NEXP, E]), ALU.mult)
            last.then_inc(scaled, 1)

            def divide(g, part):
                if part < 2:
                    dve.wait_ge(ol, 64 * g + 64)
                    nc.vector.reciprocal(LB[:, part, :], LB[:, part, :]).then_inc(fvd, 1)
                else:
                    dve.wait_ge(fvd, FV(g, "rl_1"))
                    nc.vector.tensor_tensor(OTg[:], OTg[:], LB[:], ALU.mult).then_inc(fvd, 1)

            def residual(g):
                xt = x_res[:, bass.ds(g * J, J), :]
                dve.wait_ge(fmd, FM(g, "wo"))
                for a in range(2):
                    last = nc.vector.tensor_tensor(xt[:, 2 * a:2 * a + 2, :], xt[:, 2 * a:2 * a + 2, :],
                                                   tp[:, a, :].rearrange("p (j c) -> p j c", j=2), ALU.add)
                last.then_inc(fvd, 1)
                dve.wait_ge(fvd, FV(g, "x1"))
                dve.sem_inc(held, 1)
                for j in range(J):
                    last = nc.vector.bn_stats(st6[:, j, :], xt[:, j, :])
                last.then_inc(fvd, 1)
                dve.wait_ge(fvd, FV(g, "stats"))
                dve.sem_inc(held, 1)
                for j in range(J):
                    last = nc.vector.bn_aggr(mv[:, j, :], st6[:, j, :])
                last.then_inc(fvd, 1)

            def normalise(g):
                xt = x_res[:, bass.ds(g * J, J), :]
                dve.wait_ge(fad, FA(g, "std"))
                nc.vector.reciprocal(rs[:], sd[:]).then_inc(fvd, 1)
                dve.wait_ge(fvd, FV(g, "rstd"))
                for j in range(J):
                    last = nc.vector.tensor_scalar(xn[:, j, :], xt[:, j, :], mv[:, j, 0:1], rs[:, j:j + 1],
                                                   ALU.subtract, ALU.mult)
                last.then_inc(fvd, 1)

            def route(g):
                dve.wait_ge(md, M(g, "lg"))
                lg = lgp[:, 0:J * NEXP].rearrange("p (j e) -> p j e", e=NEXP)
                nc.vector.tensor_reduce(lm[:, :, 0], lg, AX.X, ALU.max).then_inc(vd, 1)
                dve.wait_ge(vd, V(g, "lmax"))
                nc.vector.tensor_tensor(lx[:], lg, lm[:].broadcast_to([P, J, NEXP]), ALU.subtract).then_inc(vd, 1)
                dve.wait_ge(ad, A(g, "exp"))
                nc.vector.tensor_reduce(es[:, :, 0], lx[:], AX.X, ALU.add).then_inc(vd, 1)
                dve.wait_ge(vd, V(g, "esum"))
                nc.vector.reciprocal(er[:], es[:]).then_inc(vd, 1)
                dve.wait_ge(vd, V(g, "erec"))
                nc.vector.tensor_tensor(p[:], lx[:], er[:].broadcast_to([P, J, NEXP]), ALU.mult).then_inc(vd, 1)
                dve.wait_ge(vd, V(g, "p"))
                pj = p[:].rearrange("p j (o e) -> p j o e", o=1).broadcast_to([P, J, NEXP, NEXP])
                pe_ = p[:].rearrange("p j (e o) -> p j e o", o=1).broadcast_to([P, J, NEXP, NEXP])
                nc.vector.tensor_tensor(gt[:], pj, pe_, ALU.is_gt).then_inc(vd, 1)
                nc.vector.tensor_tensor(eq[:], pj, pe_, ALU.is_equal).then_inc(vd, 1)
                dve.wait_ge(vd, V(g, "eq"))
                nc.vector.tensor_tensor(eq[:], eq[:], lower[:].rearrange("p (o a) b -> p o a b", o=1)
                                        .broadcast_to([P, J, NEXP, NEXP]), ALU.mult).then_inc(vd, 1)
                dve.wait_ge(vd, V(g, "eqm"))
                nc.vector.tensor_tensor(gt[:], gt[:], eq[:], ALU.add).then_inc(vd, 1)
                dve.wait_ge(vd, V(g, "cnt"))
                nc.vector.tensor_reduce(rank[:], gt[:], AX.X, ALU.add).then_inc(vd, 1)
                dve.wait_ge(vd, V(g, "rank"))
                nc.vector.scalar_tensor_tensor(w[:], rank[:], 1.5, p[:], ALU.is_lt, ALU.mult).then_inc(vd, 1)

            def gate_hidden(g, i):
                dve.wait_ge(ad, A(g, f"sg_{i}"))
                nc.vector.tensor_tensor(sT[:, i, :], ring[:, 2 * (i % 2) + 1, :], sg[:, i % 2, :],
                                        ALU.mult).then_inc(vd, 1)

            def experts(g, j):
                xt = x_res[:, bass.ds(g * J, J), :]
                dve.wait_ge(md, M(g, f"sh_{j}"))
                nc.vector.tensor_tensor(xt[:, j, :], xt[:, j, :], (shp, lgp)[j % 2][:, 0:E],
                                        ALU.add).then_inc(vd, 1)
                for e in range(NEXP):
                    if e % 2 == 0:
                        dve.wait_ge(md, M(g, f"ex_{j}_{e // 2}"))
                    dve.wait_ge(vd, V(g, f"acc_{j}_{e}"))
                    nc.vector.scalar_tensor_tensor(xt[:, j, :], ring[:, e // 2, (e % 2) * E:(e % 2) * E + E],
                                                   w[:, j, e:e + 1], xt[:, j, :], ALU.mult, ALU.add).then_inc(vd, 1)

            dve.sem_inc(vd, V.primed)
            for part in range(3):
                divide(0, part)
            residual(0)
            normalise(0)
            with dve.Fori(0, G - 1) as g:
                route(g)
                for i in range(4):
                    gate_hidden(g, i)
                    if i < 3:
                        divide(g + 1, i)
                experts(g, 0)
                residual(g + 1)
                experts(g, 1)
                normalise(g + 1)
                experts(g, 2)
                experts(g, 3)
            route(G - 1)
            for i in range(4):
                gate_hidden(G - 1, i)
            for j in range(J):
                experts(G - 1, j)

        @block.tensor
        def _(pe):
            pe.wait_ge(scaled, 1)

            def project(g, first=False):
                if not first:
                    pe.wait_ge(fad, FA(g - 1, "hT"))
                pe.wait_ge(fvd, FV(g, "att"))
                for j in range(J):
                    dst = tp[:, j // 2, (j % 2) * E:(j % 2) * E + E]
                    nc.tensor.matmul(dst, k["ones"][0:1, :], bo[:], start=True, stop=False)
                    for h in range(EH):
                        last = nc.tensor.matmul(dst, OTg[:, h, j * P:(j + 1) * P], wo[:, h, :],
                                                start=False, stop=(h == 1))
                last.then_inc(fmd, 1)

            def turn_over(g):
                pe.wait_ge(fvd, FV(g, "xn"))
                for h in range(EH):
                    for j in range(J):
                        last = nc.tensor.transpose(tp[:, h, j * P:(j + 1) * P], xn[:, j, h * P:(h + 1) * P],
                                                   k["ident"][:])
                last.then_inc(fmd, 1)

            def network(g):
                pe.wait_ge(fad, FA(g, "hT"))
                pe.wait_ge(vd, V(g - 1, f"acc_{J - 1}_0"))
                for j in range(J):
                    dst = lgp[:, j * NEXP:(j + 1) * NEXP]
                    nc.tensor.matmul(dst, k["ones"][0:1, :], bg[:], start=True, stop=False)
                    for h in range(EH):
                        last = nc.tensor.matmul(dst, hT[:, h, j * P:(j + 1) * P], wg[:, h, :],
                                                start=False, stop=(h == 1))
                last.then_inc(md, 1)
                for i in range(4):
                    if i < 2:
                        pe.wait_ge(vd, V(g - 1, f"acc_{J - 1}_{NEXP}"))
                    else:
                        pe.wait_ge(vd, V(g, f"s_{i - 2}"))
                    for ab in range(2):
                        for h in range(EH):
                            o = ab * E + (i % 2) * P
                            last = nc.tensor.matmul(ring[:, 2 * (i % 2) + ab, :], w_in[:, h, i // 2, o:o + P],
                                                    hT[:, h, :], start=(h == 0), stop=(h == 1))
                    last.then_inc(md, 1)

            def experts(g, j):
                if j == 0:
                    pe.wait_ge(vd, V(g, "s_3"))
                if j == 1:
                    pe.wait_ge(vd, V(g, "lsub"))
                if j >= 2:
                    pe.wait_ge(vd, V(g, f"acc_{j - 2}_0"))
                for h in range(EH):
                    last = nc.tensor.matmul((shp, lgp)[j % 2][:, 0:E], sT[:, h, j * P:(j + 1) * P],
                                            w_so[:, h, :], start=(h == 0), stop=(h == 1))
                last.then_inc(md, 1)
                for e in range(NEXP // 2):
                    if j:
                        pe.wait_ge(vd, V(g, f"acc_{j - 1}_{2 * e + 2}"))
                    for h in range(EH):
                        last = nc.tensor.matmul(ring[:, e, :], sT[:, 2 + h, j * P:(j + 1) * P],
                                                w2[:, h, 2 * e:2 * e + 2, :].rearrange("p a b -> p (a b)"),
                                                start=(h == 0), stop=(h == 1))
                    last.then_inc(md, 1)

            pe.sem_inc(md, M.primed)
            project(0, True)
            turn_over(0)
            with pe.Fori(0, G - 1) as g:
                network(g)
                experts(g, 0)
                project(g + 1)
                experts(g, 1)
                turn_over(g + 1)
                experts(g, 2)
                experts(g, 3)
            network(G - 1)
            for j in range(J):
                experts(G - 1, j)


HB, DK = 4, 64
C = 32
CT = P // C
TAPS = 4


def layer1_weights(nc, d, sb, sem):
    wq = sb("front_wqkv", [P, EH, 3, E], F32); wl9 = sb("front_wl9", [P, EH, 9], F32); b9 = sb("front_b9", [1, 9], F32)
    cw = sb("front_cw", [P, 6, TAPS], F32); fw = sb("front_fw", [P, EH, 4, 2], F32); mw = sb("front_mw", [P, E], F32)
    mix = sb("front_mix", [P, HB], F32); trim = sb("front_trim", [P, C], F32)
    wl = sem("w4_loaded")

    def issue(sp):
        def w(dst, src):
            sp.dma_start(dst, src, allow_slow_non_contiguous=True).then_inc(wl, 16)
        for i, n in enumerate(("Wq", "Wk", "Wv")):
            w(wq[:, :, i, :], d[f"L1_attn_{n}"].rearrange("(h p) n -> p h n", p=P))
        w(wl9[:, :, 0:4], d["L1_attn_Wb"].rearrange("(h p) n -> p h n", p=P))
        w(wl9[:, :, 4:8], d["L1_attn_Wgamma"].rearrange("(h p) n -> p h n", p=P))
        w(wl9[:, :, 8:9], d["L1_attn_frac_gate_w"].rearrange("(h p) n -> p h n", p=P))
        w(b9[:, 8:9], d["L1_attn_frac_gate_b"].rearrange("(o n) -> o n", o=1))
        for i, n in enumerate(("conv_q", "conv_k", "conv_v")):
            w(cw[:, 2 * i:2 * i + 2, :], d[f"L1_attn_{n}"].rearrange("(h p) n -> p h n", p=P))
        for i in range(4):
            for h in range(EH):
                w(fw[:, h, i, :], d["L1_attn_frac_conv_w"][i, h * P:(h + 1) * P, :])
        w(mw[:], bcast(d["L1_attn_mixer_norm_w"], P))
        w(mix[:], bcast(d["L1_attn_rot_logit"], P))
        w(trim[:], d["c_trim"])

    return (wq, wl9, b9, cw, fw, mw, mix, trim, wl), issue


def layer1_front(nc, k, d, sem, x_res, gam, kn_dram, vk_dram, a_dram, qk_dram, weights):
    AV = Steps("stats", "aggr", "rstd", "xn", *[f"fr_{h}_{t}" for t in range(5) for h in range(2)],
               *[f"cv_{m}_{t}" for a in (0, 2, 4) for t in range(TAPS) for m in (a, a + 1)], "frr", "frg", "frx")
    BV = Steps(*[f"vb_{j}" for j in range(J)], "t1", "t2", "t3", "t4", "ra", "rb", "sc", "ro", "ss", "rr", "nrm",
               *[f"A_{j}" for j in range(J)])
    AA = Steps("std", "halo", "hT", *[f"pre_{m}" for m in range(6)], "sig", *[f"silu_{m}" for m in range(6)], "fstd")
    BA = Steps(*[f"X_{j}" for j in range(J)], "sq", "sstd", *[f"qkT_{j}" for j in range(J)])
    AM = Steps("tp", *[f"pr_{m}" for m in range(6)], "lg", "ftp")
    BM = Steps(*[f"nat_{j}" for j in range(J)], "qkT_0", *[n for j in range(1, J) for n in (f"qkT_{j}", f"G_{j - 1}")], f"G_{J - 1}")
    AO = Steps("fx")
    BO = Steps("bt", "cm", "sm", "t1", "t2", "t3", "t4", "ra", "rb", "sc", "ro", "m2", "kb")
    with ExitStack() as st:
        def sb(n, s, t=F32):
            return st.enter_context(nc.sbuf_tensor(f"front_{n}", s, t))
        def ps(n, s, t=F32):
            return st.enter_context(nc.psum_tensor(f"front_{n}", s, t))
        wq, wl9, b9, cw, fw, mw, mix, trim, wl = weights
        f1 = sb("f1", [P, EH]); omx = sb("omx", [P, HB])
        st6 = sb("st6", [P, J, 6]); mv = sb("mv", [P, J, 2]); sd = sb("sd", [P, J]); rs = sb("rs", [P, J])
        eps = sb("eps", [P, 2])
        xn = sb("xn", [P, J, E]); hT = sb("hT", [P, EH, 8 + 512])
        fr = sb("fr", [P, 2, EH, 512])
        pre = sb("pre", [P, 6, 3 + 512]); acc = sb("acc", [P, 2, 6, 512])
        lg = sb("lg", [P, J, 9]); bt4 = sb("bt4", [P, J, HB])
        X = sb("X", [P, J, 2, HB, DK]); XR = sb("XR", [P, J, 2, HB, DK]); SQ = sb("SQ", [P, J, 2, HB, DK])
        cs = sb("cs", [P, 2, J, 32]); csm = sb("csm", [P, 2, J, HB, 32])
        tq = [sb(f"tq{i}", [P, J, HB, 32]) for i in range(4)]
        tk = [sb(f"tk{i}", [P, J, HB, 32]) for i in range(4)]
        ss = sb("ss", [P, J, 2, HB]); ssd = sb("ssd", [P, J, 2, HB]); rr = sb("rr", [P, J, 2, HB, 1])
        vk = sb("vk", [P, J, HB, 2 * DK]); m2 = sb("m2", [P, J, HB, C]); AB = sb("AB", [P, J, HB, C])
        fss = sb("fss", [P, J]); fsd = sb("fsd", [P, J]); frr = sb("frr", [P, J]); frg = sb("frg", [P, J])
        qkG = sb("qkG", [P, J, 4 * P])
        fx = sb("fx", [P, J, E]); junk = sb("junk", [P, E])
        tp = ps("tp", [P, EH, 512]); pr = ps("pr", [P, 2, 512]); nat = ps("nat", [P, 2, 512]); gp = ps("gp", [P, 2, 512])
        csl, xout = sem("cs_loaded"), [sem("kn_out"), sem("vk_out"), sem("a_out"), sem("qkT_out")]
        avd, aad, amd, aod = (sem(f"front_a_{e}") for e in ("dve", "act", "pe", "pool"))
        bvd, bad, bmd, bod = (sem(f"front_b_{e}") for e in ("dve", "act", "pe", "pool"))
        held, sheld, pheld = sem("p4_held"), sem("p4_sp_held"), sem("p4_pool_held")
        sw2, fsq, cleared, mixed, coef = sem("w4_sum"), sem("frac_squares"), sem("cleared"), sem("mixed"), sem("coefs")
        block = st.enter_context(nc.Block())
        NWL = 16 * 21
        cos_v = d["c_cos"].rearrange("(t p) f -> p t f", p=P)
        sin_v = d["c_sin"].rearrange("(t p) f -> p t f", p=P)

        @block.sync
        def _(sp):
            for s in xout:
                sp.sem_inc(s, 16 * CT if s is xout[2] else 16)

            def load(g):
                tiles = bass.ds(g * J, J)
                sp.dma_start(cs[:, 0, :, :], cos_v[:, tiles, :]).then_inc(csl, 16)
                sp.dma_start(cs[:, 1, :, :], sin_v[:, tiles, :]).then_inc(csl, 16)

            def store(g):
                tiles = bass.ds(g * J, J)
                sp.wait_ge(bvd, BV(g, "nrm"))
                sp.dma_start(kn_dram[:, tiles, :], XR[:, :, 1, :, :].rearrange("p j h c -> p j (h c)"))\
                    .then_inc(xout[0], 16)
                sp.wait_ge(bod, BO(g, "kb"))
                sp.sem_inc(sheld, 1)
                sp.wait_ge(bvd, BV(g, f"vb_{J - 1}"))
                sp.dma_start(vk_dram[:, tiles, :], vk[:].rearrange("p j h c -> p j (h c)")).then_inc(xout[1], 16)
                sp.wait_ge(bvd, BV(g, f"A_{J - 1}"))
                for c in range(CT):
                    sp.dma_start(a_dram[bass.ds(g, 1), c, :, :, :, :].rearrange("o j h i x -> (o i) (j h) x"),
                                 AB[C * c:C * c + C, :, :, :].rearrange("p j h x -> p (j h) x")).then_inc(xout[2], 16)
                sp.wait_ge(bad, BA(g, f"qkT_{J - 1}"))
                sp.dma_start(qk_dram[:, tiles, :], qkG[:]).then_inc(xout[3], 16)

            load(0)
            with sp.Fori(0, G - 1) as g:
                sp.wait_ge(bod, BO(g, "sm"))
                sp.sem_inc(sheld, 1)
                load(g + 1)
                store(g)
            store(G - 1)
            for s in xout:
                sp.wait_ge(s, (16 * G + 16) * (CT if s is xout[2] else 1))

        @block.gpsimd
        def _(pool):
            nc.gpsimd.memset(eps[:, 0:1], LN_EPS)
            nc.gpsimd.memset(eps[:, 1:2], 1e-6)
            nc.gpsimd.memset(hT[:], 0.0)
            nc.gpsimd.memset(b9[:, 0:8], 0.0)
            nc.gpsimd.memset(pre[:], 0.0).then_inc(cleared, 1)
            pool.wait_ge(wl, NWL)
            pool.wait_ge(coef, 1)

            def heads(g):
                pool.wait_ge(aad, AA(g, "sig"))
                pool.wait_ge(bvd, BV(g - 1, "vb_3"))
                pool.wait_ge(bod, BO(g - 1, "kb"))
                pool.sem_inc(pheld, 1)
                nc.gpsimd.tensor_copy(bt4[:], lg[:, :, 0:4]).then_inc(bod, 1)
                mb = mix[:].rearrange("p (o h c) -> p o h c", o=1, c=1).broadcast_to([P, J, HB, 32])
                ob = omx[:].rearrange("p (o h c) -> p o h c", o=1, c=1).broadcast_to([P, J, HB, DK])
                pool.wait_ge(csl, 32 * g + 32)
                pool.wait_ge(bvd, BV(g - 1, "t4"))
                pool.wait_ge(bod, BO(g - 1, "t4"))
                for i in range(2):
                    nc.gpsimd.tensor_tensor(csm[:, i, :, :, :], cs[:, i, :, :].rearrange("p j (o c) -> p j o c", o=1)
                                            .broadcast_to([P, J, HB, 32]), mb, ALU.mult).then_inc(bod, 1)
                pool.wait_ge(bad, BA(g, "X_3"))
                pool.wait_ge(bod, BO(g, "sm"))
                c_, s_ = csm[:, 0, :, :, :], csm[:, 1, :, :, :]
                x1, x2 = X[:, :, 1, :, 0:DK:2], X[:, :, 1, :, 1:DK:2]
                for o_, a_, b_ in ((0, x1, c_), (1, x2, s_), (2, x1, s_), (3, x2, c_)):
                    nc.gpsimd.tensor_tensor(tk[o_][:], a_, b_, ALU.mult).then_inc(bod, 1)
                pool.wait_ge(bod, BO(g, "t4"))
                nc.gpsimd.tensor_tensor(tk[0][:], tk[0][:], tk[1][:], ALU.subtract).then_inc(bod, 1)
                nc.gpsimd.tensor_tensor(tk[2][:], tk[2][:], tk[3][:], ALU.add).then_inc(bod, 1)
                nc.gpsimd.tensor_tensor(X[:, :, 1, :, :], X[:, :, 1, :, :], ob, ALU.mult).then_inc(bod, 1)
                pool.wait_ge(bod, BO(g, "sc"))
                pool.wait_ge(bmd, BM(g - 1, "qkT_3"))
                pool.wait_ge(xout[0], 16 * g + 16)
                nc.gpsimd.tensor_tensor(XR[:, :, 1, :, 0:32], X[:, :, 1, :, 0:32], tk[0][:], ALU.add)
                nc.gpsimd.tensor_tensor(XR[:, :, 1, :, 32:64], X[:, :, 1, :, 32:64], tk[2][:], ALU.add).then_inc(bod, 1)
                bt = bt4[:].rearrange("p j (h o) -> p j h o", o=1)
                nc.gpsimd.tensor_tensor(m2[:], trim[:].rearrange("p (a b c) -> p a b c", a=1, b=1)
                                        .broadcast_to([P, J, HB, C]), bt.broadcast_to([P, J, HB, C]),
                                        ALU.mult).then_inc(bod, 1)
                pool.wait_ge(bvd, BV(g, "nrm"))
                nc.gpsimd.tensor_tensor(vk[:, :, :, DK:], XR[:, :, 1, :, :], bt.broadcast_to([P, J, HB, DK]),
                                        ALU.mult).then_inc(bod, 1)

            def mixer(g):
                pool.wait_ge(avd, AV(g, "frx"))
                pool.sem_inc(pheld, 1)
                xt = x_res[:, bass.ds(g * J, J), :]
                nc.gpsimd.tensor_tensor(xt, xt, fx[:], ALU.add).then_inc(aod, 1)

            pool.sem_inc(bod, BO.primed)
            pool.sem_inc(aod, AO.primed)
            mixer(0)
            with pool.Fori(1, G) as g:
                heads(g - 1)
                mixer(g)
            heads(G - 1)

        @block.scalar
        def _(act):
            act.wait_ge(wl, NWL)
            nc.scalar.activation(mix[:], mix[:], ACT.Sigmoid).then_inc(mixed, 1)
            act.wait_ge(coef, 1)
            act.wait_ge(cleared, 1)

            def spread_and_halo(g):
                act.wait_ge(avd, AV(g, "aggr"))
                nc.scalar.activation(sd[:], mv[:, :, 1], ACT.Sqrt, bias=eps[:, 0:1]).then_inc(aad, 1)
                act.wait_ge(avd, AV(g - 1, "cv_5_3"))
                act.wait_ge(amd, AM(g - 1, "lg"))
                nc.scalar.activation(hT[:, :, 0:8], hT[:, :, 512:520], ACT.Copy)
                nc.scalar.activation(pre[:, :, 0:3], pre[:, :, 512:515], ACT.Copy).then_inc(aad, 1)

            def modulate(g):
                act.wait_ge(aad, AA(g, "halo"))
                act.wait_ge(amd, AM(g, "tp"))
                for h in range(EH):
                    last = nc.scalar.activation(hT[:, h, 8:], tp[:, h, :], ACT.Identity,
                                                bias=k["mod1"][:, h:h + 1], scale=k["mod1"][:, 2 + h:3 + h])
                last.then_inc(aad, 1)

            def take_projections(g):
                for m in range(6):
                    act.wait_ge(amd, AM(g, f"pr_{m}"))
                    nc.scalar.activation(pre[:, m, 3:], pr[:, m % 2, :], ACT.Copy).then_inc(aad, 1)

            def silu(g, m):
                act.wait_ge(avd, AV(g, f"cv_{m}_3"))
                nc.scalar.activation(acc[:, 0, m, :], acc[:, 1, m, :], ACT.Silu).then_inc(aad, 1)

            def rates(g):
                act.wait_ge(amd, AM(g, "lg"))
                act.wait_ge(bod, BO(g - 1, "bt"))
                nc.scalar.activation(lg[:], pr[:, 0, 0:J * 9].rearrange("p (j e) -> p j e", e=9), ACT.Sigmoid)
                nc.scalar.activation(gam[:, bass.ds(g * J, J), :],
                                     pr[:, 0, 0:J * 9].rearrange("p (j e) -> p j e", e=9)[:, :, 4:8],
                                     ACT.Sigmoid).then_inc(aad, 1)

            def mixer_squares(g):
                act.wait_ge(amd, AM(g, "ftp"))
                for j in range(J):
                    if j:
                        act.wait_ge(fsq, J * g + j + J)
                    nc.scalar.activation(junk[:], tp[:, j // 2, (j % 2) * E:(j % 2) * E + E], ACT.Square,
                                         accum_out=fss[:, j:j + 1]).then_inc(fsq, 1)

            def mixer_spread(g):
                act.wait_ge(fsq, J * g + 2 * J)
                nc.scalar.activation(fsd[:], fss[:], ACT.Sqrt, bias=eps[:, 0:1], scale=1.0 / E).then_inc(aad, 1)

            def take_heads(g, j):
                act.wait_ge(bmd, BM(g, f"nat_{j}"))
                nc.scalar.activation(X[:, j, :, :, :].rearrange("p a h c -> p (a h c)"), nat[:, 0, :],
                                     ACT.Copy).then_inc(bad, 1)

            def head_squares(g):
                act.wait_ge(bvd, BV(g, "ro"))
                act.wait_ge(bod, BO(g, "ro"))
                nc.scalar.activation(SQ[:], XR[:], ACT.Square).then_inc(bad, 1)

            def head_spread(g):
                act.wait_ge(bvd, BV(g, "ss"))
                nc.scalar.activation(ssd[:], ss[:], ACT.Sqrt, bias=eps[:, 1:2]).then_inc(bad, 1)

            def take_turned(g, j):
                act.wait_ge(bmd, BM(g, f"qkT_{j}"))
                act.wait_ge(xout[3], 16 * g + 16)
                nc.scalar.activation(qkG[:, j, :], pr[:, j % 2, :], ACT.Copy).then_inc(bad, 1)

            def turn(g, front, back):
                if front:
                    spread_and_halo(g)
                if back:
                    take_heads(g - 1, 0)
                    take_heads(g - 1, 1)
                if front:
                    modulate(g)
                if back:
                    take_heads(g - 1, 2)
                    take_heads(g - 1, 3)
                if front:
                    take_projections(g)
                if back:
                    head_squares(g - 1)
                    head_spread(g - 1)
                if front:
                    rates(g)
                for j in range(J):
                    if back:
                        take_turned(g - 1, j)
                    if front:
                        for m in ((0, 1), (2, 3), (4, 5), ())[j]:
                            silu(g, m)
                if front:
                    mixer_squares(g)
                    mixer_spread(g)

            act.sem_inc(aad, AA.primed)
            act.sem_inc(bad, BA.primed)
            act.sem_inc(fsq, J)
            turn(0, True, False)
            with act.Fori(1, G) as g:
                turn(g, True, True)
            turn(G, False, True)

        @block.vector
        def _(dve):
            dve.wait_ge(mixed, 1)
            dve.wait_ge(wl, NWL)
            nc.vector.tensor_scalar(omx[:], mix[:], -1.0, 1.0, ALU.mult, ALU.add)
            nc.vector.tensor_tensor(mw[:], mw[:], k["ga1"][:], ALU.mult)
            nc.vector.tensor_reduce(f1[:], fw[:, :, :, 1], AX.X, ALU.add).then_inc(sw2, 1)
            dve.wait_ge(sw2, 1)
            nc.vector.tensor_scalar(f1[:], f1[:], 2.0, None, ALU.add).then_inc(coef, 1)
            dve.wait_ge(coef, 1)

            def statistics(g):
                xt = x_res[:, bass.ds(g * J, J), :]
                for j in range(J):
                    last = nc.vector.bn_stats(st6[:, j, :], xt[:, j, :])
                last.then_inc(avd, 1)
                dve.wait_ge(avd, AV(g, "stats"))
                dve.sem_inc(held, 1)
                for j in range(J):
                    last = nc.vector.bn_aggr(mv[:, j, :], st6[:, j, :])
                last.then_inc(avd, 1)

            def normalise(g):
                xt = x_res[:, bass.ds(g * J, J), :]
                dve.wait_ge(aad, AA(g, "std"))
                nc.vector.reciprocal(rs[:], sd[:]).then_inc(avd, 1)
                dve.wait_ge(avd, AV(g, "rstd"))
                for j in range(J):
                    last = nc.vector.tensor_scalar(xn[:, j, :], xt[:, j, :], mv[:, j, 0:1], rs[:, j:j + 1],
                                                   ALU.subtract, ALU.mult)
                last.then_inc(avd, 1)

            def mixer_taps(g):
                dve.wait_ge(aad, AA(g, "hT"))
                for h in range(EH):
                    nc.vector.tensor_scalar(fr[:, 0, h, :], hT[:, h, 8:], f1[:, h:h + 1], None,
                                            ALU.mult).then_inc(avd, 1)
                for t in range(1, 5):
                    sh = 8 - 2 ** (t - 1)
                    for h in range(EH):
                        dve.wait_ge(avd, AV(g, f"fr_{h}_{t - 1}"))
                        nc.vector.scalar_tensor_tensor(fr[:, t % 2, h, :], hT[:, h, sh:sh + 512], fw[:, h, t - 1, 0:1],
                                                       fr[:, (t - 1) % 2, h, :], ALU.mult, ALU.add).then_inc(avd, 1)

            def convolve(g, a):
                for t in range(TAPS):
                    for m in (a, a + 1):
                        if t == 0:
                            dve.wait_ge(aad, AA(g, f"pre_{m}"))
                            dve.wait_ge(bmd, BM(g - 1, "nat_3"))
                            nc.vector.tensor_scalar(acc[:, 0, m, :], pre[:, m, 0:512], cw[:, m, 0:1], None,
                                                    ALU.mult).then_inc(avd, 1)
                        else:
                            dve.wait_ge(avd, AV(g, f"cv_{m}_{t - 1}"))
                            nc.vector.scalar_tensor_tensor(acc[:, t % 2, m, :], pre[:, m, t:t + 512],
                                                           cw[:, m, t:t + 1], acc[:, (t - 1) % 2, m, :],
                                                           ALU.mult, ALU.add).then_inc(avd, 1)

            def mixer_out(g):
                dve.wait_ge(aad, AA(g, "fstd"))
                nc.vector.reciprocal(frr[:], fsd[:]).then_inc(avd, 1)
                dve.wait_ge(avd, AV(g, "frr"))
                nc.vector.tensor_tensor(frg[:], frr[:], lg[:, :, 8], ALU.mult).then_inc(avd, 1)
                dve.wait_ge(avd, AV(g, "frg"))
                dve.wait_ge(aod, AO(g - 1, "fx"))
                for j in range(J):
                    last = nc.vector.scalar_tensor_tensor(fx[:, j, :], tp[:, j // 2, (j % 2) * E:(j % 2) * E + E],
                                                          frg[:, j:j + 1], mw[:], ALU.mult, ALU.mult)
                last.then_inc(avd, 1)

            def take_values(g, j):
                if j == 0:
                    dve.wait_ge(bod, BO(g, "bt"))
                    dve.wait_ge(xout[1], 16 * g + 16)
                dve.wait_ge(bmd, BM(g, f"nat_{j}"))
                nc.vector.tensor_tensor(vk[:, j, :, 0:DK], nat[:, 1, 0:E].rearrange("p (h c) -> p h c", h=HB),
                                        bt4[:, j, :].rearrange("p (h o) -> p h o", o=1)
                                        .broadcast_to([P, HB, DK]), ALU.mult).then_inc(bvd, 1)

            def rotate(g):
                ob = omx[:].rearrange("p (o h c) -> p o h c", o=1, c=1).broadcast_to([P, J, HB, DK])
                dve.wait_ge(bad, BA(g, "X_3"))
                dve.wait_ge(bod, BO(g, "sm"))
                c_, s_ = csm[:, 0, :, :, :], csm[:, 1, :, :, :]
                x1, x2 = X[:, :, 0, :, 0:DK:2], X[:, :, 0, :, 1:DK:2]
                for o_, a_, b_ in ((0, x1, c_), (1, x2, s_), (2, x1, s_), (3, x2, c_)):
                    nc.vector.tensor_tensor(tq[o_][:], a_, b_, ALU.mult).then_inc(bvd, 1)
                dve.wait_ge(bvd, BV(g, "t4"))
                nc.vector.tensor_tensor(tq[0][:], tq[0][:], tq[1][:], ALU.subtract).then_inc(bvd, 1)
                nc.vector.tensor_tensor(tq[2][:], tq[2][:], tq[3][:], ALU.add).then_inc(bvd, 1)
                nc.vector.tensor_tensor(X[:, :, 0, :, :], X[:, :, 0, :, :], ob, ALU.mult).then_inc(bvd, 1)
                dve.wait_ge(bvd, BV(g, "sc"))
                dve.wait_ge(bmd, BM(g - 1, "qkT_3"))
                nc.vector.tensor_tensor(XR[:, :, 0, :, 0:32], X[:, :, 0, :, 0:32], tq[0][:], ALU.add)
                nc.vector.tensor_tensor(XR[:, :, 0, :, 32:64], X[:, :, 0, :, 32:64], tq[2][:], ALU.add).then_inc(bvd, 1)

            def norms(g):
                dve.wait_ge(bad, BA(g, "sq"))
                nc.vector.tensor_reduce(ss[:], SQ[:], AX.X, ALU.add).then_inc(bvd, 1)
                dve.wait_ge(bad, BA(g, "sstd"))
                nc.vector.reciprocal(rr[:].rearrange("p j a h o -> p (j a h o)"),
                                     ssd[:].rearrange("p j a h -> p (j a h)")).then_inc(bvd, 1)
                dve.wait_ge(bvd, BV(g, "rr"))
                xf = XR[:].rearrange("p j a h c -> p (j a h) c")
                nc.vector.tensor_tensor(xf, xf, rr[:].rearrange("p j a h o -> p (j a h) o")
                                        .broadcast_to([P, J * 2 * HB, DK]), ALU.mult).then_inc(bvd, 1)

            def mask_products(g, j):
                if j == 0:
                    dve.wait_ge(bod, BO(g, "m2"))
                    dve.wait_ge(xout[2], 16 * CT * g + 16 * CT)
                dve.wait_ge(bmd, BM(g, f"G_{j}"))
                for c in range(CT):
                    r = slice(C * c, C * c + C)
                    last = nc.vector.tensor_tensor(AB[r, j, :, :].rearrange("p (a b) c -> p b a c", b=2),
                                                   gp[r, :, 0:2 * P].rearrange("p b (a c) -> p b a c", a=2)[:, :, :, r],
                                                   m2[r, j, :, :].rearrange("p (a b) c -> p b a c", b=2), ALU.mult)
                last.then_inc(bvd, 1)

            def turn(g, front, back):
                if front:
                    statistics(g)
                if back:
                    take_values(g - 1, 0)
                if front:
                    normalise(g)
                if back:
                    take_values(g - 1, 1)
                    take_values(g - 1, 2)
                if front:
                    mixer_taps(g)
                if back:
                    take_values(g - 1, 3)
                    rotate(g - 1)
                for i in range(3):
                    if front:
                        convolve(g, 2 * i)
                    if back:
                        if i == 0:
                            norms(g - 1)
                        for j in ((), (0,), (1, 2, 3))[i]:
                            mask_products(g - 1, j)
                if front:
                    mixer_out(g)

            dve.sem_inc(avd, AV.primed)
            dve.sem_inc(bvd, BV.primed)
            turn(0, True, False)
            with dve.Fori(1, G) as g:
                turn(g, True, True)
            turn(G, False, True)

        @block.tensor
        def _(pe):
            pe.wait_ge(wl, NWL)
            pe.wait_ge(cleared, 1)

            def turn_over(g):
                pe.wait_ge(avd, AV(g, "xn"))
                for h in range(EH):
                    for j in range(J):
                        last = nc.tensor.transpose(tp[:, h, j * P:(j + 1) * P], xn[:, j, h * P:(h + 1) * P],
                                                   k["ident"][:])
                last.then_inc(amd, 1)

            def project(g):
                pe.wait_ge(aad, AA(g, "hT"))
                for m in range(6):
                    if m >= 2:
                        pe.wait_ge(aad, AA(g, f"pre_{m - 2}"))
                    for h in range(EH):
                        last = nc.tensor.matmul(pr[:, m % 2, :], wq[:, h, m // 2, (m % 2) * P:(m % 2) * P + P],
                                                hT[:, h, 8:], start=(h == 0), stop=(h == 1))
                    last.then_inc(amd, 1)

            def rates(g):
                pe.wait_ge(aad, AA(g, "pre_4"))
                for j in range(J):
                    dst = pr[:, 0, j * 9:j * 9 + 9]
                    nc.tensor.matmul(dst, k["ones"][0:1, :], b9[:], start=True, stop=False)
                    for h in range(EH):
                        last = nc.tensor.matmul(dst, hT[:, h, 8 + j * P:8 + (j + 1) * P], wl9[:, h, :],
                                                start=False, stop=(h == 1))
                last.then_inc(amd, 1)

            def turn_mixer(g):
                pe.wait_ge(avd, AV(g, "fr_1_4"))
                for j in range(J):
                    for h in range(EH):
                        o = (j % 2) * E + h * P
                        last = nc.tensor.transpose(tp[:, j // 2, o:o + P], fr[:, 0, h, j * P:(j + 1) * P],
                                                   k["ident"][:])
                last.then_inc(amd, 1)

            def turn_heads(g, j):
                if j == 0:
                    pe.wait_ge(aad, AA(g, "silu_5"))
                if j:
                    pe.wait_ge(bad, BA(g, f"X_{j - 1}"))
                    pe.wait_ge(bvd, BV(g, f"vb_{j - 1}"))
                for m in range(6):
                    last = nc.tensor.transpose(nat[:, m // 4, (m % 4) * P:(m % 4) * P + P],
                                               acc[:, 0, m, j * P:(j + 1) * P], k["ident"][:])
                last.then_inc(bmd, 1)

            def turn_rotated(g, j, last_group):
                if j == 0:
                    pe.wait_ge(bvd, BV(g, "nrm"))
                if j >= 2:
                    pe.wait_ge(bad, BA(g, f"qkT_{j - 2}"))
                elif last_group:
                    pe.wait_ge(bad, BA(g - 1, "qkT_3"))
                else:
                    pe.wait_ge(aad, AA(g + 1, "sig"))
                for pair in range(2):
                    for i, a in ((0, 1), (1, 0)):
                        last = nc.tensor.transpose(pr[:, j % 2, (2 * pair + i) * P:(2 * pair + i + 1) * P],
                                                   XR[:, j, a, 2 * pair:2 * pair + 2, :]
                                                   .rearrange("p h c -> p (h c)"), k["ident"][:])
                last.then_inc(bmd, 1)

            def square(g, j):
                pe.wait_ge(bad, BA(g, f"qkT_{j}"))
                if j:
                    pe.wait_ge(bvd, BV(g, f"A_{j - 1}"))
                for h in range(HB):
                    r = slice(DK * (h % 2), DK * (h % 2) + DK)
                    kT = qkG[r, j, (h // 2) * 2 * P:(h // 2) * 2 * P + P]
                    last = nc.tensor.matmul(gp[:, h % 2, (h // 2) * P:(h // 2) * P + P], kT, kT, start=True, stop=True)
                last.then_inc(bmd, 1)

            def turn(g, front, back):
                if back:
                    turn_heads(g - 1, 0)
                    turn_heads(g - 1, 1)
                if front:
                    turn_over(g)
                if back:
                    turn_heads(g - 1, 2)
                    turn_heads(g - 1, 3)
                if front:
                    project(g)
                    rates(g)
                    turn_mixer(g)
                if back:
                    turn_rotated(g - 1, 0, not front)
                    for j in range(1, J):
                        turn_rotated(g - 1, j, not front)
                        square(g - 1, j - 1)
                    square(g - 1, J - 1)

            pe.sem_inc(amd, AM.primed)
            pe.sem_inc(bmd, BM.primed)
            turn(0, True, False)
            with pe.Fori(1, G) as g:
                turn(g, True, True)
            turn(G, False, True)


def solve_chunks(nc, k, d, sem, a_dram, tt_dram):
    with ExitStack() as st:
        AF = st.enter_context(nc.sbuf_tensor("AF", [P, J, C, C], F32))
        TT = st.enter_context(nc.sbuf_tensor("TT", [P, J, C, C], F32))
        tmp = [st.enter_context(nc.sbuf_tensor(f"tmp{i}", [P, J, C - 1, C - 1], F32)) for i in range(2)]
        al, unit, prod, row, out = sem("a_loaded"), sem("unit_set"), sem("products"), sem("rows_done"), sem("tt_out")
        block = st.enter_context(nc.Block())

        @block.sync
        def _(sp):
            sp.dma_start(AF[:], a_dram.rearrange("g c j h i x -> (g c j) h i x")).then_inc(al, 16)
            sp.wait_ge(row, C - 1)
            for g in range(G):
                for c in range(CT):
                    r = CT * J * g + J * c
                    sp.dma_start(tt_dram[J * g:J * g + J, HB * c:HB * c + HB, :].rearrange("t h x -> t (h x)"),
                                 TT[r:r + J, :, :, :].rearrange("p h c i -> p (h c i)")).then_inc(out, 16)
            sp.wait_ge(out, 16 * G * CT)

        @block.gpsimd
        def _(pool):
            nc.gpsimd.memset(TT[:], 0.0).then_inc(unit, 1)
            pool.wait_ge(unit, 1)
            nc.gpsimd.memset(TT[:].rearrange("p t c i -> p t (c i)")[:, :, 0:C * C:C + 1], 1.0).then_inc(unit, 1)

        @block.vector
        def _(dve):
            dve.wait_ge(unit, 2)
            dve.wait_ge(al, 16)
            for i in range(1, C):
                buf = tmp[i % 2][:, :, 0:i, 0:i]
                if i >= 2:
                    dve.wait_ge(row, i - 1)
                nc.vector.tensor_tensor(buf, AF[:, :, i:i + 1, 0:i].broadcast_to([P, J, i, i]), TT[:, :, 0:i, 0:i],
                                        ALU.mult).then_inc(prod, 1)
                dve.wait_ge(prod, i)
                nc.vector.tensor_reduce(TT[:, :, 0:i, i], buf, AX.X, ALU.add).then_inc(row, 1)


def delta_rule(nc, k, d, sem, gam, o_all, kn_dram, vk_dram, qk_dram, tt_dram):
    DF = Steps("atm", "QE", "MT", back=2)
    DT = Steps("S_0", "S_1", "S_2", "S_3", back=2)
    AF_ = Steps("UW", "UBD", "B", back=2)
    AT = Steps("O", back=2)
    MF = Steps("at", "uw", "qe", "mt", "b", back=2)
    MT_ = Steps("ob", "rec_0", "rec_1", "rec_2", "rec_3", "o", back=2)
    LB = 11
    with ExitStack() as st:
        def sb(n, s, t=F32):
            return st.enter_context(nc.sbuf_tensor(f"delta_{n}", s, t))
        def ps(n, s, t=F32):
            return st.enter_context(nc.psum_tensor(f"delta_{n}", s, t))
        KN = [sb(f"KN{b}", [P, HB, DK]) for b in range(2)]
        KBD = [sb(f"KBD{b}", [P, HB, CT, DK]) for b in range(2)]
        VK = [sb(f"VK{b}", [P, HB, 2 * DK]) for b in range(2)]
        QK = [sb(f"QK{b}", [P, 2, 2, P]) for b in range(2)]
        TTb = [sb(f"TTb{b}", [P, HB, P]) for b in range(2)]
        UW = [sb(f"UW{b}", [P, HB, 2 * DK]) for b in range(2)]
        UBD = [sb(f"UBD{b}", [P, HB, CT, DK]) for b in range(2)]
        atm = [sb(f"atm{b}", [P, HB, P]) for b in range(2)]
        QE = [sb(f"QE{b}", [P, 2, P]) for b in range(2)]
        MTb = [sb(f"MTb{b}", [P, 2, CT, P]) for b in range(2)]
        BB = [sb(f"BB{b}", [P, 2, CT, P]) for b in range(2)]
        gI = [sb(f"gI{b}", [P, 2, CT, DK]) for b in range(2)]
        SB = sb("SB", [P, CT, 2, P])
        GM = sb("GM", [P, T, 2, CT, 2]); gall = sb("gall", [P, T * CT * 2])
        causal = sb("causal", [P, P]); id64 = sb("id64", [P, DK]); chunk = sb("chunk", [P, CT])
        atp = ps("atp", [P, 2, 512]); uwp = ps("uwp", [P, 512]); qep = ps("qep", [P, 512])
        mtp = ps("mtp", [P, 512]); bp = ps("bp", [P, 512]); op = ps("op", [P, 512]); rp = ps("rp", [P, 512])
        wl, gm_done, gm_mm, gm_cp = sem("w5_loaded"), sem("gm_done"), sem("gm_mm"), sem("gm_copied")
        cleared = sem("delta_cleared")
        loaded = [sem(f"tile_loaded{b}") for b in range(2)]
        df, dt_, af, at_, mf, mt_, gi = (sem(n) for n in ("dve_front", "dve_tail", "act_front", "act_tail",
                                                          "pe_front", "pe_tail", "gI_done"))
        held, sheld, aheld = sem("p5_pool_held"), sem("p5_sp_held"), sem("p5_act_held")
        block = st.enter_context(nc.Block())

        @block.sync
        def _(sp):
            sp.dma_start(causal[:], d["c_causal"]).then_inc(wl, 16)
            sp.dma_start(id64[:], d["c_id64"]).then_inc(wl, 16)
            sp.dma_start(chunk[:], d["c_chunk"]).then_inc(wl, 16)
            sp.wait_ge(cleared, 2)

            def load(t, b):
                one = bass.ds(t, 1)
                q = loaded[b]
                sp.dma_start(KN[b][:].rearrange("p h c -> p (h c)"), kn_dram[:, one, :]).then_inc(q, 16)
                sp.dma_start(VK[b][:].rearrange("p h c -> p (h c)"), vk_dram[:, one, :]).then_inc(q, 16)
                sp.dma_start(QK[b][:].rearrange("p a b c -> p (a b c)"), qk_dram[:, one, :]).then_inc(q, 16)
                for c in range(CT):
                    r = slice(C * c, C * c + C)
                    sp.dma_start(KBD[b][r, :, c, :], kn_dram[r, one, :].rearrange("p o (h c) -> p (o h) c", h=HB))\
                        .then_inc(q, 16)
                    sp.dma_start(TTb[b][r, :, r], tt_dram[one, HB * c:HB * c + HB, :]
                                 .rearrange("o h (x i) -> x (o h) i", i=C)).then_inc(q, 16)
            load(0, 0)
            load(1, 1)
            with sp.Fori(0, T // 2 - 1) as i:
                for b in range(2):
                    t = 2 * i + b
                    sp.wait_ge(mf, MF(t, "b"))
                    sp.wait_ge(df, DF(t, "QE"))
                    sp.sem_inc(sheld, 1)
                    load(t + 2, b)

        @block.gpsimd
        def _(pool):
            for b in range(2):
                for buf in (KBD, TTb):
                    nc.gpsimd.memset(buf[b][:], 0.0)
            nc.gpsimd.memset(SB[:], 0.0).then_inc(cleared, 1)
            pool.wait_ge(gm_cp, 1)

            def gi_of(t, b):
                pool.wait_ge(df, DF(t - 2, "MT"))
                pool.sem_inc(held, 1)
                gv = gall[:, bass.ds(t * CT * 2, CT * 2)].rearrange("p (c a o) -> p a c o", c=CT, o=1)
                nc.gpsimd.tensor_tensor(gI[b][:], id64[:].rearrange("p (a b c) -> p a b c", a=1, b=1)
                                        .broadcast_to([P, 2, CT, DK]), gv.broadcast_to([P, 2, CT, DK]),
                                        ALU.mult).then_inc(gi, 1)
            with pool.Fori(0, T // 2) as i:
                for b in range(2):
                    gi_of(2 * i + b, b)

        @block.scalar
        def _(act):
            act.wait_ge(cleared, 2)
            act.sem_inc(af, AF_.primed)
            act.sem_inc(at_, AT.primed)

            def front_uw(t, b):
                act.wait_ge(mf, MF(t, "uw"))
                act.wait_ge(mt_, MT_(t - 2, "ob"))
                nc.scalar.activation(UW[b][:].rearrange("p h c -> p (h c)"), uwp[:], ACT.Copy).then_inc(af, 1)
                for c in range(CT):
                    r = slice(C * c, C * c + C)
                    last = nc.scalar.activation(UBD[b][r, :, c, :],
                                                uwp[r, :].rearrange("p (h c) -> p h c", h=HB)[:, :, 0:DK], ACT.Copy)
                last.then_inc(af, 1)

            def front_b(t, b):
                act.wait_ge(mf, MF(t, "b"))
                act.wait_ge(dt_, DT(t - 2, "S_3"))
                for q in range(2):
                    r = slice(DK * q, DK * q + DK)
                    last = nc.scalar.activation(BB[b][r, :, :, r],
                                                bp[r, :].rearrange("p (a c x) -> p a c x", a=2, c=CT), ACT.Copy)
                last.then_inc(af, 1)

            def tail(t, b):
                act.wait_ge(mt_, MT_(t, "o"))
                act.sem_inc(aheld, 1)
                nc.scalar.activation(o_all[:, bass.ds(t, 1), :].rearrange("p o c -> p (o c)"), op[:, 0:E],
                                     ACT.Copy).then_inc(at_, 1)

            def both(t, b):
                front_uw(t, b)
                tail(t - 1, 1 - b)
                front_b(t, b)
            front_uw(0, 0)
            front_b(0, 0)
            with act.Fori(0, T // 2 - 1) as i:
                for b in (1, 0):
                    both(2 * i + 2 - b, b)
            both(T - 1, 1)
            tail(T - 1, 1)

        @block.vector
        def _(dve):
            for b in range(2):
                for buf in (UBD, MTb, BB):
                    last = nc.vector.memset(buf[b][:], 0.0)
            last.then_inc(cleared, 1)
            dve.wait_ge(wl, 48)
            for par in range(2):
                nc.vector.tensor_tensor(GM[:, :, par, :, :].rearrange("p t c a -> p t c a"),
                                        gam[:, :, par::2].rearrange("p t (o a) -> p t o a", o=1)
                                        .broadcast_to([P, T, CT, 2]),
                                        chunk[:].rearrange("p (o c q) -> p o c q", o=1, q=1)
                                        .broadcast_to([P, T, CT, 2]), ALU.mult).then_inc(gm_done, 1)
            dve.wait_ge(gm_mm, 1)
            nc.vector.tensor_copy(gall[:], rp[:, 0:T * CT * 2]).then_inc(gm_cp, 1)
            dve.wait_ge(cleared, 2)
            dve.sem_inc(df, DF.primed)
            dve.sem_inc(dt_, DT.primed)

            def f_at(t, b):
                dve.wait_ge(mf, MF(t, "at"))
                dve.wait_ge(mt_, MT_(t - 2, "ob"))
                nc.vector.tensor_tensor(atm[b][:].rearrange("p (a b) c -> p b a c", b=2),
                                        atp[:, :, 0:2 * P].rearrange("p b (a c) -> p b a c", a=2),
                                        causal[:].rearrange("p (a b c) -> p a b c", a=1, b=1)
                                        .broadcast_to([P, 2, 2, P]), ALU.mult).then_inc(df, 1)

            def f_qe(t, b):
                dve.wait_ge(mf, MF(t, "qe"))
                dve.wait_ge(mt_, MT_(t - 2, "o"))
                nc.vector.tensor_tensor(QE[b][:], QK[b][:, :, 1, :], qep[:, 0:2 * P]
                                        .rearrange("p (a c) -> p a c", a=2), ALU.subtract).then_inc(df, 1)

            def f_mt(t, b):
                dve.wait_ge(mf, MF(t, "mt"))
                dve.wait_ge(mt_, MT_(t - 2, "rec_3"))
                dve.wait_ge(gi, t + 1)
                for q in range(2):
                    r = slice(DK * q, DK * q + DK)
                    last = nc.vector.tensor_tensor(MTb[b][r, :, :, r], gI[b][r, :, :, :],
                                                   mtp[r, :].rearrange("p (a c x) -> p a c x", a=2, c=CT),
                                                   ALU.subtract)
                last.then_inc(df, 1)

            def t_s(t, b, c):
                dve.wait_ge(mt_, MT_(t, f"rec_{c}"))
                if c == 0:
                    dve.wait_ge(af, AF_(t, "B"))
                nc.vector.tensor_tensor(SB[:, (c + 1) % CT, :, :], BB[b][:, :, c, :],
                                        rp[:, 0:2 * P].rearrange("p (a c) -> p a c", a=2), ALU.add).then_inc(dt_, 1)

            def both(t, b):
                f_at(t, b)
                t_s(t - 1, 1 - b, 0)
                t_s(t - 1, 1 - b, 1)
                f_qe(t, b)
                t_s(t - 1, 1 - b, 2)
                f_mt(t, b)
                t_s(t - 1, 1 - b, 3)
            f_at(0, 0)
            f_qe(0, 0)
            f_mt(0, 0)
            with dve.Fori(0, T // 2 - 1) as i:
                for b in (1, 0):
                    both(2 * i + 2 - b, b)
            both(T - 1, 1)
            for c in range(CT):
                t_s(T - 1, 1, c)

        @block.tensor
        def _(pe):
            pe.wait_ge(gm_done, 2)
            for par in range(2):
                last = nc.tensor.matmul(rp[DK * par:DK * par + DK, 0:T * CT * 2], k["ones"][:, 0:DK],
                                        GM[:, :, par, :, :], start=True, stop=True)
            last.then_inc(gm_mm, 1)
            pe.wait_ge(gm_cp, 1)
            pe.wait_ge(cleared, 2)
            pe.sem_inc(mf, MF.primed)
            pe.sem_inc(mt_, MT_.primed)

            def f_at(t, b, turn):
                pe.wait_ge(loaded[b], 16 * LB * (turn + 1))
                pe.wait_ge(df, DF(t - 1, "atm"))
                for h in range(HB):
                    r = slice(DK * (h % 2), DK * (h % 2) + DK)
                    last = nc.tensor.matmul(atp[:, h % 2, (h // 2) * P:(h // 2) * P + P], QK[b][r, h // 2, 0, :],
                                            QK[b][r, h // 2, 1, :], start=True, stop=True)
                last.then_inc(mf, 1)

            def f_uw(t, b):
                pe.wait_ge(af, AF_(t - 1, "UBD"))
                for h in range(HB):
                    last = nc.tensor.matmul(uwp[:, h * P:(h + 1) * P], TTb[b][:, h, :], VK[b][:, h, :],
                                            start=True, stop=True)
                last.then_inc(mf, 1)

            def f_qe(t, b):
                pe.wait_ge(af, AF_(t, "UW"))
                pe.wait_ge(df, DF(t, "atm"))
                for h in range(HB):
                    r = slice(DK * (h % 2), DK * (h % 2) + DK)
                    last = nc.tensor.matmul(qep[r, (h // 2) * P:(h // 2) * P + P], UW[b][:, h, DK:], atm[b][:, h, :],
                                            start=True, stop=True)
                last.then_inc(mf, 1)

            def f_mt(t, b):
                pe.wait_ge(df, DF(t - 1, "MT"))
                for h in range(HB):
                    r = slice(DK * (h % 2), DK * (h % 2) + DK)
                    o = (h // 2) * 2 * P
                    last = nc.tensor.matmul(mtp[r, o:o + 2 * P], UW[b][:, h, DK:], KBD[b][:, h, :, :],
                                            start=True, stop=True)
                last.then_inc(mf, 1)

            def f_b(t, b):
                pe.wait_ge(af, AF_(t, "UBD"))
                for h in range(HB):
                    r = slice(DK * (h % 2), DK * (h % 2) + DK)
                    o = (h // 2) * 2 * P
                    last = nc.tensor.matmul(bp[r, o:o + 2 * P], KN[b][:, h, :], UBD[b][:, h, :, :],
                                            start=True, stop=True)
                last.then_inc(mf, 1)

            def t_ob(t, b):
                pe.wait_ge(at_, AT(t - 1, "O"))
                for h in range(HB):
                    last = nc.tensor.matmul(op[:, h * DK:(h + 1) * DK], atm[b][:, h, :], UW[b][:, h, 0:DK],
                                            start=(h == 0), stop=False, skip_group_check=True)
                last.then_inc(mt_, 1)

            def t_rec(t, b, c):
                pe.wait_ge(dt_, DT(t, f"S_{c - 1}") if c else DT(t - 1, "S_3"))
                if c == 0:
                    pe.wait_ge(df, DF(t, "MT"))
                for a in range(2):
                    last = nc.tensor.matmul(rp[:, a * P:(a + 1) * P], MTb[b][:, a, c, :], SB[:, c, a, :],
                                            start=True, stop=True)
                last.then_inc(mt_, 1)
                for a in range(2):
                    last = nc.tensor.matmul(op[C * c:C * c + C, a * P:(a + 1) * P], QE[b][:, a, C * c:C * c + C],
                                            SB[:, c, a, :], start=False, stop=True, skip_group_check=True)
                if c == CT - 1:
                    last.then_inc(mt_, 1)

            def both(t, b, turn):
                f_at(t, b, turn)
                t_ob(t - 1, 1 - b)
                t_rec(t - 1, 1 - b, 0)
                f_uw(t, b)
                t_rec(t - 1, 1 - b, 1)
                f_qe(t, b)
                t_rec(t - 1, 1 - b, 2)
                f_mt(t, b)
                t_rec(t - 1, 1 - b, 3)
                f_b(t, b)
            f_at(0, 0, 0)
            f_uw(0, 0)
            f_qe(0, 0)
            f_mt(0, 0)
            f_b(0, 0)
            with pe.Fori(0, T // 2 - 1) as i:
                both(2 * i + 1, 1, i)
                both(2 * i + 2, 0, i + 1)
            both(T - 1, 1, T // 2 - 1)
            t_ob(T - 1, 1)
            for c in range(CT):
                t_rec(T - 1, 1, c)


MAGIC = 1.5 * 2.0 ** 23


def layer1_back(nc, k, d, sem, x_res, o_all, out):
    V1, A1, M1 = Steps("ss", "rr", "on", "x3"), Steps("sq", "ostd", "oT"), Steps("otp", "wo")
    V2, A2, O2 = Steps("stats", "aggr", "rstd", "xn"), Steps("std"), Steps("hm", "ha")
    V3, M3, O3 = Steps("amax", "xs", "ri", "qr", "q", "qT", "y", "out"), Steps("qtp", "lin"), Steps("x3b")
    with ExitStack() as st:
        def sb(n, s, t=F32):
            return st.enter_context(nc.sbuf_tensor(f"back_{n}", s, t))
        def ps(n, s, t=F32):
            return st.enter_context(nc.psum_tensor(f"back_{n}", s, t))
        wo = sb("wo1", [P, EH, E]); w8 = sb("w8", [P, EH, E // 4], mybir.dt.int32); wq = sb("wq8", [P, EH, E], BF16)
        w8b = sb("w8b", [P, EH, E], BF16)
        onw = sb("onw", [P, 1]); ws = sb("ws", [P, E]); bi = sb("bi", [P, E]); eps = sb("eps", [P, 1])
        SQ = sb("SQ", [P, J, E]); ss = sb("ss", [P, J * HB]); osd = sb("osd", [P, J * HB]); rr = sb("rr", [P, J * HB, 1])
        on = sb("on", [P, J, E]); oT = sb("oT", [P, EH, 512])
        st6 = sb("st6", [P, J, 6]); mv = sb("mv", [P, J, 2]); sd = sb("sd", [P, J]); rs = sb("rs", [P, J])
        xn = sb("xn", [P, J, E]); h4 = sb("h4", [P, J, E])
        am = sb("am", [P, J]); xs = sb("xs", [P, J]); ri = sb("ri", [P, J])
        q32 = sb("q32", [P, J, E]); qb = sb("qb", [P, J, E], BF16); qT = sb("qT", [P, EH, 512], BF16)
        x3b = sb("x3b", [P, J, E]); y = sb("y", [P, J, E])
        otp = ps("otp", [P, EH, 512]); wop = ps("wop", [P, 2, 512]); qtp = ps("qtp", [P, EH, 512], BF16)
        lin = ps("lin", [P, 2, 512])
        wl, wready, eps_set, out_sent = sem("w6_loaded"), sem("w6_ready"), sem("eps6_set"), sem("out_sent")
        v1, a1, m1 = sem("residual_dve"), sem("residual_act"), sem("residual_pe")
        v2, a2, o2 = sem("norm_dve"), sem("norm_act"), sem("norm_pool")
        v3, m3, o3 = sem("linear_dve"), sem("linear_pe"), sem("linear_pool")
        held, held2, sheld, aheld = (sem(f"p6_{n}_held") for n in ("dve", "pool", "sp", "act"))
        wcast, wturned = sem("wq_cast"), sem("wq_turned")
        block = st.enter_context(nc.Block())
        out_v = out.rearrange("o (t p) c -> p (o t) c", p=P)

        @block.sync
        def _(sp):
            sp.dma_start(wo[:], d["L1_attn_Wo"].rearrange("(h p) n -> p h n", p=P)).then_inc(wl, 16)
            sp.dma_start(w8[:], d["L1_ffn_weight_q"].rearrange("(h p) n -> p h n", p=P)).then_inc(wl, 16)
            for h in range(2):
                sp.dma_start(onw[DK * h:DK * h + DK, :], d["L1_attn_o_norm_w"].rearrange("(c o) -> c o", o=1))\
                    .then_inc(wl, 16)
            sp.dma_start(ws[:], bcast(d["L1_ffn_weight_scale"], P)).then_inc(wl, 16)
            sp.dma_start(bi[:], bcast(d["L1_ffn_bias"], P)).then_inc(wl, 16)
            sp.sem_inc(out_sent, 16)
            with sp.Fori(0, G) as g:
                sp.wait_ge(v3, V3(g, "out"))
                sp.sem_inc(sheld, 1)
                sp.dma_start(out_v[:, bass.ds(g * J, J), :], y[:]).then_inc(out_sent, 16)
            sp.wait_ge(out_sent, 16 * G + 16)

        @block.gpsimd
        def _(pool):
            nc.gpsimd.memset(eps[:], LN_EPS).then_inc(eps_set, 1)
            row = lambda a: a[:].rearrange("p (o c) -> p o c", o=1).broadcast_to([P, J, E])
            pool.wait_ge(wready, 2)

            def modulate(g):
                pool.wait_ge(v2, V2(g, "xn"))
                nc.gpsimd.tensor_tensor(h4[:], xn[:], row(k["cb1"]), ALU.mult).then_inc(o2, 1)
                pool.wait_ge(o2, O2(g, "hm"))
                nc.gpsimd.tensor_tensor(h4[:], h4[:], row(k["sb1"]), ALU.add).then_inc(o2, 1)

            def residual_and_bias(g):
                pool.wait_ge(v3, V3(g - 1, "out"))
                pool.sem_inc(held2, 1)
                nc.gpsimd.tensor_tensor(x3b[:], x_res[:, bass.ds(g * J, J), :], row(bi), ALU.add).then_inc(o3, 1)

            def turn(n, one, two, three):
                if three:
                    residual_and_bias(n - 2)
                if two:
                    modulate(n - 1)

            pool.sem_inc(o2, O2.primed)
            pool.sem_inc(o3, O3.primed)
            turn(0, True, False, False)
            turn(1, True, True, False)
            with pool.Fori(2, G) as n:
                turn(n, True, True, True)
            turn(G, False, True, True)
            turn(G + 1, False, False, True)

        @block.scalar
        def _(act):
            act.wait_ge(wl, 16 * 6)
            act.wait_ge(eps_set, 1)

            def squares(g):
                act.wait_ge(v1, V1(g - 1, "ss"))
                act.sem_inc(aheld, 1)
                nc.scalar.activation(SQ[:], o_all[:, bass.ds(g * J, J), :], ACT.Square).then_inc(a1, 1)

            def head_spread(g):
                act.wait_ge(v1, V1(g, "ss"))
                nc.scalar.activation(osd[:], ss[:], ACT.Sqrt, bias=eps[:], scale=1.0 / DK).then_inc(a1, 1)

            def take_turned(g):
                act.wait_ge(m1, M1(g, "otp"))
                nc.scalar.activation(oT[:], otp[:], ACT.Copy, scale=onw[:]).then_inc(a1, 1)

            def spread(g):
                act.wait_ge(v2, V2(g, "aggr"))
                nc.scalar.activation(sd[:], mv[:, :, 1], ACT.Sqrt, bias=eps[:]).then_inc(a2, 1)

            def turn(n, one, two, three):
                if one:
                    squares(n)
                    head_spread(n)
                if two:
                    spread(n - 1)
                if one:
                    take_turned(n)

            act.sem_inc(a1, A1.primed)
            act.sem_inc(a2, A2.primed)
            turn(0, True, False, False)
            turn(1, True, True, False)
            with act.Fori(2, G) as n:
                turn(n, True, True, True)
            turn(G, False, True, True)
            turn(G + 1, False, False, True)

        @block.vector
        def _(dve):
            dve.wait_ge(wl, 16 * 6)
            nc.vector.tensor_tensor(wo[:], wo[:], k["ga1"][:].rearrange("p (o c) -> p o c", o=1)
                                    .broadcast_to([P, EH, E]), ALU.mult)
            nc.vector.tensor_copy(w8b[:], w8[:].bitcast(mybir.dt.int8)).then_inc(wcast, 1)
            nc.vector.tensor_tensor(ws[:], ws[:], k["gb1"][:], ALU.mult)
            nc.vector.tensor_tensor(bi[:], bi[:], k["gb1"][:], ALU.mult).then_inc(wready, 1)
            dve.wait_ge(wturned, 1)
            nc.vector.tensor_copy(wq[:], qtp[:, :, 0:E]).then_inc(wready, 1)
            dve.wait_ge(wready, 2)

            def head_sums(g):
                dve.wait_ge(a1, A1(g, "sq"))
                nc.vector.tensor_reduce(ss[:], SQ[:].rearrange("p j (h c) -> p (j h) c", c=DK), AX.X,
                                        ALU.add).then_inc(v1, 1)

            def head_norms(g):
                ot = o_all[:, bass.ds(g * J, J), :]
                dve.wait_ge(a1, A1(g, "ostd"))
                nc.vector.reciprocal(rr[:, :, 0], osd[:]).then_inc(v1, 1)
                dve.wait_ge(v1, V1(g, "rr"))
                nc.vector.tensor_tensor(on[:].rearrange("p j (h c) -> p (j h) c", c=DK),
                                        ot.rearrange("p j (h c) -> p (j h) c", c=DK),
                                        rr[:].broadcast_to([P, J * HB, DK]), ALU.mult).then_inc(v1, 1)

            def residual(g):
                xt = x_res[:, bass.ds(g * J, J), :]
                dve.wait_ge(m1, M1(g, "wo"))
                for a in range(2):
                    last = nc.vector.tensor_tensor(xt[:, 2 * a:2 * a + 2, :], xt[:, 2 * a:2 * a + 2, :],
                                                   wop[:, a, :].rearrange("p (j c) -> p j c", j=2), ALU.add)
                last.then_inc(v1, 1)

            def statistics(g):
                xt = x_res[:, bass.ds(g * J, J), :]
                dve.wait_ge(v1, V1(g, "x3"))
                dve.sem_inc(held, 1)
                for j in range(J):
                    last = nc.vector.bn_stats(st6[:, j, :], xt[:, j, :])
                last.then_inc(v2, 1)
                dve.wait_ge(v2, V2(g, "stats"))
                dve.sem_inc(held, 1)
                for j in range(J):
                    last = nc.vector.bn_aggr(mv[:, j, :], st6[:, j, :])
                last.then_inc(v2, 1)

            def normalise(g):
                xt = x_res[:, bass.ds(g * J, J), :]
                dve.wait_ge(a2, A2(g, "std"))
                nc.vector.reciprocal(rs[:], sd[:]).then_inc(v2, 1)
                dve.wait_ge(v2, V2(g, "rstd"))
                for j in range(J):
                    last = nc.vector.tensor_scalar(xn[:, j, :], xt[:, j, :], mv[:, j, 0:1], rs[:, j:j + 1],
                                                   ALU.subtract, ALU.mult)
                last.then_inc(v2, 1)

            def scales(g):
                dve.wait_ge(o2, O2(g, "ha"))
                nc.vector.tensor_reduce(am[:], h4[:], AX.X, ALU.max, apply_absolute_value=True).then_inc(v3, 1)
                dve.wait_ge(v3, V3(g, "amax"))
                nc.vector.tensor_scalar(xs[:], am[:], 1e-6, 1.0 / 127.0, ALU.max, ALU.mult).then_inc(v3, 1)
                dve.wait_ge(v3, V3(g, "xs"))
                nc.vector.reciprocal(ri[:], xs[:]).then_inc(v3, 1)

            def quantise(g):
                dve.wait_ge(v3, V3(g, "ri"))
                for j in range(J):
                    last = nc.vector.tensor_scalar(q32[:, j, :], h4[:, j, :], ri[:, j:j + 1], MAGIC,
                                                   ALU.mult, ALU.add)
                last.then_inc(v3, 1)
                dve.wait_ge(v3, V3(g, "qr"))
                nc.vector.tensor_scalar(qb[:], q32[:], -MAGIC, 127.0, ALU.add, ALU.min).then_inc(v3, 1)

            def take_turned(g):
                dve.wait_ge(m3, M3(g, "qtp"))
                nc.vector.tensor_scalar(qT[:], qtp[:], -128.0, None, ALU.max).then_inc(v3, 1)

            def output(g):
                dve.wait_ge(m3, M3(g, "lin"))
                dve.wait_ge(out_sent, 16 * g + 16)
                for j in range(J):
                    last = nc.vector.scalar_tensor_tensor(y[:, j, :], lin[:, j // 2, (j % 2) * E:(j % 2) * E + E],
                                                          xs[:, j:j + 1], ws[:], ALU.mult, ALU.mult)
                last.then_inc(v3, 1)
                dve.wait_ge(v3, V3(g, "y"))
                dve.wait_ge(o3, O3(g, "x3b"))
                nc.vector.tensor_tensor(y[:], y[:], x3b[:], ALU.add).then_inc(v3, 1)

            def turn(n, one, two, three):
                if three:
                    scales(n - 2)
                if one:
                    head_sums(n)
                if three:
                    quantise(n - 2)
                if one:
                    head_norms(n)
                if two:
                    statistics(n - 1)
                if three:
                    take_turned(n - 2)
                if two:
                    normalise(n - 1)
                if three:
                    output(n - 2)
                if one:
                    residual(n)

            dve.sem_inc(v1, V1.primed)
            dve.sem_inc(v2, V2.primed)
            dve.sem_inc(v3, V3.primed)
            turn(0, True, False, False)
            turn(1, True, True, False)
            with dve.Fori(2, G) as n:
                turn(n, True, True, True)
            turn(G, False, True, True)
            turn(G + 1, False, False, True)

        @block.tensor
        def _(pe):
            pe.wait_ge(wcast, 1)
            for h in range(EH):
                for o in range(EH):
                    last = nc.tensor.transpose(qtp[:, h, o * P:(o + 1) * P], w8b[:, o, h * P:(h + 1) * P],
                                               k["identb"][:])
            last.then_inc(wturned, 1)
            pe.wait_ge(wready, 2)

            def turn_heads(g):
                pe.wait_ge(v1, V1(g, "on"))
                for h in range(EH):
                    for j in range(J):
                        last = nc.tensor.transpose(otp[:, h, j * P:(j + 1) * P], on[:, j, h * P:(h + 1) * P],
                                                   k["ident"][:])
                last.then_inc(m1, 1)

            def project(g):
                pe.wait_ge(a1, A1(g, "oT"))
                for j in range(J):
                    for h in range(EH):
                        last = nc.tensor.matmul(wop[:, j // 2, (j % 2) * E:(j % 2) * E + E],
                                                oT[:, h, j * P:(j + 1) * P], wo[:, h, :], start=(h == 0), stop=(h == 1))
                last.then_inc(m1, 1)

            def turn_quantised(g):
                pe.wait_ge(v3, V3(g, "q"))
                for h in range(EH):
                    for j in range(J):
                        last = nc.tensor.transpose(qtp[:, h, j * P:(j + 1) * P], qb[:, j, h * P:(h + 1) * P],
                                                   k["identb"][:])
                last.then_inc(m3, 1)

            def linear(g):
                pe.wait_ge(v3, V3(g, "qT"))
                for j in range(J):
                    for h in range(EH):
                        last = nc.tensor.matmul(lin[:, j // 2, (j % 2) * E:(j % 2) * E + E],
                                                qT[:, h, j * P:(j + 1) * P], wq[:, h, :], start=(h == 0), stop=(h == 1))
                last.then_inc(m3, 1)

            def turn(n, one, two, three):
                if three:
                    turn_quantised(n - 2)
                if one:
                    turn_heads(n)
                if three:
                    linear(n - 2)
                if one:
                    project(n)

            pe.sem_inc(m1, M1.primed)
            pe.sem_inc(m3, M3.primed)
            turn(0, True, False, False)
            turn(1, True, True, False)
            with pe.Fori(2, G) as n:
                turn(n, True, True, True)
            turn(G, False, True, True)
            turn(G + 1, False, False, True)


def build(nc, d, out):
    qk_parts = nc.dram_tensor("qk_parts", [3, 2 * E, S], BF16, kind="Internal").ap()
    ot = nc.dram_tensor("attn_out", [H * (DH + 1), S], F32, kind="Internal").ap()
    kn = nc.dram_tensor("k_natural", [P, T, E], F32, kind="Internal").ap()
    vk = nc.dram_tensor("vk_beta", [P, T, 2 * E], F32, kind="Internal").ap()
    qk = nc.dram_tensor("kq_transposed", [P, T, 2 * E], F32, kind="Internal").ap()
    am = nc.dram_tensor("a_blocks", [G, CT, J, HB, C, C], F32, kind="Internal").ap()
    tt = nc.dram_tensor("t_blocks", [T, CT * HB, C * C], F32, kind="Internal").ap()
    with ExitStack() as st:
        def sb(n, s, t):
            return st.enter_context(nc.sbuf_tensor(n, s, t))

        def sem(n):
            return st.enter_context(nc.semaphore(n))

        k = {}
        setup(nc, k, d, sb, sem)
        x_res = sb("x_res", [P, T, E], F32)
        weights0, issue0 = layer0_weights(nc, d, sb, sem)
        with ExitStack() as attn:
            def wide(n, s, t=F32):
                return attn.enter_context(nc.sbuf_tensor(n, s, t))
            v17 = wide("v17", [P, T, H, DH + 1])
            HD = wide("drift_hidden", [P, T, HID])
            gate = Gate(nc, d, wide, sem, v17, HD)
            parts = [qk_parts[i] for i in range(3)]
            project(nc, k, d, sem, x_res, v17, HD, parts)
            attention(nc, k, d, sem, v17, parts, ot, gate, issue0)
        weights1, issue1 = layer1_weights(nc, d, sb, sem)
        layer0_out(nc, k, d, sem, x_res, ot, weights0, issue1)
        gam = sb("gam", [P, T, HB], F32)
        layer1_front(nc, k, d, sem, x_res, gam, kn, vk, am, qk, weights1)
        solve_chunks(nc, k, d, sem, am, tt)
        o_all = sb("o_all", [P, T, E], F32)
        delta_rule(nc, k, d, sem, gam, o_all, kn, vk, qk, tt)
        layer1_back(nc, k, d, sem, x_res, o_all, out)


def constants():
    import numpy as np
    i = np.arange(P)
    late = (i[None, :] > i[:, None]).astype(np.float32) * np.float32(NEG)
    inv = (np.float32(1.0) / np.float32(10000.0) ** (np.arange(0, DK, 2, dtype=np.float32) / np.float32(DK)))
    ang = np.arange(S, dtype=np.float32)[:, None] * inv.astype(np.float32)[None, :]
    same = i[:, None] // C == i[None, :] // C
    return {
        "c_ident": np.eye(P, dtype=np.float32),
        "c_mask": np.stack([late, late.T]),
        "c_lower": np.tril(np.ones((NEXP, NEXP), np.float32), -1),
        "c_cos": np.cos(ang).astype(np.float32),
        "c_sin": np.sin(ang).astype(np.float32),
        "c_trim": -(i[:, None] % C > np.arange(C)[None, :]).astype(np.float32),
        "c_causal": (same & (i[:, None] <= i[None, :])).astype(np.float32),
        "c_id64": (i[:, None] % DK == np.arange(DK)[None, :]).astype(np.float32),
        "c_chunk": (i[:, None] // C == np.arange(CT)[None, :]).astype(np.float32) / C,
    }


def kernel(**inputs):
    import numpy as _np
    import concourse.bacc as _bacc
    from concourse import mybir as _mybir
    from concourse.bass_utils import run_bass_kernel_spmd as _run

    nc = _bacc.Bacc("TRN2", target_bir_lowering=False, num_devices=1)
    given = {n: _np.asarray(a) for n, a in inputs.items()}
    given["L1_ffn_weight_q"] = _np.ascontiguousarray(given["L1_ffn_weight_q"]).view(_np.int32)
    given.update(constants())
    arrays, d = {}, {}
    for name, a in given.items():
        a = _np.ascontiguousarray(a)
        arrays[f"in_{name}_dram"] = a
        d[name] = nc.dram_tensor(f"in_{name}_dram", a.shape, _mybir.dt.from_np(a.dtype), kind="ExternalInput").ap()
    out = nc.dram_tensor("out_0_dram", (1, S, E), _mybir.dt.float32, kind="ExternalOutput").ap()
    build(nc, d, out)
    r = _run(nc, [arrays], core_ids=[0])
    return r.results[0]["out_0_dram"]
```
